# Optimizing a Trainium2 kernel written in Bass

```python
import numpy as np
import jax
import jax.numpy as jnp

def _softmax(x, axis=-1):
    return jax.nn.softmax(x, axis=axis)

def _gelu(x):
    return jax.nn.gelu(x, approximate=True)

def _silu(x):
    return jax.nn.silu(x)

def _sigmoid(x):
    return jax.nn.sigmoid(x)

def _layernorm(x, axis=-1, eps=1e-05):
    m = jnp.mean(x, axis=axis, keepdims=True)
    v = jnp.var(x, axis=axis, keepdims=True)
    return (x - m) / jnp.sqrt(v + eps)

def _scatter_add(tgt, idx, src, axis=0):
    return tgt.at[idx].add(src)

def _segment_sum(src, seg, n):
    return jax.ops.segment_sum(src, seg, n)
kernel_name = 'mk_sandwich_d1_jaxref_r8_4fcaf9'

def setup_inputs(seed: int=0):
    np.random.seed(seed)
    _w = jnp.asarray

    def _L0_attn_setup():
        import jax, jax.numpy as jnp
        import numpy as np
        D_MODEL = 128
        D_STATE = 16
        D_CONV = 3
        D_INNER = 2 * D_MODEL
        B, S = (4, 256)

        def _mamba_forward(x, in_proj_w, conv_w, conv_b, x_proj_w, dt_proj_w, dt_proj_b, out_proj_w, A_log, D_param):
            combined = x @ in_proj_w
            u, x_gate = jnp.split(combined, 2, axis=-1)
            u_c = jax.lax.conv_general_dilated(u.transpose(0, 2, 1), conv_w, window_strides=(1,), padding='SAME', feature_group_count=D_INNER, dimension_numbers=('NCW', 'OIW', 'NCW'))
            u = jax.nn.silu((u_c + conv_b[None, :, None]).transpose(0, 2, 1))
            x_dbl = u @ x_proj_w
            delta, b, c = jnp.split(x_dbl, [D_INNER, D_INNER + D_STATE], axis=-1)
            delta = jax.nn.softplus(delta @ dt_proj_w + dt_proj_b)
            a = -jnp.exp(A_log)

            def step(h, inp):
                u_t, d_t, b_t, c_t = inp
                h = jnp.exp(d_t[:, :, None] * a) * h + d_t[:, :, None] * b_t[:, None, :] * u_t[:, :, None]
                y_t = jnp.einsum('bds,bs->bd', h, c_t)
                return (h, y_t)
            h0 = jnp.zeros((x.shape[0], D_INNER, D_STATE), x.dtype)
            xs = (u.transpose(1, 0, 2), delta.transpose(1, 0, 2), b.transpose(1, 0, 2), c.transpose(1, 0, 2))
            _, ys = jax.lax.scan(step, h0, xs)
            y = ys.transpose(1, 0, 2)
            y = y + u * D_param
            y = y * jax.nn.silu(x_gate)
            return y @ out_proj_w
        key = jax.random.key(seed)
        ks = jax.random.split(key, 9)
        s = 0.02
        x = jax.random.normal(ks[0], (B, S, D_MODEL), jnp.float32)
        in_proj_w = jax.random.normal(ks[1], (D_MODEL, 2 * D_INNER), jnp.float32) * s
        conv_w = jax.random.normal(ks[2], (D_INNER, 1, D_CONV), jnp.float32) * s
        conv_b = jax.random.normal(ks[3], (D_INNER,), jnp.float32) * s
        x_proj_w = jax.random.normal(ks[4], (D_INNER, D_INNER + 2 * D_STATE), jnp.float32) * s
        dt_proj_w = jax.random.normal(ks[5], (D_INNER, D_INNER), jnp.float32) * s
        dt_proj_b = jax.random.normal(ks[6], (D_INNER,), jnp.float32) * s
        out_proj_w = jax.random.normal(ks[7], (D_INNER, D_MODEL), jnp.float32) * s
        A_log = jnp.tile(jnp.log(jnp.arange(1, D_STATE + 1, dtype=jnp.float32))[None, :], (D_INNER, 1))
        D_param = jnp.ones((D_INNER,), jnp.float32)
        return {'x': x, 'in_proj_w': in_proj_w, 'conv_w': conv_w, 'conv_b': conv_b, 'x_proj_w': x_proj_w, 'dt_proj_w': dt_proj_w, 'dt_proj_b': dt_proj_b, 'out_proj_w': out_proj_w, 'A_log': A_log, 'D_param': D_param}
    _L0_attn_in = _L0_attn_setup()

    def _L0_ffn_setup():
        import jax, jax.numpy as jnp
        import numpy as np
        B, S, D = (4, 512, 128)
        E, F_EXP = (16, 256)
        F_C = 2.0
        F_SH = 256
        key = jax.random.key(seed)
        ks = jax.random.split(key, 8)
        s = 0.02
        return {'hidden_states': jax.random.normal(ks[0], (B, S, D), jnp.float32), 'gate_w': jax.random.normal(ks[1], (E, D), jnp.float32) * s, 'Wg': jax.random.normal(ks[2], (E, F_EXP, D), jnp.float32) * s, 'Wu': jax.random.normal(ks[3], (E, F_EXP, D), jnp.float32) * s, 'Wd': jax.random.normal(ks[4], (E, D, F_EXP), jnp.float32) * s, 'Ws_g': jax.random.normal(ks[5], (F_SH, D), jnp.float32) * s, 'Ws_u': jax.random.normal(ks[6], (F_SH, D), jnp.float32) * s, 'Ws_d': jax.random.normal(ks[7], (D, F_SH), jnp.float32) * s}
    _L0_ffn_in = _L0_ffn_setup()
    _d = {'L0_attn_x': _L0_attn_in['x'], 'L0_attn_in_proj_w': _L0_attn_in['in_proj_w'], 'L0_attn_conv_w': _L0_attn_in['conv_w'], 'L0_attn_conv_b': _L0_attn_in['conv_b'], 'L0_attn_x_proj_w': _L0_attn_in['x_proj_w'], 'L0_attn_dt_proj_w': _L0_attn_in['dt_proj_w'], 'L0_attn_dt_proj_b': _L0_attn_in['dt_proj_b'], 'L0_attn_out_proj_w': _L0_attn_in['out_proj_w'], 'L0_attn_A_log': _L0_attn_in['A_log'], 'L0_attn_D_param': _L0_attn_in['D_param'], 'L0_ffn_gate_w': _L0_ffn_in['gate_w'], 'L0_ffn_Wg': _L0_ffn_in['Wg'], 'L0_ffn_Wu': _L0_ffn_in['Wu'], 'L0_ffn_Wd': _L0_ffn_in['Wd'], 'L0_ffn_Ws_g': _L0_ffn_in['Ws_g'], 'L0_ffn_Ws_u': _L0_ffn_in['Ws_u'], 'L0_ffn_Ws_d': _L0_ffn_in['Ws_d']}
    _x0 = _d['L0_attn_x']
    _d['L0_attn_x'] = jax.random.normal(jax.random.fold_in(jax.random.key(seed), 1), (32, 256, 128), dtype=_x0.dtype)
    del _x0
    return _d

def reference(L0_attn_x, L0_attn_in_proj_w, L0_attn_conv_w, L0_attn_conv_b, L0_attn_x_proj_w, L0_attn_dt_proj_w, L0_attn_dt_proj_b, L0_attn_out_proj_w, L0_attn_A_log, L0_attn_D_param, L0_ffn_gate_w, L0_ffn_Wg, L0_ffn_Wu, L0_ffn_Wd, L0_ffn_Ws_g, L0_ffn_Ws_u, L0_ffn_Ws_d):

    def _L0_attn_ref(x, in_proj_w, conv_w, conv_b, x_proj_w, dt_proj_w, dt_proj_b, out_proj_w, A_log, D_param):
        import jax, jax.numpy as jnp
        import numpy as np
        D_MODEL = 128
        D_STATE = 16
        D_CONV = 3
        D_INNER = 2 * D_MODEL
        B, S = (4, 256)

        def _mamba_forward(x, in_proj_w, conv_w, conv_b, x_proj_w, dt_proj_w, dt_proj_b, out_proj_w, A_log, D_param):
            combined = x @ in_proj_w
            u, x_gate = jnp.split(combined, 2, axis=-1)
            u_c = jax.lax.conv_general_dilated(u.transpose(0, 2, 1), conv_w, window_strides=(1,), padding='SAME', feature_group_count=D_INNER, dimension_numbers=('NCW', 'OIW', 'NCW'))
            u = jax.nn.silu((u_c + conv_b[None, :, None]).transpose(0, 2, 1))
            x_dbl = u @ x_proj_w
            delta, b, c = jnp.split(x_dbl, [D_INNER, D_INNER + D_STATE], axis=-1)
            delta = jax.nn.softplus(delta @ dt_proj_w + dt_proj_b)
            a = -jnp.exp(A_log)

            def step(h, inp):
                u_t, d_t, b_t, c_t = inp
                h = jnp.exp(d_t[:, :, None] * a) * h + d_t[:, :, None] * b_t[:, None, :] * u_t[:, :, None]
                y_t = jnp.einsum('bds,bs->bd', h, c_t)
                return (h, y_t)
            h0 = jnp.zeros((x.shape[0], D_INNER, D_STATE), x.dtype)
            xs = (u.transpose(1, 0, 2), delta.transpose(1, 0, 2), b.transpose(1, 0, 2), c.transpose(1, 0, 2))
            _, ys = jax.lax.scan(step, h0, xs)
            y = ys.transpose(1, 0, 2)
            y = y + u * D_param
            y = y * jax.nn.silu(x_gate)
            return y @ out_proj_w
        return _mamba_forward(x, in_proj_w, conv_w, conv_b, x_proj_w, dt_proj_w, dt_proj_b, out_proj_w, A_log, D_param)

    def _L0_ffn_ref(hidden_states, gate_w, Wg, Wu, Wd, Ws_g, Ws_u, Ws_d):
        import jax, jax.numpy as jnp
        import numpy as np
        B, S, D = (4, 512, 128)
        E, F_EXP = (16, 256)
        F_C = 2.0
        F_SH = 256
        b, s, d = hidden_states.shape
        e = gate_w.shape[0]
        cap = int(s * F_C / e)
        logits = jnp.einsum('bsd,ed->bse', hidden_states, gate_w)
        scores = jax.nn.softmax(logits, axis=-1).transpose(0, 2, 1)
        topk_w, topk_idx = jax.lax.top_k(scores, cap)
        x_tok = jnp.take_along_axis(hidden_states[:, None, :, :], topk_idx[..., None], axis=2)
        g = jnp.einsum('becd,efd->becf', x_tok, Wg)
        u = jnp.einsum('becd,efd->becf', x_tok, Wu)
        h = jax.nn.gelu(g, approximate=False) * u
        eo = jnp.einsum('becf,edf->becd', h, Wd) * topk_w[..., None]
        offs = (jnp.arange(b) * s)[:, None, None]
        flat_idx = (topk_idx + offs).reshape(-1)
        flat = jnp.zeros((b * s, d), hidden_states.dtype)
        flat = flat.at[flat_idx].add(eo.reshape(-1, d))
        out = flat.reshape(b, s, d)
        gs = jnp.einsum('bsd,fd->bsf', hidden_states, Ws_g)
        us = jnp.einsum('bsd,fd->bsf', hidden_states, Ws_u)
        shared = jnp.einsum('bsf,df->bsd', jax.nn.gelu(gs, approximate=False) * us, Ws_d)
        return out + shared
    x = L0_attn_x
    x = x + _layernorm(_L0_attn_ref(_layernorm(x, axis=-1), L0_attn_in_proj_w, L0_attn_conv_w, L0_attn_conv_b, L0_attn_x_proj_w, L0_attn_dt_proj_w, L0_attn_dt_proj_b, L0_attn_out_proj_w, L0_attn_A_log, L0_attn_D_param), axis=-1)
    x = x + _layernorm(_L0_ffn_ref(_layernorm(x, axis=-1), L0_ffn_gate_w, L0_ffn_Wg, L0_ffn_Wu, L0_ffn_Wd, L0_ffn_Ws_g, L0_ffn_Ws_u, L0_ffn_Ws_d), axis=-1)
    return x

_drawn_inputs = setup_inputs


def setup_inputs(seed=0):
    import zlib

    import numpy as np

    out = dict(_drawn_inputs(seed))
    spreads = {'L0_attn_D_param': (1.0, 0.2)}
    factors = {'L0_attn_x_proj_w': 64.0,
     'L0_attn_dt_proj_w': 64.0,
     'L0_attn_dt_proj_b': 200.0,
     'L0_attn_A_log': 200.0}
    for name, (base, spread) in spreads.items():
        noise = np.random.default_rng([zlib.crc32(name.encode()), seed]).standard_normal(out[name].shape)
        drawn = base * np.exp(spread * noise) if base else spread * noise
        out[name] = jnp.asarray(drawn.astype(out[name].dtype))
    for name, factor in factors.items():
        out[name] = (out[name] * factor).astype(out[name].dtype)
    return out
```

```python
from contextlib import ExitStack

import numpy as np
import concourse.bass as bass
from concourse import mybir

F32 = mybir.dt.float32
BF16 = mybir.dt.bfloat16
ALU = mybir.AluOpType
ACT = mybir.ActivationFunctionType
AX = mybir.AxisListType

P = 128
EPS = 1e-5
LOG_EXP = "natural_log_exp_and_others"


def build(nc, a, out):
    B, S, DM = a["x"].shape
    TOK = B * S
    TILES = TOK // P
    DI = a["w_z"].shape[1]
    H2 = DI // P
    NG = DI // 64
    NSP = 8
    PAIRS = B // 2
    N = 2 * S
    CH = N // P
    STEPS = H2 * 4
    ITEMS = 2 * STEPS
    SPI = 2

    x_v = a["x"].rearrange("b (c p) d -> p (b c) d", p=P)
    out_v = out.rearrange("b (c p) d -> p (b c) d", p=P)
    b_rows = nc.dram_tensor("b_rows", (2, 16, N), F32, kind="Internal").ap()

    with ExitStack() as top:
        def sb(name, shape, dt=F32, ctx=top):
            return ctx.enter_context(nc.sbuf_tensor(name, shape, dt))

        def sem(name, ctx=top):
            return ctx.enter_context(nc.semaphore(name))

        X = sb("X", [P, TILES, DM])
        ident = sb("ident", [P, P])
        stats = sb("stats", [P, TILES, 6])
        mv = sb("mv", [P, TILES, 2])
        lnv = sb("lnv", [P, TILES])
        rstd = sb("rstd", [P, TILES])
        eps = sb("eps", [P, 1])
        xhT = sb("xhT", [P, B, S + 2])
        O = xhT[:, :, 0:S].rearrange("p b (c d) -> p b c d", d=DM)

        mamba(nc, a, X, xhT, O, ident, stats, mv, lnv, rstd, eps, x_v, b_rows,
              dict(B=B, S=S, DM=DM, TILES=TILES, DI=DI, H2=H2, NG=NG, NSP=NSP, PAIRS=PAIRS, N=N,
                   CH=CH, STEPS=STEPS, ITEMS=ITEMS, SPI=SPI))
        experts(nc, a, X, O, xhT, ident, eps, out_v, dict(B=B, S=S, DM=DM, TILES=TILES))


def mamba(nc, a, X, xhT, O, ident, stats, mv, lnv, rstd, eps, x_v, b_rows, k):
    B, S, DM, TILES, DI, H2, NG = (k[n] for n in ("B", "S", "DM", "TILES", "DI", "H2", "NG"))
    NSP, PAIRS, N, CH, STEPS, ITEMS, SPI = (
        k[n] for n in ("NSP", "PAIRS", "N", "CH", "STEPS", "ITEMS", "SPI"))
    RING = 8
    SP1 = S + 2
    with ExitStack() as ctx:
        def sb(name, shape, dt=F32):
            return ctx.enter_context(nc.sbuf_tensor(name, shape, dt))

        def sem(name):
            return ctx.enter_context(nc.semaphore(name))

        w_z = sb("w_z", [P, DI])
        w_conv = sb("w_conv", [P, 3, DI])
        conv_b = sb("conv_b", [P, H2])
        w_delta = sb("w_delta", [P, 2, DI])
        w_bc = sb("w_bc", [P, 2, P])
        dt_b = sb("dt_b", [P, H2])
        w_out = sb("w_out", [P, 2, DM])
        decay = sb("decay", [P, NG * NSP])
        dskip = sb("dskip", [P, H2])
        skip_diag = sb("skip_diag", [P, H2, P])
        fold = sb("fold", [P, 64])
        pick = sb("pick", [P, NSP, P], BF16)

        with ExitStack() as c0:
            w_xdT = c0.enter_context(nc.sbuf_tensor("w_xdT", [P, 2, DI], F32))
            w_dt = c0.enter_context(nc.sbuf_tensor("w_dt", [P, 2, DI], F32))
            w_u = c0.enter_context(nc.sbuf_tensor("w_u", [P, DI], F32))
            conv_rows = c0.enter_context(nc.sbuf_tensor("conv_rows", [P, 3, DI], F32))
            xh = c0.enter_context(nc.sbuf_tensor("xh", [P, 4, CH, DM], F32))
            tp = c0.enter_context(nc.psum_tensor("tp", [P, 4, 512], F32))
            wp = c0.enter_context(nc.psum_tensor("wp", [P, 2, 512], F32))
            x_in = [c0.enter_context(nc.semaphore(f"x_in{i}")) for i in range(4)]
            w_loaded = c0.enter_context(nc.semaphore("w_loaded"))
            conv_loaded = c0.enter_context(nc.semaphore("conv_loaded"))
            id_zero = c0.enter_context(nc.semaphore("id_zero"))
            id_ready = c0.enter_context(nc.semaphore("id_ready"))
            pads_ready = c0.enter_context(nc.semaphore("pads_ready"))
            exp_ready = c0.enter_context(nc.semaphore("exp_ready"))
            eps_ready = c0.enter_context(nc.semaphore("eps_ready"))
            stats_ready = c0.enter_context(nc.semaphore("stats_ready"))
            mv_ready = c0.enter_context(nc.semaphore("mv_ready"))
            ln_ready = c0.enter_context(nc.semaphore("ln_ready"))
            rstd_ready = c0.enter_context(nc.semaphore("rstd_ready"))
            xh_ready = c0.enter_context(nc.semaphore("xh_ready"))
            tp_ready = c0.enter_context(nc.semaphore("tp_ready"))
            tp_free = c0.enter_context(nc.semaphore("tp_free"))
            wp_ready = c0.enter_context(nc.semaphore("wp_ready"))
            fold_done = c0.enter_context(nc.semaphore("fold_done"))
            dve_done = c0.enter_context(nc.semaphore("dve_done"))
            act_done = c0.enter_context(nc.semaphore("act_done"))
            block = c0.enter_context(nc.Block())
            QT = TILES // 4
            small = [(w_u, "w_u"), (w_z, "w_z"), (conv_b, "conv_b"), (w_xdT, "w_xdT"), (w_dt, "w_dt"),
                     (w_bc, "w_bc"), (dt_b, "dt_b"), (w_out, "w_out"), (decay, "a_log"),
                     (dskip, "dskip")]

            @block.sync
            def _(sp):
                for i in range(4):
                    sp.dma_start(X[:, i * QT:(i + 1) * QT, :], x_v[:, i * QT:(i + 1) * QT, :]).then_inc(x_in[i], 16)

            @block.gpsimd
            def _(pool):
                nc.gpsimd.memset(ident[:], 0.0).then_inc(id_zero, 1)
                nc.gpsimd.memset(pick[:], 0.0).then_inc(id_zero, 1)
                nc.gpsimd.memset(xhT[:, :, 0:1], 0.0).then_inc(pads_ready, 1)
                nc.gpsimd.memset(xhT[:, :, SP1 - 1:SP1], 0.0).then_inc(pads_ready, 1)
                pool.wait_ge(id_zero, 2)
                nc.gpsimd.affine_select(out=ident[:], in_=ident[:], compare_op=ALU.not_equal, fill=1.0,
                                        base=0, pattern=[[-1, P]], channel_multiplier=1).then_inc(id_ready, 1)
                v = pick[:].rearrange("p s (h j) -> p s h j", h=2)
                for n, off in enumerate((0, 64, 96)):
                    if n:
                        pool.wait_ge(id_ready, n + 1)
                    nc.gpsimd.affine_select(out=v, in_=v, compare_op=ALU.not_equal, fill=1.0, base=-off,
                                            pattern=[[-1, NSP], [-NSP, 2], [0, 64]],
                                            channel_multiplier=1).then_inc(id_ready, 1)

            @block.scalar
            def _(act):
                for tile, name in small:
                    act.dma_start(tile[:], a[name]).then_inc(w_loaded, 16)
                act.dma_start(conv_rows[:], a["conv_w"].unsqueeze(0).broadcast_to([P, 3, DI])).then_inc(conv_loaded, 16)
                act.wait_ge(w_loaded, 16 * len(small))
                act.wait_ge(dve_done, 1)
                nc.scalar.activation(decay[:], decay[:], ACT.Exp).then_inc(exp_ready, 1)
                act.wait_ge(wp_ready, 1)
                nc.scalar.activation(w_delta[:], wp[:, :, 0:DI], ACT.Copy).then_inc(act_done, 1)
                act.wait_ge(eps_ready, 1)
                for i in range(4):
                    act.wait_ge(mv_ready, (i + 1) * QT)
                    nc.scalar.activation(lnv[:, i * QT:(i + 1) * QT], mv[:, i * QT:(i + 1) * QT, 1], ACT.Ln,
                                         bias=eps[:, 0:1]).then_inc(ln_ready, 1)
                    act.wait_ge(ln_ready, i + 1)
                    nc.scalar.activation(rstd[:, i * QT:(i + 1) * QT], lnv[:, i * QT:(i + 1) * QT], ACT.Exp,
                                         scale=-0.5).then_inc(rstd_ready, 1)
                for n in range(PAIRS):
                    act.wait_ge(tp_ready, n + 1)
                    nc.scalar.activation(xhT[:, 2 * n:2 * n + 2, 1:S + 1],
                                         tp[:, n % 4, :].rearrange("p (b t) -> p b t", b=2), ACT.Copy).then_inc(tp_free, 1)
                act.wait_ge(tp_free, PAIRS)
                act.wait_ge(act_done, 1)

            @block.vector
            def _(dve):
                nc.vector.memset(eps[:], EPS).then_inc(eps_ready, 1)
                dve.wait_ge(w_loaded, 16 * len(small))
                nc.vector.tensor_scalar(decay[:], decay[:], 60.0, None, ALU.min).then_inc(dve_done, 1)
                dve.wait_ge(exp_ready, 1)
                nc.vector.tensor_scalar(decay[:], decay[:], -1.0, None, ALU.mult).then_inc(dve_done, 1)
                dve.wait_ge(conv_loaded, 16)
                nc.vector.tensor_tensor(w_conv[:], conv_rows[:],
                                        w_u[:].unsqueeze(1).broadcast_to([P, 3, DI]), ALU.mult).then_inc(dve_done, 1)
                dve.wait_ge(id_ready, 1)
                for h in range(H2):
                    nc.vector.tensor_scalar(skip_diag[:, h, :], ident[:], dskip[:, h:h + 1], None, ALU.mult).then_inc(dve_done, 1)
                nc.vector.tensor_tensor(fold[:], ident[:, 0:64], ident[:, 64:P], ALU.add).then_inc(fold_done, 1)
                for i in range(4):
                    dve.wait_ge(x_in[i], 16)
                    for t in range(i * QT, (i + 1) * QT):
                        nc.vector.bn_stats(stats[:, t, :], X[:, t, :]).then_inc(stats_ready, 1)
                    for t in range(i * QT, (i + 1) * QT):
                        dve.wait_ge(stats_ready, t + 1)
                        nc.vector.bn_aggr(mv[:, t, :], stats[:, t, :]).then_inc(mv_ready, 1)
                dve.wait_ge(mv_ready, TILES)
                for n in range(PAIRS):
                    if n % 4 == 0:
                        dve.wait_ge(rstd_ready, n // 4 + 1)
                    if n >= 4:
                        dve.wait_ge(tp_ready, n - 3)
                    for c in range(CH):
                        t = CH * n + c
                        nc.vector.tensor_scalar(xh[:, n % 4, c, :], X[:, t, :], mv[:, t, 0:1], rstd[:, t:t + 1],
                                                ALU.subtract, ALU.mult).then_inc(xh_ready, 1)
                dve.wait_ge(dve_done, 3 + H2)
                dve.wait_ge(fold_done, 1)

            @block.tensor
            def _(pe):
                pe.wait_ge(w_loaded, 16 * len(small))
                for c in range(2):
                    for r in range(2):
                        last = nc.tensor.matmul(wp[:, c, 0:DI], w_xdT[:, r, c * P:(c + 1) * P], w_dt[:, r, :],
                                                start=(r == 0), stop=(r == 1))
                last.then_inc(wp_ready, 1)
                pe.wait_ge(id_ready, 1)
                for n in range(PAIRS):
                    pe.wait_ge(xh_ready, CH * (n + 1))
                    if n >= 4:
                        pe.wait_ge(tp_free, n - 3)
                    for c in range(CH):
                        last = nc.tensor.transpose(tp[:, n % 4, c * P:(c + 1) * P], xh[:, n % 4, c, :], ident[:])
                    last.then_inc(tp_ready, 1)

        uz = sb("uz", [P, 2, 4, N])
        dd = sb("dd", [P, 2, H2, N])
        relux, absx = dd[:, 0], dd[:, 1]
        onep = sb("onep", [P, H2, N])
        dup = sb("dup", [P, 2, 2, H2, 2, N])
        bcf = sb("bcf", [P, N])
        c3 = sb("c3", [P, 2, N], BF16)
        b_dup = sb("b_dup", [P, 2, NSP, N])
        states = sb("states", [P, RING, SPI, N])
        da = ctx.enter_context(nc.psum_tensor("da", [P, 2, SPI, N], F32))
        cb = ctx.enter_context(nc.psum_tensor("cb", [P, SPI, N], F32))
        yp = ctx.enter_context(nc.psum_tensor("yp", [P, N], F32))
        mp = ctx.enter_context(nc.psum_tensor("mp", [P, N], F32))

        da_zeroed = sem("da_zeroed")
        da_ready = sem("da_ready")
        dbu_ready = sem("dbu_ready")
        scan_done = sem("scan_done")
        hc_ready = sem("hc_ready")
        cb_ready = sem("cb_ready")
        sum_done = sem("sum_done")
        gate_done = sem("gate_done")
        mp_ready = sem("mp_ready")
        mp_free = sem("mp_free")
        silu_done = sem("silu_done")
        sp_exp = sem("sp_exp")
        sp_one = sem("sp_one")
        sp_ready = sem("sp_ready")
        sp_lost = sem("sp_lost")
        sp_fixed = sem("sp_fixed")
        delta_ready = sem("delta_ready")
        du_ready = [sem(f"du_ready{h}") for h in range(H2)]
        c_hi = sem("c_hi")
        c_rest = sem("c_rest")
        c_mid = sem("c_mid")
        c3_ready = sem("c3_ready")
        rows_out = [sem(f"rows_out{i}") for i in range(2)]
        b_in = [sem(f"b_in{i}") for i in range(2)]
        dup_in = [[sem(f"dup_in{i}{h}") for h in range(H2)] for i in range(2)]
        block = ctx.enter_context(nc.Block())

        DELTA0, DELTA1, OUT, BC, Z0, Z1, CONV0, CONV1 = range(8)
        BEFORE = (CONV0, CONV1, DELTA0, DELTA1, BC, Z0, Z1)
        before = BEFORE.index

        def place(n, stage):
            if is_at(n, 0):
                return 9 + stage - (stage > OUT)
            if is_at(n, PAIRS - 1):
                return 8 * n + 6
            return 8 * n + 8 + stage

        def over_pairs(eng, body):
            body(0, 0, 0, True, False)
            with eng.Fori(0, (PAIRS - 4) // 2) as j:
                body(2 * j + 1, 1, j, False, False)
                body(2 * j + 2, 0, j + 1, False, False)
            for n in range(PAIRS - 3, PAIRS):
                body(n, n % 2, n // 2, False, n == PAIRS - 1)

        def item(i):
            return i // 8, SPI * (i % 8 // 2), i % 2

        @block.tensor
        def _(pe):
            def project(stage, m, par, no):
                if not (isinstance(no, int) and no == 0):
                    pe.wait_ge(mp_free, no)
                u = uz[:, 1 - par, 2:4, :]
                if stage in (CONV0, CONV1):
                    h = stage - CONV0
                    for tap in range(3):
                        last = nc.tensor.matmul(mp[:].rearrange("p (b t) -> p b t", b=2),
                                                w_conv[:, tap, h * P:(h + 1) * P],
                                                xhT[:, bass.ds(2 * m, 2), tap:tap + S], start=(tap == 0), stop=(tap == 2))
                elif stage in (Z0, Z1):
                    h = stage - Z0
                    last = nc.tensor.matmul(mp[:].rearrange("p (b t) -> p b t", b=2),
                                            w_z[:, h * P:(h + 1) * P],
                                            xhT[:, bass.ds(2 * m, 2), 1:S + 1], start=True, stop=True)
                elif stage in (DELTA0, DELTA1):
                    h = stage - DELTA0
                    pe.wait_ge(silu_done, m + 1)
                    for c in range(2):
                        last = nc.tensor.matmul(mp[:], w_delta[:, c, h * P:(h + 1) * P], u[:, c, :],
                                                start=(c == 0), stop=(c == 1))
                elif stage == BC:
                    for c in range(2):
                        last = nc.tensor.matmul(mp[:], w_bc[:, c, :], u[:, c, :], start=(c == 0), stop=(c == 1))
                last.then_inc(mp_ready, 1)

            def output(m, par, no):
                pe.wait_ge(mp_free, no)
                pe.wait_ge(gate_done, 2 * m + 2)
                for c in range(CH):
                    for h in range(H2):
                        last = nc.tensor.matmul(mp[:, c * DM:(c + 1) * DM], uz[:, par, h, c * P:(c + 1) * P],
                                                w_out[:, h, :], start=(h == 0), stop=(h == 1))
                last.then_inc(mp_ready, 1)

            def sums(m, par, step):
                h, q = step // 4, step % 4
                if q == 0:
                    if not (isinstance(m, int) and m == 0 and h == 0):
                        pe.wait_ge(gate_done, 2 * m + h)
                    nc.tensor.matmul(yp[:], skip_diag[:, h, :], uz[:, 1 - par, 2 + h, :], start=True, stop=False,
                                     skip_group_check=True)
                for s in range(SPI):
                    for i in range(2):
                        last = nc.tensor.matmul(yp[64 * i:64 * i + 64, :], fold[:], states[:, (2 * step + i) % RING, s, :],
                                                start=False, stop=(q == 3 and s == SPI - 1), skip_group_check=True)
                last.then_inc(sum_done, 1)

            for stage in BEFORE:
                project(stage, 0, 0, before(stage))
            for no, stage in enumerate((CONV0, CONV1)):
                project(stage, 1, 1, len(BEFORE) + no)

            def body(n, par, uses, first, last):
                for s in range(STEPS):
                    if not (first and s == 0):
                        pe.wait_ge(hc_ready, ITEMS * n + 2 * s)
                    if s == 0:
                        pe.wait_ge(c3_ready, n + 1)
                    for i in range(SPI):
                        mm = nc.tensor.matmul(cb[:, i, :], pick[:, SPI * (s % 4) + i, :], c3[:, par, :],
                                              start=True, stop=True)
                    mm.then_inc(cb_ready, 1)
                    if s == 0 and not first:
                        sums(n - 1, 1 - par, STEPS - 1)
                    no = place(n, s)
                    if s == OUT:
                        if not first:
                            output(n - 1, 1 - par, no)
                    elif s in (CONV0, CONV1):
                        if not is_at(n, PAIRS - 2, PAIRS - 1):
                            project(s, n + 2, par, no)
                    elif not last:
                        project(s, n + 1, 1 - par, no)
                    if s:
                        sums(n, par, s - 1)

            over_pairs(pe, body)
            pe.wait_ge(hc_ready, ITEMS * PAIRS)
            sums(PAIRS - 1, (PAIRS - 1) % 2, STEPS - 1)
            output(PAIRS - 1, (PAIRS - 1) % 2, 8 * (PAIRS - 1) + 7)

        @block.scalar
        def _(act):
            def decays(n, par, uses, first, i):
                h, s0, g = item(i)
                if i in (0, 8):
                    act.wait_ge(dup_in[par][i // 8], 64 * uses + 64)
                if not (first and i < 2):
                    act.wait_ge(scan_done, ITEMS * n + i - 1)
                src = dup[:, par, 0, h, g, :].rearrange("p (b t) -> p b t", b=2)
                for s in range(SPI):
                    col = (2 * h + g) * NSP + s0 + s
                    last = nc.scalar.activation(
                        da[:, i % 2, s, :].rearrange("p (b t) -> p b t", b=2)[:, :, 1:S], src[:, :, 1:S],
                        ACT.Exp, scale=decay[:, col:col + 1])
                last.then_inc(da_ready, 1)

            def evacuate(stage, m, par, no):
                act.wait_ge(mp_ready, no + 1)
                if stage in (CONV0, CONV1):
                    h = stage - CONV0
                    last = nc.scalar.activation(uz[:, 1 - par, 2 + h, :], mp[:], ACT.Identity, bias=conv_b[:, h:h + 1])
                elif stage in (Z0, Z1):
                    last = nc.scalar.activation(uz[:, par, stage - Z0, :], mp[:], ACT.Copy)
                elif stage in (DELTA0, DELTA1):
                    h = stage - DELTA0
                    if stage == DELTA0 and not is_at(m, 0):
                        act.wait_ge(delta_ready, H2 * m)
                    nc.scalar.activation(absx[:, h, :], mp[:], ACT.Abs, bias=dt_b[:, h:h + 1])
                    last = nc.scalar.activation(relux[:, h, :], mp[:], ACT.Relu, bias=dt_b[:, h:h + 1])
                elif stage == OUT:
                    last = nc.scalar.activation(O[:, bass.ds(2 * m, 2)], mp[:].rearrange("p (b c d) -> p b c d", b=2, d=DM),
                                                ACT.Copy)
                last.then_inc(mp_free, 1)

            def softplus(m, no):
                act.wait_ge(mp_free, no + 1)
                nc.scalar.activation(absx, absx, ACT.Exp, scale=-1.0).then_inc(sp_exp, 1)
                act.wait_ge(sp_exp, m + 1)
                nc.scalar.activation(onep[:], absx, ACT.Identity, bias=1.0).then_inc(sp_one, 1)

            def log(m):
                act.wait_ge(sp_lost, m + 1)
                nc.scalar.activation(onep[:], onep[:], ACT.Ln).then_inc(sp_ready, 1)

            def parts(m, par, uses, no):
                act.wait_ge(mp_ready, no + 1)
                if not (isinstance(m, int) and m == 0):
                    act.wait_ge(c3_ready, m)
                    act.wait_ge(rows_out[1 - par], 16 * (uses + par))
                    if not (isinstance(m, int) and m == 1):
                        act.wait_ge(cb_ready, STEPS * (m - 1))
                nc.scalar.activation(bcf[:], mp[:], ACT.Copy)
                nc.scalar.activation(c3[:, par, :], mp[:], ACT.Copy).then_inc(c_hi, 1)
                act.wait_ge(c_hi, m + 1)
                act.sem_inc(mp_free, 1)

            def middle(m, par):
                act.wait_ge(c_rest, m + 1)
                nc.scalar.activation(c3[64:P, par, :], bcf[64:P, :], ACT.Copy).then_inc(c_mid, 1)

            evacuate(CONV0, 0, 0, before(CONV0))
            evacuate(CONV1, 0, 0, before(CONV1))
            act.wait_ge(mp_free, 2)
            nc.scalar.activation(uz[:, 1, 2:4, :], uz[:, 1, 2:4, :], ACT.Silu).then_inc(silu_done, 1)
            nc.scalar.preload_act_table_set(LOG_EXP)
            evacuate(DELTA0, 0, 0, before(DELTA0))
            evacuate(DELTA1, 0, 0, before(DELTA1))
            softplus(0, before(DELTA1))
            log(0)
            parts(0, 0, 0, before(BC))
            evacuate(Z0, 0, 0, before(Z0))
            middle(0, 0)
            evacuate(Z1, 0, 0, before(Z1))
            evacuate(CONV0, 1, 1, len(BEFORE))
            act.wait_ge(da_zeroed, 1)

            def body(n, par, uses, first, last):
                nxt = uses + par if not isinstance(n, int) else (n + 1) // 2
                if not first:
                    nc.scalar.preload_act_table_set(LOG_EXP)
                for s in range(STEPS):
                    decays(n, par, uses, first, 2 * s)
                    decays(n, par, uses, first, 2 * s + 1)
                    no = place(n, s - 1)
                    if s == 0:
                        if last:
                            act.wait_ge(mp_free, 8 * n + 6)
                            nc.scalar.activation(uz[:, par, 0:2, :], uz[:, par, 0:2, :], ACT.Silu).then_inc(silu_done, 1)
                        else:
                            evacuate(CONV1, n + 1, 1 - par, 8 if first else 8 * n + 7)
                            act.wait_ge(mp_free, 9 if first else 8 * n + 8)
                            nc.scalar.activation(uz[:, par, :, :], uz[:, par, :, :], ACT.Silu).then_inc(silu_done, 1)
                        nc.scalar.preload_act_table_set(LOG_EXP)
                    elif s == OUT + 1:
                        if not first:
                            evacuate(OUT, n - 1, 1 - par, no)
                    elif s == CONV0 + 1:
                        if not is_at(n, PAIRS - 2, PAIRS - 1):
                            evacuate(CONV0, n + 2, par, no)
                    elif last:
                        pass
                    elif s == BC + 1:
                        log(n + 1)
                        parts(n + 1, 1 - par, nxt, no)
                    else:
                        if s == DELTA0 + 1:
                            act.wait_ge(dup_in[par][1], 64 * uses + 64)
                        evacuate(s - 1, n + 1, 1 - par, no)
                        if s == DELTA1 + 1:
                            softplus(n + 1, no)
                        if s == Z0 + 1:
                            middle(n + 1, 1 - par)

            over_pairs(act, body)
            evacuate(OUT, PAIRS - 1, (PAIRS - 1) % 2, 8 * (PAIRS - 1) + 7)
            act.wait_ge(mp_free, 8 * (PAIRS - 1) + 8)

        @block.gpsimd
        def _(pool):
            def delta(m, par):
                pool.wait_ge(sp_ready, m + 1)
                pool.wait_ge(sp_fixed, m + 1)
                pool.wait_ge(silu_done, m + 1)
                for h in range(H2):
                    nc.gpsimd.tensor_tensor(dd[:, 0, h], dd[:, 0, h], onep[:, h], ALU.add).then_inc(delta_ready, 1)
                    pool.wait_ge(delta_ready, H2 * m + h + 1)
                    nc.gpsimd.tensor_tensor(dd[:, 1, h], dd[:, 0, h], uz[:, 1 - par, 2 + h, :], ALU.mult).then_inc(du_ready[h], 1)

            delta(0, 0)

            def body(n, par, uses, first, last):
                for i in range(ITEMS):
                    h, s0, g = item(i)
                    if i in (0, 8):
                        pool.wait_ge(dup_in[par][h], 64 * uses + 64)
                    if i == 0:
                        pool.wait_ge(b_in[par], 32 * uses + 32)
                    if i % 2 == 0 and not (first and i < RING):
                        pool.wait_ge(sum_done, STEPS * n + (i - RING) // 2 + 1)
                    nc.gpsimd.tensor_tensor(states[:, i % RING], b_dup[:, par, s0:s0 + SPI, :],
                                            dup[:, par, 1, h, g, :].unsqueeze(1).broadcast_to([P, SPI, N]),
                                            ALU.mult).then_inc(dbu_ready, 1)
                    if i == 11 and not last:
                        delta(n + 1, 1 - par)

            over_pairs(pool, body)

        @block.vector
        def _(dve):
            nc.vector.memset(da[:].rearrange("p k s (b t) -> p (k s b) t", b=2)[:, :, 0:1], 0.0).then_inc(da_zeroed, 1)
            dve.wait_ge(da_zeroed, 1)

            def softplus(m):
                dve.wait_ge(sp_one, m + 1)
                nc.vector.scalar_tensor_tensor(absx, onep[:], -1.0, absx, ALU.add, ALU.subtract).then_inc(sp_lost, 1)
                dve.wait_ge(sp_lost, m + 1)
                nc.vector.tensor_tensor(relux, relux, absx, ALU.subtract).then_inc(sp_fixed, 1)

            def split(m, par):
                dve.wait_ge(c_hi, m + 1)
                nc.vector.tensor_tensor(bcf[64:P, :], bcf[64:P, :], c3[64:P, par, :], ALU.subtract).then_inc(c_rest, 1)

            def low(m, par):
                dve.wait_ge(c_mid, m + 1)
                nc.vector.tensor_tensor(c3[96:P, par, :], bcf[96:P, :], c3[96:P, par, :], ALU.subtract).then_inc(c3_ready, 1)

            def times_c(n, i):
                dve.wait_ge(scan_done, ITEMS * n + i + 1)
                if i % 2 == 0:
                    dve.wait_ge(cb_ready, STEPS * n + i // 2 + 1)
                nc.vector.tensor_tensor(states[:, i % RING], states[:, i % RING], cb[:], ALU.mult).then_inc(hc_ready, 1)

            def gate(n, par, h):
                dve.wait_ge(sum_done, STEPS * n + 4 * h + 4)
                if h == 0:
                    dve.wait_ge(silu_done, n + 2)
                nc.vector.tensor_tensor(uz[:, par, h, :], yp[:], uz[:, par, h, :], ALU.mult).then_inc(gate_done, 1)

            softplus(0)
            split(0, 0)
            low(0, 0)

            def body(n, par, uses, first, last):
                for i in range(ITEMS):
                    dve.wait_ge(da_ready, ITEMS * n + i + 1)
                    dve.wait_ge(dbu_ready, ITEMS * n + i + 1)
                    nc.vector.tensor_tensor_scan(states[:, i % RING].rearrange("p s t -> p (s t)"),
                                                 da[:, i % 2].rearrange("p s t -> p (s t)"),
                                                 states[:, i % RING].rearrange("p s t -> p (s t)"),
                                                 0.0, ALU.mult, ALU.add).then_inc(scan_done, 1)
                    if i:
                        times_c(n, i - 1)
                    elif not first:
                        times_c(n - 1, ITEMS - 1)
                    if i == 2 and not first:
                        gate(n - 1, 1 - par, 1)
                    if i == 10:
                        gate(n, par, 0)
                    if i == 6 and not last:
                        softplus(n + 1)
                    if i == 10 and not last:
                        split(n + 1, 1 - par)
                    if i == 12 and not last:
                        low(n + 1, 1 - par)

            over_pairs(dve, body)
            times_c(PAIRS - 1, ITEMS - 1)
            gate(PAIRS - 1, (PAIRS - 1) % 2, 1)
            dve.wait_ge(gate_done, 2 * PAIRS)

        @block.sync
        def _(sp):
            def spread(m, par, uses):
                sp.wait_ge(c_hi, m + 1)
                if not (isinstance(m, int) and m < 2):
                    sp.wait_ge(b_in[par], 32 * uses)
                    sp.wait_ge(dbu_ready, ITEMS * (m - 1))
                    sp.wait_ge(da_ready, ITEMS * (m - 1))
                sp.dma_start(b_rows[par], bcf[16:32, :]).then_inc(rows_out[par], 16)
                sp.wait_ge(rows_out[par], 16 * uses + 16)
                for sh in range(2):
                    sp.dma_start(b_dup[64 * sh:64 * sh + 64, par],
                                 b_rows[par, NSP * sh:NSP * sh + NSP, :].unsqueeze(0).broadcast_to([64, NSP, N])
                                 ).then_inc(b_in[par], 16)
                for h in range(H2):
                    sp.wait_ge(du_ready[h], m + 1)
                    for g in range(2):
                        for sh in range(2):
                            sp.dma_start(dup[64 * sh:64 * sh + 64, par, :, h, g, :],
                                         dd[64 * g:64 * g + 64, :, h]).then_inc(dup_in[par][h], 16)

            spread(0, 0, 0)
            spread(1, 1, 0)
            with sp.Fori(0, (PAIRS - 2) // 2) as j:
                spread(2 * j + 2, 0, j + 1)
                spread(2 * j + 3, 1, j + 1)
            for i in range(2):
                sp.wait_ge(rows_out[i], 16 * PAIRS // 2)
                sp.wait_ge(b_in[i], 32 * PAIRS // 2)


def experts(nc, a, X, O, xhT, ident, eps, out_v, k):
    B, S, DM, TILES = (k[n] for n in ("B", "S", "DM", "TILES"))
    E, F = a["wgT"].shape[1:]
    CAP = int(S * 2.0 / E)
    FH = F // P
    PAIRS, N, CH = B // 2, 2 * S, 2 * S // P
    GB = P // E
    GROUPS = B // GB
    SLOTS = E * CAP
    EG = SLOTS // P
    HB = B // 2
    Y = O

    with ExitStack() as ctx:
        def sb(name, shape, dt=F32, c=ctx):
            return c.enter_context(nc.sbuf_tensor(name, shape, dt))

        def ps(name, shape, c):
            return c.enter_context(nc.psum_tensor(name, shape, F32))

        def sems(c, *names):
            return [c.enter_context(nc.semaphore(n)) for n in names]

        mvf = sb("mvf", [P, TILES, 2])
        rstdf = sb("rstdf", [P, TILES])
        gate_wT = sb("gate_wT", [P, E])
        wsgT = sb("wsgT", [P, F])
        wsuT = sb("wsuT", [P, F])
        wsdT = sb("wsdT", [P, FH, DM])
        L = sb("L", [P, TILES, E])
        mask_e = sb("mask_e", [P, E])
        mask_b = sb("mask_b", [P, GB])
        pick_b = sb("pick_b", [P, GB, P], BF16)
        row_t = sb("row_t", [P, S])
        col_t = sb("col_t", [P, 2])
        idx_x = sb("idx_x", [P, GROUPS, SLOTS], BF16)
        slot_i = sb("slot_i", [P, EG, GROUPS, GB])
        slot_w = sb("slot_w", [P, EG, GROUPS, GB])

        with ExitStack() as c:
            G4, GT = 4, TILES // 4
            st = sb("st", [P, TILES, 6], c=c)
            mvo = sb("mvo", [P, TILES, 2], c=c)
            part = sb("part", [P, 2, TILES], c=c)
            comb_ready, = sems(c, "comb_ready")
            lno = sb("lno", [P, 2, TILES], c=c)
            rstdo = sb("rstdo", [P, TILES], c=c)
            i_t = sb("i_t", [P, S], mybir.dt.int32, c=c)
            i_p = sb("i_p", [P, 2], mybir.dt.int32, c=c)
            wf_loaded, ones_set, masks_ready, iota_ready = sems(c, "wf_loaded", "ones_set", "masks_ready", "iota_ready")
            so_ready, mo_ready, lo_ready, ro_ready = sems(c, "so_ready", "mo_ready", "lo_ready", "ro_ready")
            on_ready, x_ready, sx_ready, mx_ready = sems(c, "on_ready", "x_ready", "sx_ready", "mx_ready")
            lx_ready, rx_ready, copied = sems(c, "lx_ready", "rx_ready", "copied")
            block = c.enter_context(nc.Block())

            def tile_of(v, t):
                g, i = t
                return v[:, bass.ds(g * (GT // 2) + i // 2, 1), i % 2, :]

            @block.sync
            def _(sp):
                for tile, name in ((gate_wT, "gate_wT"), (wsgT, "wsgT"), (wsuT, "wsuT"), (wsdT, "wsdT")):
                    sp.dma_start(tile[:], a[name]).then_inc(wf_loaded, 16)
                sp.wait_ge(wf_loaded, 64)

            @block.gpsimd
            def _(pool):
                nc.gpsimd.memset(mask_e[:], 0.0).then_inc(ones_set, 1)
                nc.gpsimd.memset(mask_b[:], 1.0).then_inc(ones_set, 1)
                nc.gpsimd.iota(i_t[:], pattern=[[1, S]], base=0, channel_multiplier=0).then_inc(iota_ready, 1)
                nc.gpsimd.iota(i_p[:], pattern=[[P, 2]], base=0, channel_multiplier=1).then_inc(iota_ready, 1)
                pool.wait_ge(ones_set, 2)
                nc.gpsimd.affine_select(out=mask_b[:], in_=mask_b[:], compare_op=ALU.is_ge, fill=0.0, base=0,
                                        pattern=[[-E, GB]], channel_multiplier=1).then_inc(masks_ready, 1)
                pool.wait_ge(masks_ready, 1)
                nc.gpsimd.affine_select(out=mask_b[:], in_=mask_b[:], compare_op=ALU.is_ge, fill=0.0, base=E - 1,
                                        pattern=[[E, GB]], channel_multiplier=-1).then_inc(masks_ready, 1)
                for n in range(GB):
                    if n:
                        pool.wait_ge(masks_ready, n + 2)
                    nc.gpsimd.affine_select(out=mask_e[:], in_=mask_e[:], compare_op=ALU.not_equal, fill=1.0,
                                            base=-E * n, pattern=[[-1, E]], channel_multiplier=1).then_inc(masks_ready, 1)
                with pool.Fori(0, G4) as g:
                    pool.wait_ge(on_ready, GT * g + GT)
                    gx = X[:, bass.ds(g * GT, GT), :]
                    nc.gpsimd.tensor_tensor(gx.rearrange("p (b c) d -> p b c d", c=2), gx.rearrange("p (b c) d -> p b c d", c=2),
                                            O[:, bass.ds(g * (GT // 2), GT // 2)], ALU.add).then_inc(x_ready, 1)

            @block.scalar
            def _(act):
                for mvt, r, l, ready, l_ready, r_ready in ((mvo, rstdo, 0, mo_ready, lo_ready, ro_ready),
                                                           (mvf, rstdf, 1, mx_ready, lx_ready, rx_ready)):
                    with act.Fori(0, G4) as g:
                        act.wait_ge(ready, 2 * g + 2)
                        nc.scalar.activation(lno[:, l, bass.ds(g * GT, GT)], mvt[:, bass.ds(g * GT, GT), 1], ACT.Ln,
                                             scale=1.0 / P, bias=eps[:, 0:1]).then_inc(l_ready, 1)
                        act.wait_ge(l_ready, g + 1)
                        nc.scalar.activation(r[:, bass.ds(g * GT, GT)], lno[:, l, bass.ds(g * GT, GT)], ACT.Exp,
                                             scale=-0.5).then_inc(r_ready, 1)
                act.wait_ge(rx_ready, G4)

            @block.vector
            def _(dve):
                def statistics(which, source, s_ready, mvt, m_ready, before=None):
                    with dve.Fori(0, G4) as g:
                        if before is not None:
                            dve.wait_ge(before, g + 1)
                        for i in range(GT):
                            nc.vector.bn_stats(st[:, bass.ds(g * GT + i, 1), :], source(g, i)).then_inc(s_ready, 1)
                        dve.wait_ge(s_ready, GT * g + GT)
                        gs = bass.ds(g * GT, GT)
                        s_ap, d_ap = part[:, 0, gs], part[:, 1, gs]
                        nc.vector.tensor_tensor(s_ap, st[:, gs, 1], st[:, gs, 4], ALU.add).then_inc(comb_ready, 1)
                        nc.vector.tensor_tensor(d_ap, st[:, gs, 1], st[:, gs, 4], ALU.subtract).then_inc(comb_ready, 1)
                        nc.vector.tensor_tensor(mvt[:, gs, 1], st[:, gs, 2], st[:, gs, 5], ALU.add).then_inc(comb_ready, 1)
                        dve.wait_ge(comb_ready, 4 * g + 4 * G4 * which + 3)
                        nc.vector.tensor_scalar(mvt[:, gs, 0], s_ap, 0.5, None, ALU.mult).then_inc(m_ready, 1)
                        nc.vector.scalar_tensor_tensor(d_ap, d_ap, P / 4, d_ap, ALU.mult, ALU.mult).then_inc(comb_ready, 1)
                        dve.wait_ge(comb_ready, 4 * g + 4 * G4 * which + 4)
                        nc.vector.tensor_tensor(mvt[:, gs, 1], mvt[:, gs, 1], d_ap, ALU.add).then_inc(m_ready, 1)

                statistics(0, lambda g, i: tile_of(O, (g, i)), so_ready, mvo, mo_ready)
                with dve.Fori(0, G4) as g:
                    dve.wait_ge(ro_ready, g + 1)
                    for i in range(GT):
                        o = tile_of(O, (g, i))
                        nc.vector.tensor_scalar(o, o, mvo[:, bass.ds(g * GT + i, 1), 0], rstdo[:, bass.ds(g * GT + i, 1)],
                                                ALU.subtract, ALU.mult).then_inc(on_ready, 1)
                dve.wait_ge(iota_ready, 2)
                nc.vector.tensor_copy(row_t[:], i_t[:]).then_inc(copied, 1)
                nc.vector.tensor_copy(col_t[:], i_p[:]).then_inc(copied, 1)
                dve.wait_ge(masks_ready, 2 + GB)
                nc.vector.tensor_copy(pick_b[:], mask_b[:].unsqueeze(2).broadcast_to([P, GB, P])).then_inc(copied, 1)
                statistics(1, lambda g, i: X[:, bass.ds(g * GT + i, 1), :], sx_ready, mvf, mx_ready, before=x_ready)
                dve.wait_ge(mx_ready, 2 * G4)
                dve.wait_ge(copied, 3)

        def normed(dve, dst, t):
            return nc.vector.tensor_scalar(dst, X[:, bass.ds(t, 1), :], mvf[:, bass.ds(t, 1), 0], rstdf[:, bass.ds(t, 1)],
                                           ALU.subtract, ALU.mult)

        with ExitStack() as c:
            xf = sb("xf", [P, 2, CH, DM], c=c)
            hT = sb("hT", [P, 2, N], c=c)
            gl = sb("gl", [P, FH, N], c=c)
            hs = sb("hs", [P, FH, N], c=c)
            tp, lp, yp = ps("tp3", [P, N], c), ps("lp3", [P, N], c), ps("yp3", [P, N], c)
            gp, up = ps("gp", [P, FH, N], c), ps("up", [P, FH, N], c)
            xf_ready, tp_ready, hT_ready, lp_ready, lp_free = sems(c, "xf_ready", "tp3_ready", "hT_ready", "lp_ready", "lp_free")
            gp_ready, gl_ready, up_ready, hs_ready, yp_ready, yp_free = sems(
                c, "gp_ready", "gl_ready", "up_ready", "hs_ready", "yp_ready", "yp_free")
            block = c.enter_context(nc.Block())

            def pairs(eng, body):
                body(0, 0)
                with eng.Fori(0, PAIRS // 2 - 1) as j:
                    body(2 * j + 1, 1)
                    body(2 * j + 2, 0)
                body(PAIRS - 1, 1)

            def first(n):
                return isinstance(n, int) and n == 0

            @block.vector
            def _(dve):
                def norm(n, par):
                    if not (isinstance(n, int) and n < 2):
                        dve.wait_ge(tp_ready, n - 1)
                    for i in range(CH):
                        ins = normed(dve, xf[:, par, i, :], CH * n + i)
                    ins.then_inc(xf_ready, 1)

                def body(n, par):
                    if not (isinstance(n, int) and n == PAIRS - 1):
                        norm(n + 1, 1 - par)
                    dve.wait_ge(lp_ready, n + 1)
                    nc.vector.tensor_copy(L[:, bass.ds(CH * n, CH), :], lp[:, 0:CH * E].rearrange("p (c e) -> p c e", e=E)
                                          ).then_inc(lp_free, 1)
                    if not first(n):
                        dve.wait_ge(yp_ready, n)
                    for h in range(FH):
                        dve.wait_ge(up_ready, FH * n + h + 1)
                        dve.wait_ge(gl_ready, FH * n + h + 1)
                        nc.vector.tensor_tensor(hs[:, h], gl[:, h], up[:, h], ALU.mult).then_inc(hs_ready, 1)

                norm(0, 0)
                pairs(dve, body)
                dve.wait_ge(hs_ready, FH * PAIRS)

            @block.tensor
            def _(pe):
                def turn(n, par):
                    pe.wait_ge(xf_ready, n + 1)
                    if not first(n):
                        pe.wait_ge(hT_ready, n)
                    for i in range(CH):
                        mm = nc.tensor.transpose(tp[:, i * P:(i + 1) * P], xf[:, par, i, :], ident[:])
                    mm.then_inc(tp_ready, 1)

                def body(n, par):
                    pe.wait_ge(hT_ready, n + 1)
                    if not first(n):
                        pe.wait_ge(lp_free, n)
                    for i in range(CH):
                        mm = nc.tensor.matmul(lp[:, i * E:(i + 1) * E], hT[:, par, i * P:(i + 1) * P], gate_wT[:],
                                              start=True, stop=True)
                    mm.then_inc(lp_ready, 1)
                    for h in range(FH):
                        if not first(n):
                            pe.wait_ge(gl_ready, FH * (n - 1) + h + 1)
                            pe.wait_ge(hs_ready, FH * (n - 1) + h + 1)
                        nc.tensor.matmul(gp[:, h], wsgT[:, h * P:(h + 1) * P], hT[:, par, :], start=True, stop=True
                                         ).then_inc(gp_ready, 1)
                        nc.tensor.matmul(up[:, h], wsuT[:, h * P:(h + 1) * P], hT[:, par, :], start=True, stop=True
                                         ).then_inc(up_ready, 1)
                    if not (isinstance(n, int) and n == PAIRS - 1):
                        turn(n + 1, 1 - par)
                    pe.wait_ge(hs_ready, FH * n + FH)
                    if not first(n):
                        pe.wait_ge(yp_free, n)
                    for i in range(CH):
                        for h in range(FH):
                            mm = nc.tensor.matmul(yp[:, i * DM:(i + 1) * DM], hs[:, h, i * P:(i + 1) * P], wsdT[:, h, :],
                                                  start=(h == 0), stop=(h == FH - 1))
                    mm.then_inc(yp_ready, 1)

                turn(0, 0)
                pairs(pe, body)

            @block.scalar
            def _(act):
                def turned(n, par):
                    act.wait_ge(tp_ready, n + 1)
                    if not (isinstance(n, int) and n < 2):
                        act.wait_ge(up_ready, FH * (n - 1))
                    nc.scalar.activation(hT[:, par, :], tp[:], ACT.Copy).then_inc(hT_ready, 1)

                def body(n, par):
                    for h in range(FH):
                        act.wait_ge(gp_ready, FH * n + h + 1)
                        if not first(n):
                            act.wait_ge(hs_ready, FH * (n - 1) + h + 1)
                        nc.scalar.activation(gl[:, h], gp[:, h], ACT.Gelu).then_inc(gl_ready, 1)
                    if not (isinstance(n, int) and n == PAIRS - 1):
                        turned(n + 1, 1 - par)
                    act.wait_ge(yp_ready, n + 1)
                    nc.scalar.activation(Y[:, bass.ds(2 * n, 2)], yp[:].rearrange("p (b c d) -> p b c d", b=2, d=DM), ACT.Copy
                                         ).then_inc(yp_free, 1)

                turned(0, 0)
                pairs(act, body)
                act.wait_ge(yp_free, PAIRS)

        with ExitStack() as c:
            top = sb("top", [P, TILES], c=c)
            den = sb("den", [P, TILES], c=c)
            scores = sb("scores", [P, 2, B, E], c=c)
            rest = sb("rest", [P, GROUPS, 2, S], c=c)
            best = sb("best", [P, GROUPS, CAP], c=c)
            best_i = sb("best_i", [P, GROUPS, CAP], mybir.dt.uint32, c=c)
            best_f = sb("best_f", [P, GROUPS, CAP], c=c)
            w_x = sb("w_x", [P, GROUPS, SLOTS], c=c)
            i_x = sb("i_x", [P, GROUPS, SLOTS], c=c)
            sp_t = [ps(f"sp_t{g}", [P, 2 * P], c) for g in range(GROUPS)]
            sl = ps("sl", [P, GROUPS, 2, EG, GB], c)
            soft, exp_done, sc_ready, turned_s, found, taken, spread, expanded, sl_ready, sl_out = sems(
                c, "soft", "exp_done", "sc_ready", "turned_s", "found", "taken", "spread", "expanded", "sl_ready", "sl_out")
            block = c.enter_context(nc.Block())

            @block.scalar
            def _(act):
                act.wait_ge(soft, 2)
                nc.scalar.activation(L[:], L[:], ACT.Exp).then_inc(exp_done, 1)

            @block.vector
            def _(dve):
                wide = [P, TILES, E]
                nc.vector.tensor_reduce(top[:], L[:], AX.X, ALU.max).then_inc(soft, 1)
                dve.wait_ge(soft, 1)
                nc.vector.tensor_tensor(L[:], L[:], top[:].unsqueeze(2).broadcast_to(wide), ALU.subtract).then_inc(soft, 1)
                dve.wait_ge(exp_done, 1)
                nc.vector.tensor_reduce(den[:], L[:], AX.X, ALU.add).then_inc(soft, 1)
                dve.wait_ge(soft, 3)
                nc.vector.reciprocal(den[:], den[:]).then_inc(soft, 1)
                dve.wait_ge(soft, 4)
                lv = L[:].rearrange("p (b c) e -> p c b e", c=2)
                dv = den[:].rearrange("p (b c) -> p c b", c=2)
                for h in range(2):
                    nc.vector.tensor_tensor(scores[:, h], lv[:, h], dv[:, h].unsqueeze(2).broadcast_to([P, B, E]),
                                            ALU.mult).then_inc(sc_ready, 1)
                nf = nt = 0
                for r in range(CAP // 8):
                    for g in range(GROUPS):
                        src = sp_t[g][:] if r == 0 else rest[:, g, (r - 1) % 2, :]
                        if r == 0:
                            dve.wait_ge(turned_s, g + 1)
                        else:
                            dve.wait_ge(taken, GROUPS * (r - 1) + g + 1)
                        b8 = best[:, g, 8 * r:8 * r + 8]
                        nc.vector.max(b8, src).then_inc(found, 1)
                        nf += 1
                        dve.wait_ge(found, nf)
                        nc.vector.max_index(best_i[:, g, 8 * r:8 * r + 8], b8, src).then_inc(spread, 1)
                        if r < CAP // 8 - 1:
                            nc.vector.match_replace(rest[:, g, r % 2, :], b8, src, -1.0).then_inc(taken, 1)
                n = CAP // 8 * GROUPS
                dve.wait_ge(spread, n)
                nc.vector.tensor_copy(best_f[:], best_i[:]).then_inc(spread, 1)
                dve.wait_ge(spread, n + 1)
                me = mask_e[:].unsqueeze(2).broadcast_to([P, E, CAP])
                for g in range(GROUPS):
                    nc.vector.tensor_tensor(i_x[:, g].rearrange("p (e c) -> p e c", e=E), me,
                                            best_f[:, g].unsqueeze(1).broadcast_to([P, E, CAP]), ALU.mult).then_inc(expanded, 1)
                    nc.vector.tensor_tensor(w_x[:, g].rearrange("p (e c) -> p e c", e=E), me,
                                            best[:, g].unsqueeze(1).broadcast_to([P, E, CAP]), ALU.mult).then_inc(expanded, 1)
                dve.wait_ge(expanded, 2 * GROUPS)
                nc.vector.tensor_copy(idx_x[:], i_x[:]).then_inc(sl_out, 1)
                dve.wait_ge(sl_ready, 1)
                nc.vector.tensor_copy(slot_i[:], sl[:, :, 0].rearrange("p g e b -> p e g b")).then_inc(sl_out, 1)
                nc.vector.tensor_copy(slot_w[:], sl[:, :, 1].rearrange("p g e b -> p e g b")).then_inc(sl_out, 1)
                dve.wait_ge(sl_out, 3)

            @block.tensor
            def _(pe):
                pe.wait_ge(sc_ready, 2)
                for g in range(GROUPS):
                    for h in range(2):
                        mm = nc.tensor.transpose(sp_t[g][:, h * P:(h + 1) * P],
                                                 scores[:, h, g * GB:(g + 1) * GB, :].rearrange("p b e -> p (b e)"), ident[:])
                    mm.then_inc(turned_s, 1)
                pe.wait_ge(expanded, 2 * GROUPS)
                for g in range(GROUPS):
                    for w, x in enumerate((i_x, w_x)):
                        for e in range(EG):
                            mm = nc.tensor.matmul(sl[:, g, w, e, :], x[:, g, e * P:(e + 1) * P], mask_b[:], start=True, stop=True)
                mm.then_inc(sl_ready, 1)

        XG = sb("XG", [P, E, HB, CAP])
        for half in range(2):
            b0 = half * HB
            gather(nc, a, XG, normed, idx_x, pick_b, col_t, b0, k, half)
            run_experts(nc, a, XG, half, DM)
            scatter(nc, a, X, Y, XG, row_t, slot_i, slot_w, ident, eps, out_v, b0, k, half)


def by_two(eng, count, body, tail=1):
    body(0, 0)
    with eng.Fori(0, (count - tail) // 2) as j:
        body(2 * j + 1, 1)
        body(2 * j + 2, 0)
    for n in range(count - tail, count):
        body(n, n % 2)


def is_at(n, *values):
    return isinstance(n, int) and n in values


def gather(nc, a, XG, normed, idx_x, pick_b, col_t, b0, k, half):
    S = k["S"]
    E, HB, CAP = XG.shape[1:]
    SLOTS, GB, DM = E * CAP, pick_b.shape[1], k["DM"]
    with ExitStack() as c:
        xt = c.enter_context(nc.sbuf_tensor(f"xt{half}", [P, 2, 2, DM], F32))
        hot = c.enter_context(nc.sbuf_tensor(f"hot{half}", [P, 2, 2, SLOTS], F32))
        ip = c.enter_context(nc.psum_tensor(f"ip{half}", [P, 2, SLOTS], F32))
        xp = c.enter_context(nc.psum_tensor(f"xp{half}", [P, 2, SLOTS], F32))
        xt_ready, ip_ready, hot_ready, xp_ready, xp_free = [
            c.enter_context(nc.semaphore(f"{n}{half}")) for n in ("xt_ready", "ip_ready", "hot_ready", "xp_ready", "xp_free")]
        block = c.enter_context(nc.Block())

        @block.tensor
        def _(pe):
            def indices(n, par, g, b):
                if not is_at(n, 0, 1):
                    pe.wait_ge(hot_ready, n - 1)
                nc.tensor.matmul(ip[:, par], pick_b[:, bass.ds(b, 1), :], idx_x[:, b0 // GB + g, :], start=True, stop=True
                                 ).then_inc(ip_ready, 1)

            def take(n, par):
                pe.wait_ge(xt_ready, n + 1)
                pe.wait_ge(hot_ready, n + 1)
                if not is_at(n, 0, 1):
                    pe.wait_ge(xp_free, n - 1)
                for h in range(2):
                    mm = nc.tensor.matmul(xp[:, par], xt[:, par, h, :], hot[:, par, h, :], start=(h == 0), stop=(h == 1))
                mm.then_inc(xp_ready, 1)

            indices(0, 0, 0, 0)
            for g in range(HB // GB):
                n = GB * g
                indices(n + 1, 1, g, 1)
                take(n, 0)
                with pe.Fori(0, GB // 2 - 1) as j:
                    for i in range(2):
                        indices(n + 2 * j + i + 2, i, g, 2 * j + i + 2)
                        take(n + 2 * j + i + 1, 1 - i)
                if g < HB // GB - 1:
                    indices(n + GB, 0, g + 1, 0)
                take(n + GB - 1, 1)

        @block.vector
        def _(dve):
            def body(n, par):
                if not is_at(n, 0, 1):
                    dve.wait_ge(xp_ready, n - 1)
                for h in range(2):
                    ins = normed(dve, xt[:, par, h, :], 2 * b0 + 2 * n + h)
                ins.then_inc(xt_ready, 1)
                dve.wait_ge(ip_ready, n + 1)
                for h in range(2):
                    ins = nc.vector.tensor_scalar(hot[:, par, h, :], ip[:, par], col_t[:, h:h + 1], None, ALU.is_equal)
                ins.then_inc(hot_ready, 1)

            by_two(dve, HB, body)

        @block.scalar
        def _(act):
            def body(n, par):
                act.wait_ge(xp_ready, n + 1)
                nc.scalar.activation(XG[:, :, bass.ds(n, 1), :], xp[:, par].rearrange("p (e c) -> p e c", e=E), ACT.Copy
                                     ).then_inc(xp_free, 1)

            by_two(act, HB, body)
            act.wait_ge(xp_free, HB)


def run_experts(nc, a, XG, half, DM):
    E, HB, CAP = XG.shape[1:]
    F = a["wgT"].shape[2]
    FH, M = F // P, HB * CAP
    WB = 2
    with ExitStack() as c:
        def sb(name, shape):
            return c.enter_context(nc.sbuf_tensor(f"{name}{half}", shape, F32))

        wg, wu, wd = sb("wg", [P, WB, F]), sb("wu", [P, WB, F]), sb("wd", [P, WB, FH, DM])
        gl, hx = sb("glx", [P, FH, M]), sb("hx", [P, FH, M])
        gp = c.enter_context(nc.psum_tensor(f"gpx{half}", [P, FH, M], F32))
        up = c.enter_context(nc.psum_tensor(f"upx{half}", [P, FH, M], F32))
        dp = c.enter_context(nc.psum_tensor(f"dpx{half}", [P, 2, M], F32))
        w_in = [c.enter_context(nc.semaphore(f"we{half}{i}")) for i in range(WB)]
        gp_ready, up_ready, gl_ready, hx_ready, dp_ready, dp_free = [
            c.enter_context(nc.semaphore(f"{n}x{half}")) for n in ("gp_ready", "up_ready", "gl_ready", "hx_ready", "dp_ready", "dp_free")]
        block = c.enter_context(nc.Block())

        @block.sync
        def _(sp):
            def body(n, par):
                if not is_at(n, 0, 1):
                    sp.wait_ge(dp_ready, n - 1)
                sp.dma_start(wg[:, par], a["wgT"][:, bass.ds(n, 1), :]).then_inc(w_in[par], 16)
                sp.dma_start(wu[:, par], a["wuT"][:, bass.ds(n, 1), :]).then_inc(w_in[par], 16)
                sp.dma_start(wd[:, par], a["wdT"][:, bass.ds(n, 1)]).then_inc(w_in[par], 16)

            by_two(sp, E, body)

        @block.tensor
        def _(pe):
            def up_gate(n, par, uses):
                pe.wait_ge(w_in[par], 48 * uses + 48)
                for h in range(FH):
                    if not is_at(n, 0):
                        pe.wait_ge(gl_ready, FH * (n - 1) + h + 1)
                        pe.wait_ge(hx_ready, FH * (n - 1) + h + 1)
                    x = XG[:, bass.ds(n, 1)]
                    nc.tensor.matmul(gp[:, h], wg[:, par, h * P:(h + 1) * P], x, start=True, stop=True).then_inc(gp_ready, 1)
                    nc.tensor.matmul(up[:, h], wu[:, par, h * P:(h + 1) * P], x, start=True, stop=True).then_inc(up_ready, 1)

            def down(n, par):
                pe.wait_ge(hx_ready, FH * n + FH)
                if not is_at(n, 0, 1):
                    pe.wait_ge(dp_free, n - 1)
                for h in range(FH):
                    mm = nc.tensor.matmul(dp[:, par], wd[:, par, h, :], hx[:, h], start=(h == 0), stop=(h == FH - 1))
                mm.then_inc(dp_ready, 1)

            up_gate(0, 0, 0)
            up_gate(1, 1, 0)
            down(0, 0)
            with pe.Fori(0, E // 2 - 1) as j:
                up_gate(2 * j + 2, 0, j + 1)
                down(2 * j + 1, 1)
                up_gate(2 * j + 3, 1, j + 1)
                down(2 * j + 2, 0)
            down(E - 1, 1)

        @block.scalar
        def _(act):
            def gelus(n):
                for h in range(FH):
                    act.wait_ge(gp_ready, FH * n + h + 1)
                    if not is_at(n, 0):
                        act.wait_ge(hx_ready, FH * (n - 1) + h + 1)
                    nc.scalar.activation(gl[:, h], gp[:, h], ACT.Gelu).then_inc(gl_ready, 1)

            def evacuate(n, par):
                act.wait_ge(dp_ready, n + 1)
                nc.scalar.activation(XG[:, bass.ds(n, 1)], dp[:, par].rearrange("p (b c) -> p b c", b=HB), ACT.Copy
                                     ).then_inc(dp_free, 1)

            gelus(0)
            gelus(1)
            evacuate(0, 0)
            with act.Fori(0, E // 2 - 1) as j:
                gelus(2 * j + 2)
                evacuate(2 * j + 1, 1)
                gelus(2 * j + 3)
                evacuate(2 * j + 2, 0)
            evacuate(E - 1, 1)
            act.wait_ge(dp_free, E)

        @block.vector
        def _(dve):
            def body(n, par):
                for h in range(FH):
                    dve.wait_ge(gl_ready, FH * n + h + 1)
                    dve.wait_ge(up_ready, FH * n + h + 1)
                    if not is_at(n, 0):
                        dve.wait_ge(dp_ready, n)
                    nc.vector.tensor_tensor(hx[:, h], gl[:, h], up[:, h], ALU.mult).then_inc(hx_ready, 1)

            by_two(dve, E, body)
            dve.wait_ge(hx_ready, FH * E)


def scatter(nc, a, X, Y, XG, row_t, slot_i, slot_w, ident, eps, out_v, b0, k, half):
    S, DM = k["S"], k["DM"]
    E, HB, CAP = XG.shape[1:]
    SLOTS = E * CAP
    EG = slot_i.shape[1]
    slot_ib, slot_wb = (v[:].rearrange("p e g b -> p e (g b)") for v in (slot_i, slot_w))
    with ExitStack() as c:
        def sb(name, shape):
            return c.enter_context(nc.sbuf_tensor(f"{name}{half}", shape, F32))

        eT = sb("eT", [P, 2, SLOTS])
        eo = sb("eo", [P, 2, EG, DM])
        put = sb("put", [P, 2, EG, S])
        y = sb("y", [P, 2, 2, DM])
        stt, mvt, lnt, rst = sb("stt", [P, 2, 2, 6]), sb("mvt", [P, 2, 2, 2]), sb("lnt", [P, 2, 2]), sb("rst", [P, 2, 2])
        tp = c.enter_context(nc.psum_tensor(f"tps{half}", [P, 2, SLOTS], F32))
        yp = c.enter_context(nc.psum_tensor(f"yss{half}", [P, 2, 512], F32))
        (eT_ready, tp_ready, eo_ready, put_ready, yp_ready, y_ready, st_ready, mv_ready, ln_ready, r_ready, n_ready,
         x_ready) = [c.enter_context(nc.semaphore(f"{n}s{half}")) for n in (
             "eT_ready", "tp_ready", "eo_ready", "put_ready", "yp_ready", "y_ready", "st_ready", "mv_ready", "ln_ready",
             "r_ready", "n_ready", "x_ready")]
        stored = c.enter_context(nc.semaphore(f"stored{half}"))
        block = c.enter_context(nc.Block())

        @block.gpsimd
        def _(pool):
            def copy(n, par):
                if not is_at(n, 0, 1):
                    pool.wait_ge(tp_ready, n - 1)
                nc.gpsimd.tensor_copy(eT[:, par].rearrange("p (e c) -> p e c", e=E), XG[:, :, bass.ds(n, 1), :]
                                      ).then_inc(eT_ready, 1)

            def body(n, par):
                if not is_at(n, HB - 2, HB - 1):
                    copy(n + 2, par)
                pool.wait_ge(n_ready, n + 1)
                xv = X[:, bass.ds(2 * b0 + 2 * n, 2), :]
                nc.gpsimd.tensor_tensor(xv, xv, y[:, par], ALU.add).then_inc(x_ready, 1)

            copy(0, 0)
            copy(1, 1)
            by_two(pool, HB, body, 3)

        @block.tensor
        def _(pe):
            def turn(n, par):
                pe.wait_ge(eT_ready, n + 1)
                if not is_at(n, 0, 1):
                    pe.wait_ge(eo_ready, n - 1)
                for g in range(EG):
                    mm = nc.tensor.transpose(tp[:, par, g * P:(g + 1) * P], eT[:, par, g * P:(g + 1) * P], ident[:])
                mm.then_inc(tp_ready, 1)

            def body(n, par):
                if not is_at(n, HB - 1):
                    turn(n + 1, 1 - par)
                pe.wait_ge(eo_ready, n + 1)
                pe.wait_ge(put_ready, n + 1)
                if not is_at(n, 0, 1):
                    pe.wait_ge(y_ready, n - 1)
                for h in range(2):
                    for g in range(EG):
                        mm = nc.tensor.matmul(yp[:, par, h * DM:(h + 1) * DM], put[:, par, g, h * P:(h + 1) * P],
                                              eo[:, par, g, :], start=(g == 0), stop=(g == EG - 1))
                mm.then_inc(yp_ready, 1)

            turn(0, 0)
            by_two(pe, HB, body)

        @block.scalar
        def _(act):
            def spread(n, par):
                act.wait_ge(tp_ready, n + 1)
                if not is_at(n, 0, 1):
                    act.wait_ge(yp_ready, n - 1)
                nc.scalar.activation(eo[:, par].rearrange("p g d -> p (g d)"), tp[:, par], ACT.Copy).then_inc(eo_ready, 1)

            def body(n, par):
                if not is_at(n, HB - 1):
                    spread(n + 1, 1 - par)
                act.wait_ge(mv_ready, 2 * n + 2)
                nc.scalar.activation(lnt[:, par], mvt[:, par, :, 1], ACT.Ln, bias=eps[:, 0:1]).then_inc(ln_ready, 1)
                act.wait_ge(ln_ready, n + 1)
                nc.scalar.activation(rst[:, par], lnt[:, par], ACT.Exp, scale=-0.5).then_inc(r_ready, 1)

            spread(0, 0)
            by_two(act, HB, body)

        @block.vector
        def _(dve):
            def places(n, par):
                if not is_at(n, 0, 1):
                    dve.wait_ge(yp_ready, n - 1)
                for e in range(EG):
                    ins = nc.vector.tensor_scalar(put[:, par, e, :], row_t[:], slot_ib[:, e, bass.ds(b0 + n, 1)],
                                                  slot_wb[:, e, bass.ds(b0 + n, 1)], ALU.is_equal, ALU.mult)
                ins.then_inc(put_ready, 1)

            def add(n, par):
                dve.wait_ge(yp_ready, n + 1)
                if not is_at(n, 0, 1):
                    dve.wait_ge(x_ready, n - 1)
                nc.vector.tensor_tensor(y[:, par], yp[:, par, 0:2 * DM].rearrange("p (c d) -> p c d", c=2),
                                        Y[:, bass.ds(b0 + n, 1)], ALU.add).then_inc(y_ready, 1)
                dve.wait_ge(y_ready, n + 1)
                for h in range(2):
                    nc.vector.bn_stats(stt[:, par, h, :], y[:, par, h, :]).then_inc(st_ready, 1)
                dve.wait_ge(st_ready, 2 * n + 2)

            def aggregate(n, par):
                for h in range(2):
                    nc.vector.bn_aggr(mvt[:, par, h, :], stt[:, par, h, :]).then_inc(mv_ready, 1)

            def norm(n, par):
                dve.wait_ge(r_ready, n + 1)
                for h in range(2):
                    ins = nc.vector.tensor_scalar(y[:, par, h, :], y[:, par, h, :], mvt[:, par, h, 0:1], rst[:, par, h:h + 1],
                                                  ALU.subtract, ALU.mult)
                ins.then_inc(n_ready, 1)

            def body(n, par):
                if not is_at(n, 0):
                    norm(n - 1, 1 - par)
                add(n, par)
                if not is_at(n, HB - 1):
                    places(n + 1, 1 - par)
                aggregate(n, par)

            places(0, 0)
            by_two(dve, HB, body)
            norm(HB - 1, (HB - 1) % 2)

        @block.sync
        def _(sp):
            with sp.Fori(0, HB // 2) as j:
                sp.wait_ge(x_ready, 2 * j + 2)
                sp.dma_start(out_v[:, bass.ds(2 * b0 + 4 * j, 4), :], X[:, bass.ds(2 * b0 + 4 * j, 4), :]).then_inc(stored, 16)
            sp.wait_ge(stored, 16 * (HB // 2))


def kernel(**inputs):
    import concourse.bacc as bacc
    from concourse.bass_utils import run_bass_kernel_spmd

    arrays = lay_out(inputs)
    nc = bacc.Bacc("TRN2", target_bir_lowering=False, num_devices=1)
    feeds, aps = {}, {}
    for name, v in arrays.items():
        feeds[f"in_{name}"] = v
        aps[name] = nc.dram_tensor(f"in_{name}", v.shape, mybir.dt.from_np(v.dtype), kind="ExternalInput").ap()
    shape = inputs["L0_attn_x"].shape
    out = nc.dram_tensor("out", shape, F32, kind="ExternalOutput").ap()
    build(nc, aps, out)
    r = run_bass_kernel_spmd(nc, [feeds], core_ids=[0])
    return r.results[0]["out"]


def lay_out(inputs):
    i = {n.removeprefix("L0_"): np.asarray(v) for n, v in inputs.items()}
    DI, E, F, D = i["attn_out_proj_w"].shape[0], *i["ffn_Wg"].shape

    def rows(w):
        return np.ascontiguousarray(w.reshape(-1, P, w.shape[1]).transpose(1, 0, 2))

    wx = i["attn_x_proj_w"]
    bc = np.concatenate([wx[:, DI + 16:DI + 32], wx[:, DI:DI + 16]], 1)
    return {
        "x": np.ascontiguousarray(i["attn_x"]),
        "w_u": np.ascontiguousarray(i["attn_in_proj_w"][:, 0:DI]),
        "w_z": np.ascontiguousarray(i["attn_in_proj_w"][:, DI:]),
        "conv_w": np.ascontiguousarray(i["attn_conv_w"][:, 0, :].T),
        "conv_b": np.ascontiguousarray(i["attn_conv_b"].reshape(-1, P).T),
        "w_xdT": rows(wx[:, 0:DI].T),
        "w_dt": rows(i["attn_dt_proj_w"]),
        "w_bc": rows(np.concatenate([bc] * 4, 1)),
        "dt_b": np.ascontiguousarray(i["attn_dt_proj_b"].reshape(-1, P).T),
        "w_out": rows(i["attn_out_proj_w"]),
        "a_log": np.ascontiguousarray(i["attn_A_log"].reshape(DI // 64, 64, 2, 8).transpose(2, 1, 0, 3).reshape(P, -1)),
        "dskip": np.ascontiguousarray(i["attn_D_param"].reshape(-1, P).T),
        "gate_wT": np.ascontiguousarray(i["ffn_gate_w"].T),
        "wgT": np.ascontiguousarray(i["ffn_Wg"].transpose(2, 0, 1)),
        "wuT": np.ascontiguousarray(i["ffn_Wu"].transpose(2, 0, 1)),
        "wdT": np.ascontiguousarray(i["ffn_Wd"].reshape(E, D, F // P, P).transpose(3, 0, 2, 1)),
        "wsgT": np.ascontiguousarray(i["ffn_Ws_g"].T),
        "wsuT": np.ascontiguousarray(i["ffn_Ws_u"].T),
        "wsdT": np.ascontiguousarray(i["ffn_Ws_d"].reshape(D, F // P, P).transpose(2, 1, 0)),
    }
```

```python
from contextlib import ExitStack

import numpy as np
import concourse.bass as bass
from concourse import mybir

F32 = mybir.dt.float32
BF16 = mybir.dt.bfloat16
ALU = mybir.AluOpType
ACT = mybir.ActivationFunctionType
AX = mybir.AxisListType

P = 128
EPS = 1e-5
LOG_EXP = "natural_log_exp_and_others"


def build(nc, a, out):
    B, S, DM = a["x"].shape
    TOK = B * S
    TILES = TOK // P
    DI = a["w_z"].shape[1]
    H2 = DI // P
    NG = DI // 64
    NSP = 8
    PAIRS = B // 2
    N = 2 * S
    CH = N // P
    STEPS = H2 * 4
    ITEMS = 2 * STEPS
    SPI = 2

    x_v = a["x"].rearrange("b (c p) d -> p (b c) d", p=P)
    out_v = out.rearrange("b (c p) d -> p (b c) d", p=P)
    b_rows = nc.dram_tensor("b_rows", (2, 16, N), F32, kind="Internal").ap()

    with ExitStack() as top:
        def sb(name, shape, dt=F32, ctx=top):
            return ctx.enter_context(nc.sbuf_tensor(name, shape, dt))

        def sem(name, ctx=top):
            return ctx.enter_context(nc.semaphore(name))

        X = sb("X", [P, TILES, DM])
        ident = sb("ident", [P, P])
        stats = sb("stats", [P, TILES, 6])
        mv = sb("mv", [P, TILES, 2])
        lnv = sb("lnv", [P, TILES])
        rstd = sb("rstd", [P, TILES])
        eps = sb("eps", [P, 1])
        xhT = sb("xhT", [P, B, S + 2])
        O = xhT[:, :, 0:S].rearrange("p b (c d) -> p b c d", d=DM)

        mamba(nc, a, X, xhT, O, ident, stats, mv, lnv, rstd, eps, x_v, b_rows,
              dict(B=B, S=S, DM=DM, TILES=TILES, DI=DI, H2=H2, NG=NG, NSP=NSP, PAIRS=PAIRS, N=N,
                   CH=CH, STEPS=STEPS, ITEMS=ITEMS, SPI=SPI))
        experts(nc, a, X, O, xhT, ident, eps, out_v, dict(B=B, S=S, DM=DM, TILES=TILES))


def mamba(nc, a, X, xhT, O, ident, stats, mv, lnv, rstd, eps, x_v, b_rows, k):
    B, S, DM, TILES, DI, H2, NG = (k[n] for n in ("B", "S", "DM", "TILES", "DI", "H2", "NG"))
    NSP, PAIRS, N, CH, STEPS, ITEMS, SPI = (
        k[n] for n in ("NSP", "PAIRS", "N", "CH", "STEPS", "ITEMS", "SPI"))
    RING = 8
    SP1 = S + 2
    with ExitStack() as ctx:
        def sb(name, shape, dt=F32):
            return ctx.enter_context(nc.sbuf_tensor(name, shape, dt))

        def sem(name):
            return ctx.enter_context(nc.semaphore(name))

        w_z = sb("w_z", [P, DI])
        w_conv = sb("w_conv", [P, 3, DI])
        conv_b = sb("conv_b", [P, H2])
        w_delta = sb("w_delta", [P, 2, DI])
        w_bc = sb("w_bc", [P, 2, P])
        dt_b = sb("dt_b", [P, H2])
        w_out = sb("w_out", [P, 2, DM])
        decay = sb("decay", [P, NG * NSP])
        dskip = sb("dskip", [P, H2])
        skip_diag = sb("skip_diag", [P, H2, P])
        fold = sb("fold", [P, 64])
        pick = sb("pick", [P, NSP, P], BF16)

        with ExitStack() as c0:
            w_xdT = c0.enter_context(nc.sbuf_tensor("w_xdT", [P, 2, DI], F32))
            w_dt = c0.enter_context(nc.sbuf_tensor("w_dt", [P, 2, DI], F32))
            w_u = c0.enter_context(nc.sbuf_tensor("w_u", [P, DI], F32))
            conv_rows = c0.enter_context(nc.sbuf_tensor("conv_rows", [P, 3, DI], F32))
            xh = c0.enter_context(nc.sbuf_tensor("xh", [P, 4, CH, DM], F32))
            tp = c0.enter_context(nc.psum_tensor("tp", [P, 4, 512], F32))
            wp = c0.enter_context(nc.psum_tensor("wp", [P, 2, 512], F32))
            x_in = [c0.enter_context(nc.semaphore(f"x_in{i}")) for i in range(4)]
            w_loaded = c0.enter_context(nc.semaphore("w_loaded"))
            conv_loaded = c0.enter_context(nc.semaphore("conv_loaded"))
            id_zero = c0.enter_context(nc.semaphore("id_zero"))
            id_ready = c0.enter_context(nc.semaphore("id_ready"))
            pads_ready = c0.enter_context(nc.semaphore("pads_ready"))
            exp_ready = c0.enter_context(nc.semaphore("exp_ready"))
            eps_ready = c0.enter_context(nc.semaphore("eps_ready"))
            stats_ready = c0.enter_context(nc.semaphore("stats_ready"))
            mv_ready = c0.enter_context(nc.semaphore("mv_ready"))
            ln_ready = c0.enter_context(nc.semaphore("ln_ready"))
            rstd_ready = c0.enter_context(nc.semaphore("rstd_ready"))
            xh_ready = c0.enter_context(nc.semaphore("xh_ready"))
            tp_ready = c0.enter_context(nc.semaphore("tp_ready"))
            tp_free = c0.enter_context(nc.semaphore("tp_free"))
            wp_ready = c0.enter_context(nc.semaphore("wp_ready"))
            fold_done = c0.enter_context(nc.semaphore("fold_done"))
            dve_done = c0.enter_context(nc.semaphore("dve_done"))
            act_done = c0.enter_context(nc.semaphore("act_done"))
            block = c0.enter_context(nc.Block())
            QT = TILES // 4
            small = [(w_u, "w_u"), (w_z, "w_z"), (conv_b, "conv_b"), (w_xdT, "w_xdT"), (w_dt, "w_dt"),
                     (w_bc, "w_bc"), (dt_b, "dt_b"), (w_out, "w_out"), (decay, "a_log"),
                     (dskip, "dskip")]

            @block.sync
            def _(sp):
                for i in range(4):
                    sp.dma_start(X[:, i * QT:(i + 1) * QT, :], x_v[:, i * QT:(i + 1) * QT, :]).then_inc(x_in[i], 16)

            @block.gpsimd
            def _(pool):
                nc.gpsimd.memset(ident[:], 0.0).then_inc(id_zero, 1)
                nc.gpsimd.memset(pick[:], 0.0).then_inc(id_zero, 1)
                nc.gpsimd.memset(xhT[:, :, 0:1], 0.0).then_inc(pads_ready, 1)
                nc.gpsimd.memset(xhT[:, :, SP1 - 1:SP1], 0.0).then_inc(pads_ready, 1)
                pool.wait_ge(id_zero, 2)
                nc.gpsimd.affine_select(out=ident[:], in_=ident[:], compare_op=ALU.not_equal, fill=1.0,
                                        base=0, pattern=[[-1, P]], channel_multiplier=1).then_inc(id_ready, 1)
                v = pick[:].rearrange("p s (h j) -> p s h j", h=2)
                for n, off in enumerate((0, 64, 96)):
                    if n:
                        pool.wait_ge(id_ready, n + 1)
                    nc.gpsimd.affine_select(out=v, in_=v, compare_op=ALU.not_equal, fill=1.0, base=-off,
                                            pattern=[[-1, NSP], [-NSP, 2], [0, 64]],
                                            channel_multiplier=1).then_inc(id_ready, 1)

            @block.scalar
            def _(act):
                for tile, name in small:
                    act.dma_start(tile[:], a[name]).then_inc(w_loaded, 16)
                act.dma_start(conv_rows[:], a["conv_w"].unsqueeze(0).broadcast_to([P, 3, DI])).then_inc(conv_loaded, 16)
                act.wait_ge(w_loaded, 16 * len(small))
                act.wait_ge(dve_done, 1)
                nc.scalar.activation(decay[:], decay[:], ACT.Exp).then_inc(exp_ready, 1)
                act.wait_ge(wp_ready, 1)
                nc.scalar.activation(w_delta[:], wp[:, :, 0:DI], ACT.Copy).then_inc(act_done, 1)
                act.wait_ge(eps_ready, 1)
                for i in range(4):
                    act.wait_ge(mv_ready, (i + 1) * QT)
                    nc.scalar.activation(lnv[:, i * QT:(i + 1) * QT], mv[:, i * QT:(i + 1) * QT, 1], ACT.Ln,
                                         bias=eps[:, 0:1]).then_inc(ln_ready, 1)
                    act.wait_ge(ln_ready, i + 1)
                    nc.scalar.activation(rstd[:, i * QT:(i + 1) * QT], lnv[:, i * QT:(i + 1) * QT], ACT.Exp,
                                         scale=-0.5).then_inc(rstd_ready, 1)
                for n in range(PAIRS):
                    act.wait_ge(tp_ready, n + 1)
                    nc.scalar.activation(xhT[:, 2 * n:2 * n + 2, 1:S + 1],
                                         tp[:, n % 4, :].rearrange("p (b t) -> p b t", b=2), ACT.Copy).then_inc(tp_free, 1)
                act.wait_ge(tp_free, PAIRS)
                act.wait_ge(act_done, 1)

            @block.vector
            def _(dve):
                nc.vector.memset(eps[:], EPS).then_inc(eps_ready, 1)
                dve.wait_ge(w_loaded, 16 * len(small))
                nc.vector.tensor_scalar(decay[:], decay[:], 60.0, None, ALU.min).then_inc(dve_done, 1)
                dve.wait_ge(exp_ready, 1)
                nc.vector.tensor_scalar(decay[:], decay[:], -1.0, None, ALU.mult).then_inc(dve_done, 1)
                dve.wait_ge(conv_loaded, 16)
                nc.vector.tensor_tensor(w_conv[:], conv_rows[:],
                                        w_u[:].unsqueeze(1).broadcast_to([P, 3, DI]), ALU.mult).then_inc(dve_done, 1)
                dve.wait_ge(id_ready, 1)
                for h in range(H2):
                    nc.vector.tensor_scalar(skip_diag[:, h, :], ident[:], dskip[:, h:h + 1], None, ALU.mult).then_inc(dve_done, 1)
                nc.vector.tensor_tensor(fold[:], ident[:, 0:64], ident[:, 64:P], ALU.add).then_inc(fold_done, 1)
                for i in range(4):
                    dve.wait_ge(x_in[i], 16)
                    for t in range(i * QT, (i + 1) * QT):
                        nc.vector.bn_stats(stats[:, t, :], X[:, t, :]).then_inc(stats_ready, 1)
                    for t in range(i * QT, (i + 1) * QT):
                        dve.wait_ge(stats_ready, t + 1)
                        nc.vector.bn_aggr(mv[:, t, :], stats[:, t, :]).then_inc(mv_ready, 1)
                dve.wait_ge(mv_ready, TILES)
                for n in range(PAIRS):
                    if n % 4 == 0:
                        dve.wait_ge(rstd_ready, n // 4 + 1)
                    if n >= 4:
                        dve.wait_ge(tp_ready, n - 3)
                    for c in range(CH):
                        t = CH * n + c
                        nc.vector.tensor_scalar(xh[:, n % 4, c, :], X[:, t, :], mv[:, t, 0:1], rstd[:, t:t + 1],
                                                ALU.subtract, ALU.mult).then_inc(xh_ready, 1)
                dve.wait_ge(dve_done, 3 + H2)
                dve.wait_ge(fold_done, 1)

            @block.tensor
            def _(pe):
                pe.wait_ge(w_loaded, 16 * len(small))
                for c in range(2):
                    for r in range(2):
                        last = nc.tensor.matmul(wp[:, c, 0:DI], w_xdT[:, r, c * P:(c + 1) * P], w_dt[:, r, :],
                                                start=(r == 0), stop=(r == 1))
                last.then_inc(wp_ready, 1)
                pe.wait_ge(id_ready, 1)
                for n in range(PAIRS):
                    pe.wait_ge(xh_ready, CH * (n + 1))
                    if n >= 4:
                        pe.wait_ge(tp_free, n - 3)
                    for c in range(CH):
                        last = nc.tensor.transpose(tp[:, n % 4, c * P:(c + 1) * P], xh[:, n % 4, c, :], ident[:])
                    last.then_inc(tp_ready, 1)

        uz = sb("uz", [P, 2, 4, N])
        dd = sb("dd", [P, 2, H2, N])
        relux, absx = dd[:, 0], dd[:, 1]
        onep = sb("onep", [P, H2, N])
        dup = sb("dup", [P, 2, 2, H2, 2, N])
        bcf = sb("bcf", [P, N])
        c3 = sb("c3", [P, 2, N], BF16)
        b_dup = sb("b_dup", [P, 2, NSP, N])
        states = sb("states", [P, RING, SPI, N])
        da = ctx.enter_context(nc.psum_tensor("da", [P, 2, SPI, N], F32))
        cb = ctx.enter_context(nc.psum_tensor("cb", [P, SPI, N], F32))
        yp = ctx.enter_context(nc.psum_tensor("yp", [P, N], F32))
        mp = ctx.enter_context(nc.psum_tensor("mp", [P, N], F32))

        da_zeroed = sem("da_zeroed")
        da_ready = sem("da_ready")
        dbu_ready = sem("dbu_ready")
        scan_done = sem("scan_done")
        hc_ready = sem("hc_ready")
        cb_ready = sem("cb_ready")
        sum_done = sem("sum_done")
        gate_done = sem("gate_done")
        mp_ready = sem("mp_ready")
        mp_free = sem("mp_free")
        silu_done = sem("silu_done")
        sp_exp = sem("sp_exp")
        sp_one = sem("sp_one")
        sp_ready = sem("sp_ready")
        sp_lost = sem("sp_lost")
        sp_fixed = sem("sp_fixed")
        delta_ready = sem("delta_ready")
        du_ready = [sem(f"du_ready{h}") for h in range(H2)]
        c_hi = sem("c_hi")
        c_rest = sem("c_rest")
        c_mid = sem("c_mid")
        c3_ready = sem("c3_ready")
        rows_out = [sem(f"rows_out{i}") for i in range(2)]
        b_in = [sem(f"b_in{i}") for i in range(2)]
        dup_in = [[sem(f"dup_in{i}{h}") for h in range(H2)] for i in range(2)]
        block = ctx.enter_context(nc.Block())

        DELTA0, DELTA1, OUT, BC, Z0, Z1, CONV0, CONV1 = range(8)
        BEFORE = (CONV0, CONV1, DELTA0, DELTA1, BC, Z0, Z1)
        before = BEFORE.index

        def place(n, stage):
            if is_at(n, 0):
                return 9 + stage - (stage > OUT)
            if is_at(n, PAIRS - 1):
                return 8 * n + 6
            return 8 * n + 8 + stage

        def over_pairs(eng, body):
            body(0, 0, 0, True, False)
            with eng.Fori(0, (PAIRS - 4) // 2) as j:
                body(2 * j + 1, 1, j, False, False)
                body(2 * j + 2, 0, j + 1, False, False)
            for n in range(PAIRS - 3, PAIRS):
                body(n, n % 2, n // 2, False, n == PAIRS - 1)

        def item(i):
            return i // 8, SPI * (i % 8 // 2), i % 2

        @block.tensor
        def _(pe):
            def project(stage, m, par, no):
                if not (isinstance(no, int) and no == 0):
                    pe.wait_ge(mp_free, no)
                u = uz[:, 1 - par, 2:4, :]
                if stage in (CONV0, CONV1):
                    h = stage - CONV0
                    for tap in range(3):
                        last = nc.tensor.matmul(mp[:].rearrange("p (b t) -> p b t", b=2),
                                                w_conv[:, tap, h * P:(h + 1) * P],
                                                xhT[:, bass.ds(2 * m, 2), tap:tap + S], start=(tap == 0), stop=(tap == 2))
                elif stage in (Z0, Z1):
                    h = stage - Z0
                    last = nc.tensor.matmul(mp[:].rearrange("p (b t) -> p b t", b=2),
                                            w_z[:, h * P:(h + 1) * P],
                                            xhT[:, bass.ds(2 * m, 2), 1:S + 1], start=True, stop=True)
                elif stage in (DELTA0, DELTA1):
                    h = stage - DELTA0
                    pe.wait_ge(silu_done, m + 1)
                    for c in range(2):
                        last = nc.tensor.matmul(mp[:], w_delta[:, c, h * P:(h + 1) * P], u[:, c, :],
                                                start=(c == 0), stop=(c == 1))
                elif stage == BC:
                    for c in range(2):
                        last = nc.tensor.matmul(mp[:], w_bc[:, c, :], u[:, c, :], start=(c == 0), stop=(c == 1))
                last.then_inc(mp_ready, 1)

            def output(m, par, no):
                pe.wait_ge(mp_free, no)
                pe.wait_ge(gate_done, 2 * m + 2)
                for c in range(CH):
                    for h in range(H2):
                        last = nc.tensor.matmul(mp[:, c * DM:(c + 1) * DM], uz[:, par, h, c * P:(c + 1) * P],
                                                w_out[:, h, :], start=(h == 0), stop=(h == 1))
                last.then_inc(mp_ready, 1)

            def sums(m, par, step):
                h, q = step // 4, step % 4
                if q == 0:
                    if not (isinstance(m, int) and m == 0 and h == 0):
                        pe.wait_ge(gate_done, 2 * m + h)
                    nc.tensor.matmul(yp[:], skip_diag[:, h, :], uz[:, 1 - par, 2 + h, :], start=True, stop=False,
                                     skip_group_check=True)
                for s in range(SPI):
                    for i in range(2):
                        last = nc.tensor.matmul(yp[64 * i:64 * i + 64, :], fold[:], states[:, (2 * step + i) % RING, s, :],
                                                start=False, stop=(q == 3 and s == SPI - 1), skip_group_check=True)
                last.then_inc(sum_done, 1)

            for stage in BEFORE:
                project(stage, 0, 0, before(stage))
            for no, stage in enumerate((CONV0, CONV1)):
                project(stage, 1, 1, len(BEFORE) + no)

            def body(n, par, uses, first, last):
                for s in range(STEPS):
                    if not (first and s == 0):
                        pe.wait_ge(hc_ready, ITEMS * n + 2 * s)
                    if s == 0:
                        pe.wait_ge(c3_ready, n + 1)
                    for i in range(SPI):
                        mm = nc.tensor.matmul(cb[:, i, :], pick[:, SPI * (s % 4) + i, :], c3[:, par, :],
                                              start=True, stop=True)
                    mm.then_inc(cb_ready, 1)
                    if s == 0 and not first:
                        sums(n - 1, 1 - par, STEPS - 1)
                    no = place(n, s)
                    if s == OUT:
                        if not first:
                            output(n - 1, 1 - par, no)
                    elif s in (CONV0, CONV1):
                        if not is_at(n, PAIRS - 2, PAIRS - 1):
                            project(s, n + 2, par, no)
                    elif not last:
                        project(s, n + 1, 1 - par, no)
                    if s:
                        sums(n, par, s - 1)

            over_pairs(pe, body)
            pe.wait_ge(hc_ready, ITEMS * PAIRS)
            sums(PAIRS - 1, (PAIRS - 1) % 2, STEPS - 1)
            output(PAIRS - 1, (PAIRS - 1) % 2, 8 * (PAIRS - 1) + 7)

        @block.scalar
        def _(act):
            def decays(n, par, uses, first, i):
                h, s0, g = item(i)
                if i in (0, 8):
                    act.wait_ge(dup_in[par][i // 8], 64 * uses + 64)
                if not (first and i < 2):
                    act.wait_ge(scan_done, ITEMS * n + i - 1)
                src = dup[:, par, 0, h, g, :].rearrange("p (b t) -> p b t", b=2)
                for s in range(SPI):
                    col = (2 * h + g) * NSP + s0 + s
                    last = nc.scalar.activation(
                        da[:, i % 2, s, :].rearrange("p (b t) -> p b t", b=2)[:, :, 1:S], src[:, :, 1:S],
                        ACT.Exp, scale=decay[:, col:col + 1])
                last.then_inc(da_ready, 1)

            def evacuate(stage, m, par, no):
                act.wait_ge(mp_ready, no + 1)
                if stage in (CONV0, CONV1):
                    h = stage - CONV0
                    last = nc.scalar.activation(uz[:, 1 - par, 2 + h, :], mp[:], ACT.Identity, bias=conv_b[:, h:h + 1])
                elif stage in (Z0, Z1):
                    last = nc.scalar.activation(uz[:, par, stage - Z0, :], mp[:], ACT.Copy)
                elif stage in (DELTA0, DELTA1):
                    h = stage - DELTA0
                    if stage == DELTA0 and not is_at(m, 0):
                        act.wait_ge(delta_ready, H2 * m)
                    nc.scalar.activation(absx[:, h, :], mp[:], ACT.Abs, bias=dt_b[:, h:h + 1])
                    last = nc.scalar.activation(relux[:, h, :], mp[:], ACT.Relu, bias=dt_b[:, h:h + 1])
                elif stage == OUT:
                    last = nc.scalar.activation(O[:, bass.ds(2 * m, 2)], mp[:].rearrange("p (b c d) -> p b c d", b=2, d=DM),
                                                ACT.Copy)
                last.then_inc(mp_free, 1)

            def softplus(m, no):
                act.wait_ge(mp_free, no + 1)
                nc.scalar.activation(absx, absx, ACT.Exp, scale=-1.0).then_inc(sp_exp, 1)
                act.wait_ge(sp_exp, m + 1)
                nc.scalar.activation(onep[:], absx, ACT.Identity, bias=1.0).then_inc(sp_one, 1)

            def log(m):
                act.wait_ge(sp_lost, m + 1)
                nc.scalar.activation(onep[:], onep[:], ACT.Ln).then_inc(sp_ready, 1)

            def parts(m, par, uses, no):
                act.wait_ge(mp_ready, no + 1)
                if not (isinstance(m, int) and m == 0):
                    act.wait_ge(c3_ready, m)
                    act.wait_ge(rows_out[1 - par], 16 * (uses + par))
                    if not (isinstance(m, int) and m == 1):
                        act.wait_ge(cb_ready, STEPS * (m - 1))
                nc.scalar.activation(bcf[:], mp[:], ACT.Copy)
                nc.scalar.activation(c3[:, par, :], mp[:], ACT.Copy).then_inc(c_hi, 1)
                act.wait_ge(c_hi, m + 1)
                act.sem_inc(mp_free, 1)

            def middle(m, par):
                act.wait_ge(c_rest, m + 1)
                nc.scalar.activation(c3[64:P, par, :], bcf[64:P, :], ACT.Copy).then_inc(c_mid, 1)

            evacuate(CONV0, 0, 0, before(CONV0))
            evacuate(CONV1, 0, 0, before(CONV1))
            act.wait_ge(mp_free, 2)
            nc.scalar.activation(uz[:, 1, 2:4, :], uz[:, 1, 2:4, :], ACT.Silu).then_inc(silu_done, 1)
            nc.scalar.preload_act_table_set(LOG_EXP)
            evacuate(DELTA0, 0, 0, before(DELTA0))
            evacuate(DELTA1, 0, 0, before(DELTA1))
            softplus(0, before(DELTA1))
            log(0)
            parts(0, 0, 0, before(BC))
            evacuate(Z0, 0, 0, before(Z0))
            middle(0, 0)
            evacuate(Z1, 0, 0, before(Z1))
            evacuate(CONV0, 1, 1, len(BEFORE))
            act.wait_ge(da_zeroed, 1)

            def body(n, par, uses, first, last):
                nxt = uses + par if not isinstance(n, int) else (n + 1) // 2
                if not first:
                    nc.scalar.preload_act_table_set(LOG_EXP)
                for s in range(STEPS):
                    decays(n, par, uses, first, 2 * s)
                    decays(n, par, uses, first, 2 * s + 1)
                    no = place(n, s - 1)
                    if s == 0:
                        if last:
                            act.wait_ge(mp_free, 8 * n + 6)
                            nc.scalar.activation(uz[:, par, 0:2, :], uz[:, par, 0:2, :], ACT.Silu).then_inc(silu_done, 1)
                        else:
                            evacuate(CONV1, n + 1, 1 - par, 8 if first else 8 * n + 7)
                            act.wait_ge(mp_free, 9 if first else 8 * n + 8)
                            nc.scalar.activation(uz[:, par, :, :], uz[:, par, :, :], ACT.Silu).then_inc(silu_done, 1)
                        nc.scalar.preload_act_table_set(LOG_EXP)
                    elif s == OUT + 1:
                        if not first:
                            evacuate(OUT, n - 1, 1 - par, no)
                    elif s == CONV0 + 1:
                        if not is_at(n, PAIRS - 2, PAIRS - 1):
                            evacuate(CONV0, n + 2, par, no)
                    elif last:
                        pass
                    elif s == BC + 1:
                        log(n + 1)
                        parts(n + 1, 1 - par, nxt, no)
                    else:
                        if s == DELTA0 + 1:
                            act.wait_ge(dup_in[par][1], 64 * uses + 64)
                        evacuate(s - 1, n + 1, 1 - par, no)
                        if s == DELTA1 + 1:
                            softplus(n + 1, no)
                        if s == Z0 + 1:
                            middle(n + 1, 1 - par)

            over_pairs(act, body)
            evacuate(OUT, PAIRS - 1, (PAIRS - 1) % 2, 8 * (PAIRS - 1) + 7)
            act.wait_ge(mp_free, 8 * (PAIRS - 1) + 8)

        @block.gpsimd
        def _(pool):
            def delta(m, par):
                pool.wait_ge(sp_ready, m + 1)
                pool.wait_ge(sp_fixed, m + 1)
                pool.wait_ge(silu_done, m + 1)
                for h in range(H2):
                    nc.gpsimd.tensor_tensor(dd[:, 0, h], dd[:, 0, h], onep[:, h], ALU.add).then_inc(delta_ready, 1)
                    pool.wait_ge(delta_ready, H2 * m + h + 1)
                    nc.gpsimd.tensor_tensor(dd[:, 1, h], dd[:, 0, h], uz[:, 1 - par, 2 + h, :], ALU.mult).then_inc(du_ready[h], 1)

            delta(0, 0)

            def body(n, par, uses, first, last):
                for i in range(ITEMS):
                    h, s0, g = item(i)
                    if i in (0, 8):
                        pool.wait_ge(dup_in[par][h], 64 * uses + 64)
                    if i == 0:
                        pool.wait_ge(b_in[par], 32 * uses + 32)
                    if i % 2 == 0 and not (first and i < RING):
                        pool.wait_ge(sum_done, STEPS * n + (i - RING) // 2 + 1)
                    nc.gpsimd.tensor_tensor(states[:, i % RING], b_dup[:, par, s0:s0 + SPI, :],
                                            dup[:, par, 1, h, g, :].unsqueeze(1).broadcast_to([P, SPI, N]),
                                            ALU.mult).then_inc(dbu_ready, 1)
                    if i == 11 and not last:
                        delta(n + 1, 1 - par)

            over_pairs(pool, body)

        @block.vector
        def _(dve):
            nc.vector.memset(da[:].rearrange("p k s (b t) -> p (k s b) t", b=2)[:, :, 0:1], 0.0).then_inc(da_zeroed, 1)
            dve.wait_ge(da_zeroed, 1)

            def softplus(m):
                dve.wait_ge(sp_one, m + 1)
                nc.vector.scalar_tensor_tensor(absx, onep[:], -1.0, absx, ALU.add, ALU.subtract).then_inc(sp_lost, 1)
                dve.wait_ge(sp_lost, m + 1)
                nc.vector.tensor_tensor(relux, relux, absx, ALU.subtract).then_inc(sp_fixed, 1)

            def split(m, par):
                dve.wait_ge(c_hi, m + 1)
                nc.vector.tensor_tensor(bcf[64:P, :], bcf[64:P, :], c3[64:P, par, :], ALU.subtract).then_inc(c_rest, 1)

            def low(m, par):
                dve.wait_ge(c_mid, m + 1)
                nc.vector.tensor_tensor(c3[96:P, par, :], bcf[96:P, :], c3[96:P, par, :], ALU.subtract).then_inc(c3_ready, 1)

            def times_c(n, i):
                dve.wait_ge(scan_done, ITEMS * n + i + 1)
                if i % 2 == 0:
                    dve.wait_ge(cb_ready, STEPS * n + i // 2 + 1)
                nc.vector.tensor_tensor(states[:, i % RING], states[:, i % RING], cb[:], ALU.mult).then_inc(hc_ready, 1)

            def gate(n, par, h):
                dve.wait_ge(sum_done, STEPS * n + 4 * h + 4)
                if h == 0:
                    dve.wait_ge(silu_done, n + 2)
                nc.vector.tensor_tensor(uz[:, par, h, :], yp[:], uz[:, par, h, :], ALU.mult).then_inc(gate_done, 1)

            softplus(0)
            split(0, 0)
            low(0, 0)

            def body(n, par, uses, first, last):
                for i in range(ITEMS):
                    dve.wait_ge(da_ready, ITEMS * n + i + 1)
                    dve.wait_ge(dbu_ready, ITEMS * n + i + 1)
                    nc.vector.tensor_tensor_scan(states[:, i % RING].rearrange("p s t -> p (s t)"),
                                                 da[:, i % 2].rearrange("p s t -> p (s t)"),
                                                 states[:, i % RING].rearrange("p s t -> p (s t)"),
                                                 0.0, ALU.mult, ALU.add).then_inc(scan_done, 1)
                    if i:
                        times_c(n, i - 1)
                    elif not first:
                        times_c(n - 1, ITEMS - 1)
                    if i == 2 and not first:
                        gate(n - 1, 1 - par, 1)
                    if i == 10:
                        gate(n, par, 0)
                    if i == 6 and not last:
                        softplus(n + 1)
                    if i == 10 and not last:
                        split(n + 1, 1 - par)
                    if i == 12 and not last:
                        low(n + 1, 1 - par)

            over_pairs(dve, body)
            times_c(PAIRS - 1, ITEMS - 1)
            gate(PAIRS - 1, (PAIRS - 1) % 2, 1)
            dve.wait_ge(gate_done, 2 * PAIRS)

        @block.sync
        def _(sp):
            def spread(m, par, uses):
                sp.wait_ge(c_hi, m + 1)
                if not (isinstance(m, int) and m < 2):
                    sp.wait_ge(b_in[par], 32 * uses)
                    sp.wait_ge(dbu_ready, ITEMS * (m - 1))
                    sp.wait_ge(da_ready, ITEMS * (m - 1))
                sp.dma_start(b_rows[par], bcf[16:32, :]).then_inc(rows_out[par], 16)
                sp.wait_ge(rows_out[par], 16 * uses + 16)
                for sh in range(2):
                    sp.dma_start(b_dup[64 * sh:64 * sh + 64, par],
                                 b_rows[par, NSP * sh:NSP * sh + NSP, :].unsqueeze(0).broadcast_to([64, NSP, N])
                                 ).then_inc(b_in[par], 16)
                for h in range(H2):
                    sp.wait_ge(du_ready[h], m + 1)
                    for g in range(2):
                        for sh in range(2):
                            sp.dma_start(dup[64 * sh:64 * sh + 64, par, :, h, g, :],
                                         dd[64 * g:64 * g + 64, :, h]).then_inc(dup_in[par][h], 16)

            spread(0, 0, 0)
            spread(1, 1, 0)
            with sp.Fori(0, (PAIRS - 2) // 2) as j:
                spread(2 * j + 2, 0, j + 1)
                spread(2 * j + 3, 1, j + 1)
            for i in range(2):
                sp.wait_ge(rows_out[i], 16 * PAIRS // 2)
                sp.wait_ge(b_in[i], 32 * PAIRS // 2)


def experts(nc, a, X, O, xhT, ident, eps, out_v, k):
    B, S, DM, TILES = (k[n] for n in ("B", "S", "DM", "TILES"))
    E, F = a["wgT"].shape[1:]
    CAP = int(S * 2.0 / E)
    FH = F // P
    PAIRS, N, CH = B // 2, 2 * S, 2 * S // P
    GB = P // E
    GROUPS = B // GB
    SLOTS = E * CAP
    EG = SLOTS // P
    Y = O

    with ExitStack() as ctx:
        def sb(name, shape, dt=F32, c=ctx):
            return c.enter_context(nc.sbuf_tensor(name, shape, dt))

        def ps(name, shape, c):
            return c.enter_context(nc.psum_tensor(name, shape, F32))

        def sems(c, *names):
            return [c.enter_context(nc.semaphore(n)) for n in names]

        mvf = sb("mvf", [P, TILES, 2])
        rstdf = sb("rstdf", [P, TILES])
        gate_wT = sb("gate_wT", [P, E])
        wsgT = sb("wsgT", [P, F])
        wsuT = sb("wsuT", [P, F])
        wsdT = sb("wsdT", [P, FH, DM])
        L = sb("L", [P, TILES, E])
        mask_e = sb("mask_e", [P, E])
        mask_b = sb("mask_b", [P, GB])
        pick_b = sb("pick_b", [P, GB, P], BF16)
        row_t = sb("row_t", [P, S])
        col_t = sb("col_t", [P, 2])
        idx_x = sb("idx_x", [P, GROUPS, SLOTS], BF16)
        slot_i = sb("slot_i", [P, EG, GROUPS, GB])
        slot_w = sb("slot_w", [P, EG, GROUPS, GB])

        def normed(dve, dst, t):
            return nc.vector.tensor_scalar(dst, X[:, bass.ds(t, 1), :], mvf[:, bass.ds(t, 1), 0], rstdf[:, bass.ds(t, 1)],
                                           ALU.subtract, ALU.mult)

        with ExitStack() as c:
            G4 = 4
            GP, GT = PAIRS // G4, TILES // G4
            st = sb("st", [P, TILES, 6], c=c)
            mvo = sb("mvo", [P, TILES, 2], c=c)
            part = sb("part", [P, 2, TILES], c=c)
            lno = sb("lno", [P, 2, TILES], c=c)
            rstdo = sb("rstdo", [P, TILES], c=c)
            i_t = sb("i_t", [P, S], mybir.dt.int32, c=c)
            i_p = sb("i_p", [P, 2], mybir.dt.int32, c=c)
            xf = sb("xf", [P, 2, CH, DM], c=c)
            hT = sb("hT", [P, 2, N], c=c)
            gl = sb("gl", [P, FH, N], c=c)
            hs = sb("hs", [P, FH, N], c=c)
            tp, lp, yp = ps("tp3", [P, N], c), ps("lp3", [P, N], c), ps("yp3", [P, N], c)
            gp, up = ps("gp", [P, FH, N], c), ps("up", [P, FH, N], c)
            wf_loaded, ones_set, masks_ready, iota_ready, copied = sems(
                c, "wf_loaded", "ones_set", "masks_ready", "iota_ready", "copied")
            so_ready, mo_ready, lo_ready, ro_ready, on_ready = sems(c, "so_ready", "mo_ready", "lo_ready", "ro_ready", "on_ready")
            sx_ready, mx_ready, lx_ready, rx_ready, x_ready = sems(c, "sx_ready", "mx_ready", "lx_ready", "rx_ready", "x_ready")
            comb_ready, xf_ready, tp_ready, hT_ready, lp_ready, lp_free = sems(
                c, "comb_ready", "xf_ready", "tp3_ready", "hT_ready", "lp_ready", "lp_free")
            gp_ready, gl_ready, up_ready, hs_ready, yp_ready, yp_free = sems(
                c, "gp_ready", "gl_ready", "up_ready", "hs_ready", "yp_ready", "yp_free")
            block = c.enter_context(nc.Block())

            def groups(eng, body):
                body(0, False)
                with eng.Fori(0, G4 - 2) as j:
                    body(j + 1, False)
                body(G4 - 1, True)

            @block.sync
            def _(sp):
                for tile, name in ((gate_wT, "gate_wT"), (wsgT, "wsgT"), (wsuT, "wsuT"), (wsdT, "wsdT")):
                    sp.dma_start(tile[:], a[name]).then_inc(wf_loaded, 16)

            @block.gpsimd
            def _(pool):
                nc.gpsimd.memset(mask_e[:], 0.0).then_inc(ones_set, 1)
                nc.gpsimd.memset(mask_b[:], 1.0).then_inc(ones_set, 1)
                nc.gpsimd.iota(i_t[:], pattern=[[1, S]], base=0, channel_multiplier=0).then_inc(iota_ready, 1)
                nc.gpsimd.iota(i_p[:], pattern=[[P, 2]], base=0, channel_multiplier=1).then_inc(iota_ready, 1)
                pool.wait_ge(ones_set, 2)
                nc.gpsimd.affine_select(out=mask_b[:], in_=mask_b[:], compare_op=ALU.is_ge, fill=0.0, base=0,
                                        pattern=[[-E, GB]], channel_multiplier=1).then_inc(masks_ready, 1)
                pool.wait_ge(masks_ready, 1)
                nc.gpsimd.affine_select(out=mask_b[:], in_=mask_b[:], compare_op=ALU.is_ge, fill=0.0, base=E - 1,
                                        pattern=[[E, GB]], channel_multiplier=-1).then_inc(masks_ready, 1)
                for n in range(GB):
                    if n:
                        pool.wait_ge(masks_ready, n + 2)
                    nc.gpsimd.affine_select(out=mask_e[:], in_=mask_e[:], compare_op=ALU.not_equal, fill=1.0,
                                            base=-E * n, pattern=[[-1, E]], channel_multiplier=1).then_inc(masks_ready, 1)
                with pool.Fori(0, G4) as g:
                    pool.wait_ge(on_ready, GT * g + GT)
                    gx = X[:, bass.ds(g * GT, GT), :].rearrange("p (b c) d -> p b c d", c=2)
                    nc.gpsimd.tensor_tensor(gx, gx, O[:, bass.ds(g * (GT // 2), GT // 2)], ALU.add).then_inc(x_ready, 1)

            @block.scalar
            def _(act):
                def inverse(g, mvt, r, l, ready, l_ready, r_ready):
                    act.wait_ge(ready, 2 * g + 2)
                    nc.scalar.activation(lno[:, l, bass.ds(g * GT, GT)], mvt[:, bass.ds(g * GT, GT), 1], ACT.Ln,
                                         scale=1.0 / P, bias=eps[:, 0:1]).then_inc(l_ready, 1)
                    act.wait_ge(l_ready, g + 1)
                    nc.scalar.activation(r[:, bass.ds(g * GT, GT)], lno[:, l, bass.ds(g * GT, GT)], ACT.Exp,
                                         scale=-0.5).then_inc(r_ready, 1)

                def inverse_o(g):
                    inverse(g, mvo, rstdo, 0, mo_ready, lo_ready, ro_ready)

                def inverse_x(g):
                    inverse(g, mvf, rstdf, 1, mx_ready, lx_ready, rx_ready)

                def turned(n, par):
                    act.wait_ge(tp_ready, n + 1)
                    if not is_at(n, 0, 1):
                        act.wait_ge(up_ready, FH * (n - 1))
                    nc.scalar.activation(hT[:, par, :], tp[:], ACT.Copy).then_inc(hT_ready, 1)

                def body(g, last):
                    for i in range(GP):
                        n, par = GP * g + i, i % 2
                        for h in range(FH):
                            act.wait_ge(gp_ready, FH * n + h + 1)
                            if not is_at(n, 0):
                                act.wait_ge(hs_ready, FH * (n - 1) + h + 1)
                            nc.scalar.activation(gl[:, h], gp[:, h], ACT.Gelu).then_inc(gl_ready, 1)
                        if i == 1 and not last:
                            inverse_o(g + 1)
                        if i == 3 and not last:
                            inverse_x(g + 1)
                        if i < 3:
                            turned(n + 1, 1 - par)
                        act.wait_ge(yp_ready, n + 1)
                        nc.scalar.activation(Y[:, bass.ds(2 * n, 2)], yp[:].rearrange("p (b c d) -> p b c d", b=2, d=DM),
                                             ACT.Copy).then_inc(yp_free, 1)
                        if i == 3 and not last:
                            turned(n + 1, 1 - par)

                inverse_o(0)
                inverse_x(0)
                turned(0, 0)
                groups(act, body)
                act.wait_ge(yp_free, PAIRS)

            @block.vector
            def _(dve):
                def statistics(g, which, source, s_ready, mvt, m_ready):
                    for t in range(GT * g, GT * g + GT):
                        nc.vector.bn_stats(st[:, t, :], source(t)).then_inc(s_ready, 1)
                    dve.wait_ge(s_ready, GT * g + GT)
                    gs = bass.ds(g * GT, GT)
                    s_ap, d_ap = part[:, 0, gs], part[:, 1, gs]
                    nc.vector.tensor_tensor(s_ap, st[:, gs, 1], st[:, gs, 4], ALU.add).then_inc(comb_ready, 1)
                    nc.vector.tensor_tensor(d_ap, st[:, gs, 1], st[:, gs, 4], ALU.subtract).then_inc(comb_ready, 1)
                    nc.vector.tensor_tensor(mvt[:, gs, 1], st[:, gs, 2], st[:, gs, 5], ALU.add).then_inc(comb_ready, 1)
                    dve.wait_ge(comb_ready, 8 * g + 4 * which + 3)
                    nc.vector.tensor_scalar(mvt[:, gs, 0], s_ap, 0.5, None, ALU.mult).then_inc(m_ready, 1)
                    nc.vector.scalar_tensor_tensor(d_ap, d_ap, P / 4, d_ap, ALU.mult, ALU.mult).then_inc(comb_ready, 1)
                    dve.wait_ge(comb_ready, 8 * g + 4 * which + 4)
                    nc.vector.tensor_tensor(mvt[:, gs, 1], mvt[:, gs, 1], d_ap, ALU.add).then_inc(m_ready, 1)

                def statistics_o(g):
                    statistics(g, 0, lambda t: O[:, t // 2, t % 2, :], so_ready, mvo, mo_ready)

                def statistics_x(g):
                    dve.wait_ge(x_ready, g + 1)
                    statistics(g, 1, lambda t: X[:, t, :], sx_ready, mvf, mx_ready)

                def norm_o(g):
                    dve.wait_ge(ro_ready, g + 1)
                    for t in range(GT * g, GT * g + GT):
                        o = O[:, t // 2, t % 2, :]
                        nc.vector.tensor_scalar(o, o, mvo[:, t, 0:1], rstdo[:, t:t + 1], ALU.subtract, ALU.mult
                                                ).then_inc(on_ready, 1)

                def norm(n, par):
                    if not is_at(n, 0, 1):
                        dve.wait_ge(tp_ready, n - 1)
                    for i in range(CH):
                        ins = normed(dve, xf[:, par, i, :], CH * n + i)
                    ins.then_inc(xf_ready, 1)

                def body(g, last):
                    for i in range(GP):
                        n, par = GP * g + i, i % 2
                        dve.wait_ge(lp_ready, n + 1)
                        nc.vector.tensor_copy(L[:, bass.ds(CH * n, CH), :], lp[:, 0:CH * E].rearrange("p (c e) -> p c e", e=E)
                                              ).then_inc(lp_free, 1)
                        if not is_at(n, 0):
                            dve.wait_ge(yp_ready, n)
                        for h in range(FH):
                            dve.wait_ge(up_ready, FH * n + h + 1)
                            dve.wait_ge(gl_ready, FH * n + h + 1)
                            nc.vector.tensor_tensor(hs[:, h], gl[:, h], up[:, h], ALU.mult).then_inc(hs_ready, 1)
                        if i < 2:
                            norm(n + 2, par)
                        if last:
                            continue
                        if i == 0:
                            statistics_o(g + 1)
                        elif i == 1:
                            norm_o(g + 1)
                        elif i == 2:
                            statistics_x(g + 1)
                        else:
                            dve.wait_ge(rx_ready, g + 2)
                            norm(n + 1, 1 - par)
                            norm(n + 2, par)

                statistics_o(0)
                dve.wait_ge(iota_ready, 2)
                nc.vector.tensor_copy(row_t[:], i_t[:]).then_inc(copied, 1)
                nc.vector.tensor_copy(col_t[:], i_p[:]).then_inc(copied, 1)
                norm_o(0)
                dve.wait_ge(masks_ready, 2 + GB)
                nc.vector.tensor_copy(pick_b[:], mask_b[:].unsqueeze(2).broadcast_to([P, GB, P])).then_inc(copied, 1)
                statistics_x(0)
                dve.wait_ge(rx_ready, 1)
                norm(0, 0)
                norm(1, 1)
                for g in range(G4):
                    body(g, g == G4 - 1)
                dve.wait_ge(hs_ready, FH * PAIRS)
                dve.wait_ge(copied, 3)

            @block.tensor
            def _(pe):
                def turn(n, par):
                    pe.wait_ge(xf_ready, n + 1)
                    if not is_at(n, 0):
                        pe.wait_ge(hT_ready, n)
                    for i in range(CH):
                        mm = nc.tensor.transpose(tp[:, i * P:(i + 1) * P], xf[:, par, i, :], ident[:])
                    mm.then_inc(tp_ready, 1)

                def body(g, last):
                    for k in range(GP):
                        n, par = GP * g + k, k % 2
                        pe.wait_ge(hT_ready, n + 1)
                        if not is_at(n, 0):
                            pe.wait_ge(lp_free, n)
                        for i in range(CH):
                            mm = nc.tensor.matmul(lp[:, i * E:(i + 1) * E], hT[:, par, i * P:(i + 1) * P], gate_wT[:],
                                                  start=True, stop=True)
                        mm.then_inc(lp_ready, 1)
                        for h in range(FH):
                            if not is_at(n, 0):
                                pe.wait_ge(gl_ready, FH * (n - 1) + h + 1)
                                pe.wait_ge(hs_ready, FH * (n - 1) + h + 1)
                            nc.tensor.matmul(gp[:, h], wsgT[:, h * P:(h + 1) * P], hT[:, par, :], start=True, stop=True
                                             ).then_inc(gp_ready, 1)
                            nc.tensor.matmul(up[:, h], wsuT[:, h * P:(h + 1) * P], hT[:, par, :], start=True, stop=True
                                             ).then_inc(up_ready, 1)
                        if k < 3:
                            turn(n + 1, 1 - par)
                        pe.wait_ge(hs_ready, FH * n + FH)
                        if not is_at(n, 0):
                            pe.wait_ge(yp_free, n)
                        for i in range(CH):
                            for h in range(FH):
                                mm = nc.tensor.matmul(yp[:, i * DM:(i + 1) * DM], hs[:, h, i * P:(i + 1) * P], wsdT[:, h, :],
                                                      start=(h == 0), stop=(h == FH - 1))
                        mm.then_inc(yp_ready, 1)
                        if k == 3 and not last:
                            turn(n + 1, 1 - par)

                pe.wait_ge(wf_loaded, 64)
                turn(0, 0)
                groups(pe, body)

        with ExitStack() as c:
            top = sb("top", [P, TILES], c=c)
            den = sb("den", [P, TILES], c=c)
            scores = sb("scores", [P, 2, B, E], c=c)
            rest = sb("rest", [P, GROUPS, 2, S], c=c)
            best = sb("best", [P, GROUPS, CAP], c=c)
            best_i = sb("best_i", [P, GROUPS, CAP], mybir.dt.uint32, c=c)
            best_f = sb("best_f", [P, GROUPS, CAP], c=c)
            w_x = sb("w_x", [P, GROUPS, SLOTS], c=c)
            i_x = sb("i_x", [P, GROUPS, SLOTS], c=c)
            sp_t = [ps(f"sp_t{g}", [P, 2 * P], c) for g in range(GROUPS)]
            sl = ps("sl", [P, GROUPS, 2, EG, GB], c)
            soft, exp_done, sc_ready, turned_s, found, taken, spread, expanded, sl_ready, sl_out = sems(
                c, "soft", "exp_done", "sc_ready", "turned_s", "found", "taken", "spread", "expanded", "sl_ready", "sl_out")
            block = c.enter_context(nc.Block())

            @block.scalar
            def _(act):
                act.wait_ge(soft, 2)
                nc.scalar.activation(L[:], L[:], ACT.Exp).then_inc(exp_done, 1)

            @block.vector
            def _(dve):
                wide = [P, TILES, E]
                nc.vector.tensor_reduce(top[:], L[:], AX.X, ALU.max).then_inc(soft, 1)
                dve.wait_ge(soft, 1)
                nc.vector.tensor_tensor(L[:], L[:], top[:].unsqueeze(2).broadcast_to(wide), ALU.subtract).then_inc(soft, 1)
                dve.wait_ge(exp_done, 1)
                nc.vector.tensor_reduce(den[:], L[:], AX.X, ALU.add).then_inc(soft, 1)
                dve.wait_ge(soft, 3)
                nc.vector.reciprocal(den[:], den[:]).then_inc(soft, 1)
                dve.wait_ge(soft, 4)
                lv = L[:].rearrange("p (b c) e -> p c b e", c=2)
                dv = den[:].rearrange("p (b c) -> p c b", c=2)
                for h in range(2):
                    nc.vector.tensor_tensor(scores[:, h], lv[:, h], dv[:, h].unsqueeze(2).broadcast_to([P, B, E]),
                                            ALU.mult).then_inc(sc_ready, 1)
                nf = nt = 0
                for r in range(CAP // 8):
                    for g in range(GROUPS):
                        src = sp_t[g][:] if r == 0 else rest[:, g, (r - 1) % 2, :]
                        if r == 0:
                            dve.wait_ge(turned_s, g + 1)
                        else:
                            dve.wait_ge(taken, GROUPS * (r - 1) + g + 1)
                        b8 = best[:, g, 8 * r:8 * r + 8]
                        nc.vector.max(b8, src).then_inc(found, 1)
                        nf += 1
                        dve.wait_ge(found, nf)
                        nc.vector.max_index(best_i[:, g, 8 * r:8 * r + 8], b8, src).then_inc(spread, 1)
                        if r < CAP // 8 - 1:
                            nc.vector.match_replace(rest[:, g, r % 2, :], b8, src, -1.0).then_inc(taken, 1)
                n = CAP // 8 * GROUPS
                dve.wait_ge(spread, n)
                nc.vector.tensor_copy(best_f[:], best_i[:]).then_inc(spread, 1)
                dve.wait_ge(spread, n + 1)
                me = mask_e[:].unsqueeze(2).broadcast_to([P, E, CAP])
                for g in range(GROUPS):
                    nc.vector.tensor_tensor(i_x[:, g].rearrange("p (e c) -> p e c", e=E), me,
                                            best_f[:, g].unsqueeze(1).broadcast_to([P, E, CAP]), ALU.mult).then_inc(expanded, 1)
                    nc.vector.tensor_tensor(w_x[:, g].rearrange("p (e c) -> p e c", e=E), me,
                                            best[:, g].unsqueeze(1).broadcast_to([P, E, CAP]), ALU.mult).then_inc(expanded, 1)
                dve.wait_ge(expanded, 2 * GROUPS)
                nc.vector.tensor_copy(idx_x[:], i_x[:]).then_inc(sl_out, 1)
                dve.wait_ge(sl_ready, 1)
                nc.vector.tensor_copy(slot_i[:], sl[:, :, 0].rearrange("p g e b -> p e g b")).then_inc(sl_out, 1)
                nc.vector.tensor_copy(slot_w[:], sl[:, :, 1].rearrange("p g e b -> p e g b")).then_inc(sl_out, 1)
                dve.wait_ge(sl_out, 3)

            @block.tensor
            def _(pe):
                pe.wait_ge(sc_ready, 2)
                for g in range(GROUPS):
                    for h in range(2):
                        mm = nc.tensor.transpose(sp_t[g][:, h * P:(h + 1) * P],
                                                 scores[:, h, g * GB:(g + 1) * GB, :].rearrange("p b e -> p (b e)"), ident[:])
                    mm.then_inc(turned_s, 1)
                pe.wait_ge(expanded, 2 * GROUPS)
                for g in range(GROUPS):
                    for w, x in enumerate((i_x, w_x)):
                        for e in range(EG):
                            mm = nc.tensor.matmul(sl[:, g, w, e, :], x[:, g, e * P:(e + 1) * P], mask_b[:], start=True, stop=True)
                mm.then_inc(sl_ready, 1)

        XG = sb("XG", [P, E, B, CAP])
        gather(nc, XG, normed, idx_x, pick_b, col_t, k)
        run_experts(nc, a, XG, DM)
        scatter(nc, X, Y, XG, row_t, slot_i, slot_w, ident, eps, out_v, k)


def by_two(eng, count, body, tail=1):
    body(0, 0)
    with eng.Fori(0, (count - tail) // 2) as j:
        body(2 * j + 1, 1)
        body(2 * j + 2, 0)
    for n in range(count - tail, count):
        body(n, n % 2)


def is_at(n, *values):
    return isinstance(n, int) and n in values


def gather(nc, XG, normed, idx_x, pick_b, col_t, k):
    S = k["S"]
    E, B, CAP = XG.shape[1:]
    SLOTS, GB, DM = E * CAP, pick_b.shape[1], k["DM"]
    with ExitStack() as c:
        xt = c.enter_context(nc.sbuf_tensor("xt", [P, 2, 2, DM], F32))
        hot = c.enter_context(nc.sbuf_tensor("hot", [P, 2, 2, SLOTS], F32))
        ip = c.enter_context(nc.psum_tensor("ip", [P, 2, SLOTS], F32))
        xp = c.enter_context(nc.psum_tensor("xp", [P, 2, SLOTS], F32))
        xt_ready, ip_ready, hot_ready, xp_ready, xp_free = [
            c.enter_context(nc.semaphore(n)) for n in ("xt_ready", "ip_ready", "hot_ready", "xp_ready", "xp_free")]
        block = c.enter_context(nc.Block())

        @block.tensor
        def _(pe):
            def indices(n, par, g, b):
                if not is_at(n, 0, 1):
                    pe.wait_ge(hot_ready, n - 1)
                nc.tensor.matmul(ip[:, par], pick_b[:, bass.ds(b, 1), :], idx_x[:, g, :], start=True, stop=True
                                 ).then_inc(ip_ready, 1)

            def take(n, par):
                pe.wait_ge(xt_ready, n + 1)
                pe.wait_ge(hot_ready, n + 1)
                if not is_at(n, 0, 1):
                    pe.wait_ge(xp_free, n - 1)
                for h in range(2):
                    mm = nc.tensor.matmul(xp[:, par], xt[:, par, h, :], hot[:, par, h, :], start=(h == 0), stop=(h == 1))
                mm.then_inc(xp_ready, 1)

            indices(0, 0, 0, 0)
            for g in range(B // GB):
                n = GB * g
                indices(n + 1, 1, g, 1)
                take(n, 0)
                with pe.Fori(0, GB // 2 - 1) as j:
                    for i in range(2):
                        indices(n + 2 * j + i + 2, i, g, 2 * j + i + 2)
                        take(n + 2 * j + i + 1, 1 - i)
                if g < B // GB - 1:
                    indices(n + GB, 0, g + 1, 0)
                take(n + GB - 1, 1)

        @block.vector
        def _(dve):
            def body(n, par):
                if not is_at(n, 0, 1):
                    dve.wait_ge(xp_ready, n - 1)
                for h in range(2):
                    ins = normed(dve, xt[:, par, h, :], 2 * n + h)
                ins.then_inc(xt_ready, 1)
                dve.wait_ge(ip_ready, n + 1)
                for h in range(2):
                    ins = nc.vector.tensor_scalar(hot[:, par, h, :], ip[:, par], col_t[:, h:h + 1], None, ALU.is_equal)
                ins.then_inc(hot_ready, 1)

            by_two(dve, B, body)

        @block.scalar
        def _(act):
            def body(n, par):
                act.wait_ge(xp_ready, n + 1)
                nc.scalar.activation(XG[:, :, bass.ds(n, 1), :], xp[:, par].rearrange("p (e c) -> p e c", e=E), ACT.Copy
                                     ).then_inc(xp_free, 1)

            by_two(act, B, body)
            act.wait_ge(xp_free, B)


def run_experts(nc, a, XG, DM):
    E, B, CAP = XG.shape[1:]
    F = a["wgT"].shape[2]
    FH = F // P
    CB = B // 2
    M = CB * CAP
    WB = 2
    with ExitStack() as c:
        def sb(name, shape):
            return c.enter_context(nc.sbuf_tensor(name, shape, F32))

        wg, wu, wd = sb("wg", [P, WB, F]), sb("wu", [P, WB, F]), sb("wd", [P, WB, FH, DM])
        gl, hx = sb("glx", [P, FH, M]), sb("hx", [P, 2, FH, M])
        gp = c.enter_context(nc.psum_tensor("gpx", [P, FH, M], F32))
        up = c.enter_context(nc.psum_tensor("upx", [P, FH, M], F32))
        dp = c.enter_context(nc.psum_tensor("dpx", [P, 2, M], F32))
        w_in = [c.enter_context(nc.semaphore(f"we{i}")) for i in range(WB)]
        gp_ready, up_ready, gl_ready, hx_ready, dp_ready, dp_free = [
            c.enter_context(nc.semaphore(n)) for n in ("gpx_ready", "upx_ready", "glx_ready", "hx_ready", "dpx_ready", "dpx_free")]
        block = c.enter_context(nc.Block())

        @block.sync
        def _(sp):
            def body(n, par):
                if not is_at(n, 0, 1):
                    sp.wait_ge(dp_ready, 2 * n - 2)
                sp.dma_start(wg[:, par], a["wgT"][:, bass.ds(n, 1), :]).then_inc(w_in[par], 16)
                sp.dma_start(wu[:, par], a["wuT"][:, bass.ds(n, 1), :]).then_inc(w_in[par], 16)
                sp.dma_start(wd[:, par], a["wdT"][:, bass.ds(n, 1)]).then_inc(w_in[par], 16)

            by_two(sp, E, body)

        @block.tensor
        def _(pe):
            def up_gate(n, par, chunk):
                k = 2 * n + chunk
                for h in range(FH):
                    if not is_at(k, 0):
                        pe.wait_ge(hx_ready, FH * (k - 1) + h + 1)
                    x = XG[:, bass.ds(n, 1), CB * chunk:CB * chunk + CB]
                    nc.tensor.matmul(gp[:, h], wg[:, par, h * P:(h + 1) * P], x, start=True, stop=True).then_inc(gp_ready, 1)
                    nc.tensor.matmul(up[:, h], wu[:, par, h * P:(h + 1) * P], x, start=True, stop=True).then_inc(up_ready, 1)

            def down(n, par, chunk):
                k = 2 * n + chunk
                pe.wait_ge(hx_ready, FH * k + FH)
                if not is_at(k, 0, 1):
                    pe.wait_ge(dp_free, k - 1)
                for h in range(FH):
                    mm = nc.tensor.matmul(dp[:, chunk], wd[:, par, h, :], hx[:, chunk, h], start=(h == 0), stop=(h == FH - 1))
                mm.then_inc(dp_ready, 1)

            def expert(n, par, uses, last=False):
                up_gate(n, par, 1)
                down(n, par, 0)
                if not last:
                    pe.wait_ge(w_in[1 - par], 48 * uses + 48)
                    up_gate(n + 1, 1 - par, 0)
                down(n, par, 1)

            pe.wait_ge(w_in[0], 48)
            up_gate(0, 0, 0)
            expert(0, 0, 0)
            with pe.Fori(0, E // 2 - 1) as j:
                expert(2 * j + 1, 1, j + 1)
                expert(2 * j + 2, 0, j + 1)
            expert(E - 1, 1, 0, last=True)

        @block.scalar
        def _(act):
            def gelus(k):
                for h in range(FH):
                    act.wait_ge(gp_ready, FH * k + h + 1)
                    if not is_at(k, 0):
                        act.wait_ge(hx_ready, FH * (k - 1) + h + 1)
                    nc.scalar.activation(gl[:, h], gp[:, h], ACT.Gelu).then_inc(gl_ready, 1)

            def evacuate(n, chunk):
                act.wait_ge(dp_ready, 2 * n + chunk + 1)
                nc.scalar.activation(XG[:, bass.ds(n, 1), CB * chunk:CB * chunk + CB],
                                     dp[:, chunk].rearrange("p (b c) -> p b c", b=CB), ACT.Copy).then_inc(dp_free, 1)

            def body(n, par):
                gelus(2 * n + 1)
                evacuate(n, 0)
                if not is_at(n, E - 1):
                    gelus(2 * n + 2)
                evacuate(n, 1)

            gelus(0)
            by_two(act, E, body)
            act.wait_ge(dp_free, 2 * E)

        @block.vector
        def _(dve):
            def body(k, par):
                for h in range(FH):
                    dve.wait_ge(gl_ready, FH * k + h + 1)
                    dve.wait_ge(up_ready, FH * k + h + 1)
                    if not is_at(k, 0, 1):
                        dve.wait_ge(dp_ready, k - 1)
                    nc.vector.tensor_tensor(hx[:, par, h], gl[:, h], up[:, h], ALU.mult).then_inc(hx_ready, 1)

            by_two(dve, 2 * E, body)
            dve.wait_ge(hx_ready, FH * 2 * E)


def scatter(nc, X, Y, XG, row_t, slot_i, slot_w, ident, eps, out_v, k):
    S, DM, TILES = k["S"], k["DM"], k["TILES"]
    E, B, CAP = XG.shape[1:]
    SLOTS = E * CAP
    EG = slot_i.shape[1]
    G4, GB = 4, B // 4
    PB = 3 * GB // 8
    slot_ib, slot_wb = (v[:].rearrange("p e g b -> p e (g b)") for v in (slot_i, slot_w))
    with ExitStack() as c:
        def sb(name, shape):
            return c.enter_context(nc.sbuf_tensor(name, shape, F32))

        eT = sb("eT", [P, 2, SLOTS])
        eo = sb("eo", [P, 2, EG, DM])
        put = sb("put", [P, 2, EG, S])
        st, part = sb("st5", [P, TILES, 6]), sb("part5", [P, 3, TILES])
        mean, lnv, rstd = sb("mean5", [P, TILES]), sb("lnv5", [P, TILES]), sb("rstd5", [P, TILES])
        tp = c.enter_context(nc.psum_tensor("tps", [P, 2, SLOTS], F32))
        yp = c.enter_context(nc.psum_tensor("yss", [P, 2, 512], F32))
        (eT_ready, tp_ready, eo_ready, put_ready, yp_ready, y_ready, st_ready, sq_ready, var_ready, ln_ready, r_ready,
         n_ready, x_dve, x_pool, stored) = [c.enter_context(nc.semaphore(f"{n}5")) for n in (
             "eT_ready", "tp_ready", "eo_ready", "put_ready", "yp_ready", "y_ready", "st_ready", "sq_ready", "var_ready",
             "ln_ready", "r_ready", "n_ready", "x_dve", "x_pool", "stored")]
        block = c.enter_context(nc.Block())

        @block.tensor
        def _(pe):
            def turn(n, par):
                pe.wait_ge(eT_ready, n + 1)
                if not is_at(n, 0, 1):
                    pe.wait_ge(eo_ready, n - 1)
                for g in range(EG):
                    mm = nc.tensor.transpose(tp[:, par, g * P:(g + 1) * P], eT[:, par, g * P:(g + 1) * P], ident[:])
                mm.then_inc(tp_ready, 1)

            def body(n, par):
                if not is_at(n, B - 1):
                    turn(n + 1, 1 - par)
                pe.wait_ge(eo_ready, n + 1)
                pe.wait_ge(put_ready, n + 1)
                if not is_at(n, 0, 1):
                    pe.wait_ge(y_ready, n - 1)
                for h in range(2):
                    for g in range(EG):
                        mm = nc.tensor.matmul(yp[:, par, h * DM:(h + 1) * DM], put[:, par, g, h * P:(h + 1) * P],
                                              eo[:, par, g, :], start=(g == 0), stop=(g == EG - 1))
                mm.then_inc(yp_ready, 1)

            turn(0, 0)
            by_two(pe, B, body)

        @block.scalar
        def _(act):
            def copy(n, par):
                if not is_at(n, 0, 1):
                    act.wait_ge(tp_ready, n - 1)
                nc.scalar.activation(eT[:, par].rearrange("p (e c) -> p e c", e=E), XG[:, :, bass.ds(n, 1), :], ACT.Copy
                                     ).then_inc(eT_ready, 1)

            def turned(n, par):
                act.wait_ge(tp_ready, n + 1)
                if not is_at(n, 0, 1):
                    act.wait_ge(yp_ready, n - 1)
                nc.scalar.activation(eo[:, par].rearrange("p g d -> p (g d)"), tp[:, par], ACT.Copy).then_inc(eo_ready, 1)

            def body(n, par):
                if not is_at(n, B - 2, B - 1):
                    copy(n + 2, par)
                if not is_at(n, B - 1):
                    turned(n + 1, 1 - par)

            copy(0, 0)
            copy(1, 1)
            turned(0, 0)
            by_two(act, B, body, 3)
            act.wait_ge(var_ready, 1)
            nc.scalar.activation(lnv[:], part[:, 2, :], ACT.Ln, scale=1.0 / P, bias=eps[:, 0:1]).then_inc(ln_ready, 1)
            act.wait_ge(ln_ready, 1)
            nc.scalar.activation(rstd[:], lnv[:], ACT.Exp, scale=-0.5).then_inc(r_ready, 1)

        @block.vector
        def _(dve):
            def places(n, par):
                if not is_at(n, 0, 1):
                    dve.wait_ge(yp_ready, n - 1)
                for e in range(EG):
                    ins = nc.vector.tensor_scalar(put[:, par, e, :], row_t[:], slot_ib[:, e, bass.ds(n, 1)],
                                                  slot_wb[:, e, bass.ds(n, 1)], ALU.is_equal, ALU.mult)
                ins.then_inc(put_ready, 1)

            def body(n, par):
                dve.wait_ge(yp_ready, n + 1)
                yb = Y[:, bass.ds(n, 1)]
                nc.vector.tensor_tensor(yb, yp[:, par, 0:2 * DM].rearrange("p (c d) -> p c d", c=2), yb, ALU.add
                                        ).then_inc(y_ready, 1)
                dve.wait_ge(y_ready, n + 1)
                if not is_at(n, B - 1, B - 2):
                    places(n + 2, par)
                for h in range(2):
                    nc.vector.bn_stats(st[:, bass.ds(2 * n + h, 1), :], Y[:, bass.ds(n, 1), h, :]).then_inc(st_ready, 1)

            places(0, 0)
            places(1, 1)
            by_two(dve, B, body, 3)
            dve.wait_ge(st_ready, TILES)
            total, diff, var = part[:, 0, :], part[:, 1, :], part[:, 2, :]
            nc.vector.tensor_tensor(diff, st[:, :, 1], st[:, :, 4], ALU.subtract).then_inc(sq_ready, 1)
            nc.vector.tensor_tensor(var, st[:, :, 2], st[:, :, 5], ALU.add).then_inc(sq_ready, 1)
            nc.vector.tensor_tensor(total, st[:, :, 1], st[:, :, 4], ALU.add).then_inc(sq_ready, 1)
            dve.wait_ge(sq_ready, 3)
            nc.vector.scalar_tensor_tensor(diff, diff, P / 4, diff, ALU.mult, ALU.mult).then_inc(sq_ready, 1)
            dve.wait_ge(sq_ready, 4)
            nc.vector.tensor_tensor(var, var, diff, ALU.add).then_inc(var_ready, 1)
            nc.vector.tensor_scalar(mean[:], total, 0.5, None, ALU.mult).then_inc(sq_ready, 1)
            dve.wait_ge(sq_ready, 5)
            dve.wait_ge(r_ready, 1)
            with dve.Fori(0, G4) as g:
                for i in range(2 * GB):
                    t = bass.ds(g * (2 * GB) + i, 1)
                    yt = Y[:, bass.ds(g * GB + i // 2, 1), i % 2, :]
                    nc.vector.tensor_scalar(yt, yt, mean[:, t], rstd[:, t], ALU.subtract, ALU.mult).then_inc(n_ready, 1)
                dve.wait_ge(n_ready, 2 * GB * g + 2 * GB)
                xv = X[:, bass.ds(2 * GB * g + 2 * PB, 2 * (GB - PB)), :].rearrange("p (b c) d -> p b c d", c=2)
                nc.vector.tensor_tensor(xv, xv, Y[:, bass.ds(GB * g + PB, GB - PB)], ALU.add).then_inc(x_dve, 1)

        @block.gpsimd
        def _(pool):
            with pool.Fori(0, G4) as g:
                pool.wait_ge(n_ready, 2 * GB * g + 2 * PB)
                xv = X[:, bass.ds(2 * GB * g, 2 * PB), :].rearrange("p (b c) d -> p b c d", c=2)
                nc.gpsimd.tensor_tensor(xv, xv, Y[:, bass.ds(GB * g, PB)], ALU.add).then_inc(x_pool, 1)

        @block.sync
        def _(sp):
            with sp.Fori(0, G4) as g:
                sp.wait_ge(x_dve, g + 1)
                sp.wait_ge(x_pool, g + 1)
                tiles = bass.ds(2 * GB * g, 2 * GB)
                sp.dma_start(out_v[:, tiles, :], X[:, tiles, :]).then_inc(stored, 16)
            sp.wait_ge(stored, 16 * G4)


def kernel(**inputs):
    import concourse.bacc as bacc
    from concourse.bass_utils import run_bass_kernel_spmd

    arrays = lay_out(inputs)
    nc = bacc.Bacc("TRN2", target_bir_lowering=False, num_devices=1)
    feeds, aps = {}, {}
    for name, v in arrays.items():
        feeds[f"in_{name}"] = v
        aps[name] = nc.dram_tensor(f"in_{name}", v.shape, mybir.dt.from_np(v.dtype), kind="ExternalInput").ap()
    shape = inputs["L0_attn_x"].shape
    out = nc.dram_tensor("out", shape, F32, kind="ExternalOutput").ap()
    build(nc, aps, out)
    r = run_bass_kernel_spmd(nc, [feeds], core_ids=[0])
    return r.results[0]["out"]


def lay_out(inputs):
    i = {n.removeprefix("L0_"): np.asarray(v) for n, v in inputs.items()}
    DI, E, F, D = i["attn_out_proj_w"].shape[0], *i["ffn_Wg"].shape

    def rows(w):
        return np.ascontiguousarray(w.reshape(-1, P, w.shape[1]).transpose(1, 0, 2))

    wx = i["attn_x_proj_w"]
    bc = np.concatenate([wx[:, DI + 16:DI + 32], wx[:, DI:DI + 16]], 1)
    return {
        "x": np.ascontiguousarray(i["attn_x"]),
        "w_u": np.ascontiguousarray(i["attn_in_proj_w"][:, 0:DI]),
        "w_z": np.ascontiguousarray(i["attn_in_proj_w"][:, DI:]),
        "conv_w": np.ascontiguousarray(i["attn_conv_w"][:, 0, :].T),
        "conv_b": np.ascontiguousarray(i["attn_conv_b"].reshape(-1, P).T),
        "w_xdT": rows(wx[:, 0:DI].T),
        "w_dt": rows(i["attn_dt_proj_w"]),
        "w_bc": rows(np.concatenate([bc] * 4, 1)),
        "dt_b": np.ascontiguousarray(i["attn_dt_proj_b"].reshape(-1, P).T),
        "w_out": rows(i["attn_out_proj_w"]),
        "a_log": np.ascontiguousarray(i["attn_A_log"].reshape(DI // 64, 64, 2, 8).transpose(2, 1, 0, 3).reshape(P, -1)),
        "dskip": np.ascontiguousarray(i["attn_D_param"].reshape(-1, P).T),
        "gate_wT": np.ascontiguousarray(i["ffn_gate_w"].T),
        "wgT": np.ascontiguousarray(i["ffn_Wg"].transpose(2, 0, 1)),
        "wuT": np.ascontiguousarray(i["ffn_Wu"].transpose(2, 0, 1)),
        "wdT": np.ascontiguousarray(i["ffn_Wd"].reshape(E, D, F // P, P).transpose(3, 0, 2, 1)),
        "wsgT": np.ascontiguousarray(i["ffn_Ws_g"].T),
        "wsuT": np.ascontiguousarray(i["ffn_Ws_u"].T),
        "wsdT": np.ascontiguousarray(i["ffn_Ws_d"].reshape(D, F // P, P).transpose(2, 1, 0)),
    }
```

```python
from contextlib import ExitStack

import numpy as np
import concourse.bass as bass
from concourse import mybir

F32 = mybir.dt.float32
BF16 = mybir.dt.bfloat16
ALU = mybir.AluOpType
ACT = mybir.ActivationFunctionType
AX = mybir.AxisListType

P = 128
EPS = 1e-5
LOG = "natural_log"
LOG_EXP = "natural_log_exp_and_others"


def build(nc, a, out):
    B, S, DM = a["x"].shape
    TOK = B * S
    TILES = TOK // P
    DI = a["w_z"].shape[1]
    H2 = DI // P
    NG = DI // 64
    NSP = 8
    PAIRS = B // 2
    N = 2 * S
    CH = N // P
    STEPS = H2 * 4
    ITEMS = 2 * STEPS
    SPI = 2

    x_v = a["x"].rearrange("b (c p) d -> p (b c) d", p=P)
    out_v = out.rearrange("b (c p) d -> p (b c) d", p=P)
    b_rows = nc.dram_tensor("b_rows", (2, 16, N), F32, kind="Internal").ap()

    with ExitStack() as top:
        def sb(name, shape, dt=F32, ctx=top):
            return ctx.enter_context(nc.sbuf_tensor(name, shape, dt))

        def sem(name, ctx=top):
            return ctx.enter_context(nc.semaphore(name))

        X = sb("X", [P, TILES, DM])
        ident = sb("ident", [P, P])
        stats = sb("stats", [P, TILES, 6])
        mv = sb("mv", [P, TILES, 2])
        lnv = sb("lnv", [P, TILES])
        rstd = sb("rstd", [P, TILES])
        eps = sb("eps", [P, 1])
        xhT = sb("xhT", [P, B, S + 2])
        O = xhT[:, :, 0:S].rearrange("p b (c d) -> p b c d", d=DM)

        mamba(nc, a, X, xhT, O, ident, stats, mv, lnv, rstd, eps, x_v, b_rows,
              dict(B=B, S=S, DM=DM, TILES=TILES, DI=DI, H2=H2, NG=NG, NSP=NSP, PAIRS=PAIRS, N=N,
                   CH=CH, STEPS=STEPS, ITEMS=ITEMS, SPI=SPI))
        experts(nc, a, X, O, xhT, ident, eps, out_v, dict(B=B, S=S, DM=DM, TILES=TILES))


def mamba(nc, a, X, xhT, O, ident, stats, mv, lnv, rstd, eps, x_v, b_rows, k):
    B, S, DM, TILES, DI, H2, NG = (k[n] for n in ("B", "S", "DM", "TILES", "DI", "H2", "NG"))
    NSP, PAIRS, N, CH, STEPS, ITEMS, SPI = (
        k[n] for n in ("NSP", "PAIRS", "N", "CH", "STEPS", "ITEMS", "SPI"))
    RING = 8
    SP1 = S + 2
    with ExitStack() as ctx:
        def sb(name, shape, dt=F32):
            return ctx.enter_context(nc.sbuf_tensor(name, shape, dt))

        def sem(name):
            return ctx.enter_context(nc.semaphore(name))

        w_z = sb("w_z", [P, DI])
        w_conv = sb("w_conv", [P, 3, DI])
        conv_b = sb("conv_b", [P, H2])
        w_delta = sb("w_delta", [P, 2, DI])
        w_bc = sb("w_bc", [P, 2, P])
        dt_b = sb("dt_b", [P, H2])
        w_out = sb("w_out", [P, 2, DM])
        decay = sb("decay", [P, NG * NSP])
        dskip = sb("dskip", [P, H2])
        skip_diag = sb("skip_diag", [P, H2, P])
        fold = sb("fold", [P, 64])
        pick = sb("pick", [P, NSP, P], BF16)

        uz = sb("uz", [P, 2, 4, N])
        dd = sb("dd", [P, 2, H2, N])
        relux, absx = dd[:, 0], dd[:, 1]
        onep = sb("onep", [P, H2, N])
        dup = sb("dup", [P, 2, 2, H2, 2, N])
        bcf = sb("bcf", [P, N])
        c3 = sb("c3", [P, 2, N], BF16)
        b_dup = sb("b_dup", [P, 2, NSP, N])
        states = sb("states", [P, RING, SPI, N])
        da = ctx.enter_context(nc.psum_tensor("da", [P, 2, SPI, N], F32))
        cb = ctx.enter_context(nc.psum_tensor("cb", [P, SPI, N], F32))
        yp = ctx.enter_context(nc.psum_tensor("yp", [P, N], F32))
        mp = ctx.enter_context(nc.psum_tensor("mp", [P, N], F32))

        xh = dup[:, 1, 0].rearrange("p h g (c d) -> p (h g) c d", d=DM)
        w_xdT = dup[:, 1, 1, 0, 0, :].rearrange("p (k n) -> p k n", k=2)
        w_dt = dup[:, 1, 1, 0, 1, :].rearrange("p (k n) -> p k n", k=2)
        w_rest = dup[:, 1, 1, 1].rearrange("p g n -> p (g n)")
        w_u = w_rest[:, 0:DI]
        conv_rows = w_rest[:, DI:4 * DI].rearrange("p (k n) -> p k n", k=3)
        tp = da[:].rearrange("p k s n -> p (k s) n")
        wp = cb
        QT, QP = TILES // 4, PAIRS // 4
        small = [(w_u, "w_u"), (w_z[:], "w_z"), (conv_b[:], "conv_b"), (w_xdT, "w_xdT"), (w_dt, "w_dt"),
                 (w_bc[:], "w_bc"), (dt_b[:], "dt_b"), (w_out[:], "w_out"), (decay[:], "a_log"), (dskip[:], "dskip")]
        SMALL = 16 * len(small)

        x_in = [sem(f"x_in{i}") for i in range(4)]
        w_loaded = sem("w_loaded")
        conv_loaded = sem("conv_loaded")
        id_zero = sem("id_zero")
        id_ready = sem("id_ready")
        pads_ready = sem("pads_ready")
        eps_ready = sem("eps_ready")
        exp_ready = sem("exp_ready")
        decay_ready = sem("decay_ready")
        wc_ready = sem("wc_ready")
        skip_ready = sem("skip_ready")
        wp_ready = sem("wp_ready")
        wd_ready = sem("wd_ready")
        stats_ready = sem("stats_ready")
        mv_ready = sem("mv_ready")
        ln_ready = sem("ln_ready")
        rstd_ready = sem("rstd_ready")
        xh_ready = sem("xh_ready")
        tp_ready = sem("tp_ready")
        tp_free = sem("tp_free")
        da_zeroed = sem("da_zeroed")
        da_ready = sem("da_ready")
        dbu_ready = sem("dbu_ready")
        scan_done = sem("scan_done")
        hc_ready = sem("hc_ready")
        cb_ready = sem("cb_ready")
        sum_done = sem("sum_done")
        gate_done = sem("gate_done")
        mp_ready = sem("mp_ready")
        mp_free = sem("mp_free")
        silu_done = sem("silu_done")
        sp_exp = sem("sp_exp")
        sp_one = sem("sp_one")
        sp_ready = sem("sp_ready")
        sp_lost = sem("sp_lost")
        sp_fixed = sem("sp_fixed")
        delta_ready = sem("delta_ready")
        du_ready = [sem(f"du_ready{h}") for h in range(H2)]
        c_hi = sem("c_hi")
        c_rest = sem("c_rest")
        c_mid = sem("c_mid")
        c3_ready = sem("c3_ready")
        rows_out = [sem(f"rows_out{i}") for i in range(2)]
        b_in = [sem(f"b_in{i}") for i in range(2)]
        dup_in = [[sem(f"dup_in{i}{h}") for h in range(H2)] for i in range(2)]
        block = ctx.enter_context(nc.Block())

        DELTA0, DELTA1, OUT, BC, Z0, Z1, CONV0, CONV1 = range(8)
        BEFORE = (CONV0, CONV1, DELTA0, DELTA1, BC, Z0, Z1)
        before = BEFORE.index

        def place(n, stage):
            if is_at(n, 0):
                return 9 + stage - (stage > OUT)
            if is_at(n, PAIRS - 1):
                return 8 * n + 6
            return 8 * n + 8 + stage

        def over_pairs(eng, body):
            body(0, 0, 0, True, False)
            with eng.Fori(0, (PAIRS - 4) // 2) as j:
                body(2 * j + 1, 1, j, False, False)
                body(2 * j + 2, 0, j + 1, False, False)
            for n in range(PAIRS - 3, PAIRS):
                body(n, n % 2, n // 2, False, n == PAIRS - 1)

        def item(i):
            return i // 8, SPI * (i % 8 // 2), i % 2

        def factors_of(i, par):
            return onep if i == 2 else da[:, (i - (i > 2) + par) % 2]

        def first_columns(v):
            return v.rearrange("p k (b t) -> p (k b) t", b=2)[:, :, 0:1]

        @block.tensor
        def _(pe):
            def project(stage, m, par, no):
                if not (isinstance(no, int) and no == 0):
                    pe.wait_ge(mp_free, no)
                u = uz[:, 1 - par, 2:4, :]
                if stage in (CONV0, CONV1):
                    h = stage - CONV0
                    for tap in range(3):
                        last = nc.tensor.matmul(mp[:].rearrange("p (b t) -> p b t", b=2),
                                                w_conv[:, tap, h * P:(h + 1) * P],
                                                xhT[:, bass.ds(2 * m, 2), tap:tap + S], start=(tap == 0), stop=(tap == 2))
                elif stage in (Z0, Z1):
                    h = stage - Z0
                    last = nc.tensor.matmul(mp[:].rearrange("p (b t) -> p b t", b=2),
                                            w_z[:, h * P:(h + 1) * P],
                                            xhT[:, bass.ds(2 * m, 2), 1:S + 1], start=True, stop=True)
                elif stage in (DELTA0, DELTA1):
                    h = stage - DELTA0
                    pe.wait_ge(silu_done, m + 1)
                    for c in range(2):
                        last = nc.tensor.matmul(mp[:], w_delta[:, c, h * P:(h + 1) * P], u[:, c, :],
                                                start=(c == 0), stop=(c == 1))
                elif stage == BC:
                    for c in range(2):
                        last = nc.tensor.matmul(mp[:], w_bc[:, c, :], u[:, c, :], start=(c == 0), stop=(c == 1))
                last.then_inc(mp_ready, 1)

            def output(m, par, no):
                pe.wait_ge(mp_free, no)
                pe.wait_ge(gate_done, 2 * m + 2)
                for c in range(CH):
                    for h in range(H2):
                        last = nc.tensor.matmul(mp[:, c * DM:(c + 1) * DM], uz[:, par, h, c * P:(c + 1) * P],
                                                w_out[:, h, :], start=(h == 0), stop=(h == 1))
                last.then_inc(mp_ready, 1)

            def sums(m, par, step):
                h, q = step // 4, step % 4
                if q == 0:
                    if not (isinstance(m, int) and m == 0 and h == 0):
                        pe.wait_ge(gate_done, 2 * m + h)
                    nc.tensor.matmul(yp[:], skip_diag[:, h, :], uz[:, 1 - par, 2 + h, :], start=True, stop=False,
                                     skip_group_check=True)
                for s in range(SPI):
                    for i in range(2):
                        last = nc.tensor.matmul(yp[64 * i:64 * i + 64, :], fold[:], states[:, (2 * step + i) % RING, s, :],
                                                start=False, stop=(q == 3 and s == SPI - 1), skip_group_check=True)
                last.then_inc(sum_done, 1)

            def turn(q):
                for n in range(QP * q, QP * q + QP):
                    pe.wait_ge(xh_ready, CH * (n + 1))
                    if n >= 4:
                        pe.wait_ge(tp_free, n - 3)
                    for c in range(CH):
                        last = nc.tensor.transpose(tp[:, n % 4, c * P:(c + 1) * P], xh[:, n % 4, c, :], ident[:])
                    last.then_inc(tp_ready, 1)

            pe.wait_ge(id_ready, 1)
            turn(0)
            pe.wait_ge(w_loaded, SMALL)
            pe.wait_ge(wc_ready, 1)
            pe.wait_ge(pads_ready, 2)
            pe.wait_ge(tp_free, 1)
            project(CONV0, 0, 0, before(CONV0))
            project(CONV1, 0, 0, before(CONV1))
            for c in range(2):
                for r in range(2):
                    last = nc.tensor.matmul(wp[:, c, 0:DI], w_xdT[:, r, c * P:(c + 1) * P], w_dt[:, r, :],
                                            start=(r == 0), stop=(r == 1))
            last.then_inc(wp_ready, 1)
            pe.wait_ge(wd_ready, 1)
            project(DELTA0, 0, 0, before(DELTA0))
            project(DELTA1, 0, 0, before(DELTA1))
            project(BC, 0, 0, before(BC))
            turn(1)
            project(Z0, 0, 0, before(Z0))
            turn(2)
            project(Z1, 0, 0, before(Z1))
            turn(3)
            for no, stage in enumerate((CONV0, CONV1)):
                project(stage, 1, 1, len(BEFORE) + no)
            pe.wait_ge(tp_free, PAIRS)
            pe.wait_ge(id_ready, 4)
            pe.wait_ge(skip_ready, H2 + 1)

            def body(n, par, uses, first, last):
                for s in range(STEPS):
                    if not (first and s == 0):
                        pe.wait_ge(hc_ready, ITEMS * n + 2 * s)
                    if s == 0:
                        pe.wait_ge(c3_ready, n + 1)
                    for i in range(SPI):
                        mm = nc.tensor.matmul(cb[:, i, :], pick[:, SPI * (s % 4) + i, :], c3[:, par, :],
                                              start=True, stop=True)
                    mm.then_inc(cb_ready, 1)
                    if s == 0 and not first:
                        sums(n - 1, 1 - par, STEPS - 1)
                    if s in (1, 2):
                        sums(n, par, s - 1)
                    no = place(n, s)
                    if s == OUT:
                        if not first:
                            output(n - 1, 1 - par, no)
                    elif s in (CONV0, CONV1):
                        if not is_at(n, PAIRS - 2, PAIRS - 1):
                            project(s, n + 2, par, no)
                    elif not last:
                        project(s, n + 1, 1 - par, no)
                    if s > 2:
                        sums(n, par, s - 1)

            over_pairs(pe, body)
            pe.wait_ge(hc_ready, ITEMS * PAIRS)
            sums(PAIRS - 1, (PAIRS - 1) % 2, STEPS - 1)
            output(PAIRS - 1, (PAIRS - 1) % 2, 8 * (PAIRS - 1) + 7)

        @block.scalar
        def _(act):
            def decays(n, par, uses, first, i):
                h, s0, g = item(i)
                factors = factors_of(i, par)
                if i in (0, 8):
                    act.wait_ge(dup_in[par][i // 8], 64 * uses + 64)
                if i == 2:
                    act.wait_ge(delta_ready, H2 * (n + 1))
                elif not (first and i < 2):
                    act.wait_ge(scan_done, ITEMS * n + i - 1 - (i in (3, 4)))
                src = dup[:, par, 0, h, g, :].rearrange("p (b t) -> p b t", b=2)
                for s in range(SPI):
                    col = (2 * h + g) * NSP + s0 + s
                    last = nc.scalar.activation(
                        factors[:, s, :].rearrange("p (b t) -> p b t", b=2)[:, :, 1:S], src[:, :, 1:S],
                        ACT.Exp, scale=decay[:, col:col + 1])
                last.then_inc(da_ready, 1)

            def evacuate(stage, m, par, no):
                act.wait_ge(mp_ready, no + 1)
                if stage in (CONV0, CONV1):
                    h = stage - CONV0
                    last = nc.scalar.activation(uz[:, 1 - par, 2 + h, :], mp[:], ACT.Identity, bias=conv_b[:, h:h + 1])
                elif stage in (Z0, Z1):
                    last = nc.scalar.activation(uz[:, par, stage - Z0, :], mp[:], ACT.Copy)
                elif stage in (DELTA0, DELTA1):
                    h = stage - DELTA0
                    if stage == DELTA0 and not is_at(m, 0):
                        act.wait_ge(delta_ready, H2 * m)
                    nc.scalar.activation(absx[:, h, :], mp[:], ACT.Abs, bias=dt_b[:, h:h + 1])
                    last = nc.scalar.activation(relux[:, h, :], mp[:], ACT.Relu, bias=dt_b[:, h:h + 1])
                elif stage == OUT:
                    last = nc.scalar.activation(O[:, bass.ds(2 * m, 2)], mp[:].rearrange("p (b c d) -> p b c d", b=2, d=DM),
                                                ACT.Copy)
                last.then_inc(mp_free, 1)

            def softplus(m, no):
                act.wait_ge(mp_free, no + 1)
                nc.scalar.activation(absx, absx, ACT.Exp, scale=-1.0).then_inc(sp_exp, 1)
                act.wait_ge(sp_exp, m + 1)
                nc.scalar.activation(onep[:], absx, ACT.Identity, bias=1.0).then_inc(sp_one, 1)

            def log(m):
                act.wait_ge(sp_lost, m + 1)
                nc.scalar.activation(onep[:], onep[:], ACT.Ln).then_inc(sp_ready, 1)

            def parts(m, par, uses, no):
                act.wait_ge(mp_ready, no + 1)
                if not (isinstance(m, int) and m == 0):
                    act.wait_ge(c3_ready, m)
                    act.wait_ge(rows_out[1 - par], 16 * (uses + par))
                    if not (isinstance(m, int) and m == 1):
                        act.wait_ge(cb_ready, STEPS * (m - 1))
                nc.scalar.activation(bcf[:], mp[:], ACT.Copy)
                nc.scalar.activation(c3[:, par, :], mp[:], ACT.Copy).then_inc(c_hi, 1)
                act.wait_ge(c_hi, m + 1)
                act.sem_inc(mp_free, 1)

            def middle(m, par):
                act.wait_ge(c_rest, m + 1)
                nc.scalar.activation(c3[64:P, par, :], bcf[64:P, :], ACT.Copy).then_inc(c_mid, 1)

            def inverse(part, t0, t1):
                act.wait_ge(mv_ready, t1)
                nc.scalar.activation(lnv[:, t0:t1], mv[:, t0:t1, 1], ACT.Ln, bias=eps[:, 0:1]).then_inc(ln_ready, 1)
                act.wait_ge(ln_ready, part + 1)
                nc.scalar.activation(rstd[:, t0:t1], lnv[:, t0:t1], ACT.Exp, scale=-0.5).then_inc(rstd_ready, 1)

            def turned(q):
                for n in range(QP * q, QP * q + QP):
                    act.wait_ge(tp_ready, n + 1)
                    nc.scalar.activation(xhT[:, 2 * n:2 * n + 2, 1:S + 1], tp[:, n % 4, :].rearrange("p (b t) -> p b t", b=2),
                                         ACT.Copy).then_inc(tp_free, 1)

            for tile, name in small:
                act.dma_start(tile, a[name]).then_inc(w_loaded, 16)
            act.dma_start(conv_rows, a["conv_w"].unsqueeze(0).broadcast_to([P, 3, DI])).then_inc(conv_loaded, 16)
            act.wait_ge(eps_ready, 1)
            inverse(0, 0, QT)
            act.wait_ge(decay_ready, 1)
            nc.scalar.activation(decay[:], decay[:], ACT.Exp).then_inc(exp_ready, 1)
            turned(0)
            act.wait_ge(w_loaded, SMALL)
            evacuate(CONV0, 0, 0, before(CONV0))
            evacuate(CONV1, 0, 0, before(CONV1))
            act.wait_ge(mp_free, 2)
            nc.scalar.activation(uz[:, 1, 2:4, :], uz[:, 1, 2:4, :], ACT.Silu).then_inc(silu_done, 1)
            act.wait_ge(wp_ready, 1)
            nc.scalar.activation(w_delta[:], wp[:, :, 0:DI], ACT.Copy).then_inc(wd_ready, 1)
            nc.scalar.preload_act_table_set(LOG_EXP)
            inverse(1, QT, TILES)
            evacuate(DELTA0, 0, 0, before(DELTA0))
            evacuate(DELTA1, 0, 0, before(DELTA1))
            softplus(0, before(DELTA1))
            log(0)
            parts(0, 0, 0, before(BC))
            middle(0, 0)
            turned(1)
            evacuate(Z0, 0, 0, before(Z0))
            turned(2)
            evacuate(Z1, 0, 0, before(Z1))
            turned(3)
            evacuate(CONV0, 1, 1, len(BEFORE))
            act.wait_ge(da_zeroed, 1)
            act.wait_ge(decay_ready, 2)

            def body(n, par, uses, first, last):
                nxt = uses + par if not isinstance(n, int) else (n + 1) // 2
                if not first:
                    nc.scalar.preload_act_table_set(LOG_EXP)
                for s in range(STEPS):
                    for i in ((0, 2, 1), (3,))[s] if s < 2 else (2 * s, 2 * s + 1):
                        decays(n, par, uses, first, i)
                    no = place(n, s - 1)
                    if s == 0:
                        if last:
                            act.wait_ge(mp_free, 8 * n + 6)
                            nc.scalar.activation(uz[:, par, 0:2, :], uz[:, par, 0:2, :], ACT.Silu).then_inc(silu_done, 1)
                        else:
                            evacuate(CONV1, n + 1, 1 - par, 8 if first else 8 * n + 7)
                            act.wait_ge(mp_free, 9 if first else 8 * n + 8)
                            nc.scalar.activation(uz[:, par, :, :], uz[:, par, :, :], ACT.Silu).then_inc(silu_done, 1)
                        nc.scalar.preload_act_table_set(LOG_EXP)
                    elif s == OUT + 1:
                        if not first:
                            evacuate(OUT, n - 1, 1 - par, no)
                    elif s == CONV0 + 1:
                        if not is_at(n, PAIRS - 2, PAIRS - 1):
                            evacuate(CONV0, n + 2, par, no)
                    elif last:
                        pass
                    elif s == BC + 1:
                        log(n + 1)
                        parts(n + 1, 1 - par, nxt, no)
                    else:
                        if s == DELTA0 + 1:
                            act.wait_ge(dup_in[par][1], 64 * uses + 64)
                        evacuate(s - 1, n + 1, 1 - par, no)
                        if s == DELTA1 + 1:
                            softplus(n + 1, no)
                        if s == Z0 + 1:
                            middle(n + 1, 1 - par)

            over_pairs(act, body)
            evacuate(OUT, PAIRS - 1, (PAIRS - 1) % 2, 8 * (PAIRS - 1) + 7)
            act.wait_ge(mp_free, 8 * (PAIRS - 1) + 8)

        @block.gpsimd
        def _(pool):
            def delta(m, par):
                pool.wait_ge(sp_ready, m + 1)
                pool.wait_ge(sp_fixed, m + 1)
                pool.wait_ge(silu_done, m + 1)
                for h in range(H2):
                    nc.gpsimd.tensor_tensor(dd[:, 0, h], dd[:, 0, h], onep[:, h], ALU.add).then_inc(delta_ready, 1)
                    pool.wait_ge(delta_ready, H2 * m + h + 1)
                    nc.gpsimd.tensor_tensor(dd[:, 1, h], dd[:, 0, h], uz[:, 1 - par, 2 + h, :], ALU.mult).then_inc(du_ready[h], 1)

            nc.gpsimd.memset(ident[:], 0.0).then_inc(id_zero, 1)
            nc.gpsimd.memset(pick[:], 0.0).then_inc(id_zero, 1)
            pool.wait_ge(id_zero, 2)
            nc.gpsimd.affine_select(out=ident[:], in_=ident[:], compare_op=ALU.not_equal, fill=1.0,
                                    base=0, pattern=[[-1, P]], channel_multiplier=1).then_inc(id_ready, 1)
            nc.gpsimd.memset(xhT[:, :, 0:1], 0.0).then_inc(pads_ready, 1)
            nc.gpsimd.memset(xhT[:, :, SP1 - 1:SP1], 0.0).then_inc(pads_ready, 1)
            v = pick[:].rearrange("p s (h j) -> p s h j", h=2)
            for n, off in enumerate((0, 64, 96)):
                if n:
                    pool.wait_ge(id_ready, n + 1)
                nc.gpsimd.affine_select(out=v, in_=v, compare_op=ALU.not_equal, fill=1.0, base=-off,
                                        pattern=[[-1, NSP], [-NSP, 2], [0, 64]],
                                        channel_multiplier=1).then_inc(id_ready, 1)
            delta(0, 0)

            def body(n, par, uses, first, last):
                for i in range(ITEMS):
                    h, s0, g = item(i)
                    if i in (0, 8):
                        pool.wait_ge(dup_in[par][h], 64 * uses + 64)
                    if i == 0:
                        pool.wait_ge(b_in[par], 32 * uses + 32)
                    if i % 2 == 0 and not (first and i < RING):
                        pool.wait_ge(sum_done, STEPS * n + (i - RING) // 2 + 1)
                    nc.gpsimd.tensor_tensor(states[:, i % RING], b_dup[:, par, s0:s0 + SPI, :],
                                            dup[:, par, 1, h, g, :].unsqueeze(1).broadcast_to([P, SPI, N]),
                                            ALU.mult).then_inc(dbu_ready, 1)
                    if i == 11 and not last:
                        delta(n + 1, 1 - par)

            over_pairs(pool, body)

        @block.vector
        def _(dve):
            def softplus(m):
                dve.wait_ge(sp_one, m + 1)
                nc.vector.scalar_tensor_tensor(absx, onep[:], -1.0, absx, ALU.add, ALU.subtract).then_inc(sp_lost, 1)
                dve.wait_ge(sp_lost, m + 1)
                nc.vector.tensor_tensor(relux, relux, absx, ALU.subtract).then_inc(sp_fixed, 1)

            def split(m, par):
                dve.wait_ge(c_hi, m + 1)
                nc.vector.tensor_tensor(bcf[64:P, :], bcf[64:P, :], c3[64:P, par, :], ALU.subtract).then_inc(c_rest, 1)

            def low(m, par):
                dve.wait_ge(c_mid, m + 1)
                nc.vector.tensor_tensor(c3[96:P, par, :], bcf[96:P, :], c3[96:P, par, :], ALU.subtract).then_inc(c3_ready, 1)

            def times_c(n, i):
                dve.wait_ge(scan_done, ITEMS * n + i + 1)
                if i % 2 == 0:
                    dve.wait_ge(cb_ready, STEPS * n + i // 2 + 1)
                nc.vector.tensor_tensor(states[:, i % RING], states[:, i % RING], cb[:], ALU.mult).then_inc(hc_ready, 1)

            def gate(n, par, h):
                dve.wait_ge(sum_done, STEPS * n + 4 * h + 4)
                if h == 0:
                    dve.wait_ge(silu_done, n + 2)
                nc.vector.tensor_tensor(uz[:, par, h, :], yp[:], uz[:, par, h, :], ALU.mult).then_inc(gate_done, 1)

            def statistics(t0, t1):
                for t in range(t0, t1):
                    nc.vector.bn_stats(stats[:, t, :], X[:, t, :]).then_inc(stats_ready, 1)
                for t in range(t0, t1):
                    dve.wait_ge(stats_ready, t + 1)
                    nc.vector.bn_aggr(mv[:, t, :], stats[:, t, :]).then_inc(mv_ready, 1)

            def norm(q):
                for n in range(QP * q, QP * q + QP):
                    if n >= 4:
                        dve.wait_ge(tp_ready, n - 3)
                    for c in range(CH):
                        t = CH * n + c
                        nc.vector.tensor_scalar(xh[:, n % 4, c, :], X[:, t, :], mv[:, t, 0:1], rstd[:, t:t + 1],
                                                ALU.subtract, ALU.mult).then_inc(xh_ready, 1)

            nc.vector.memset(eps[:], EPS).then_inc(eps_ready, 1)
            dve.wait_ge(x_in[0], 16)
            statistics(0, QT)
            dve.wait_ge(w_loaded, SMALL)
            nc.vector.tensor_scalar(decay[:], decay[:], 60.0, None, ALU.min).then_inc(decay_ready, 1)
            dve.wait_ge(conv_loaded, 16)
            nc.vector.tensor_tensor(w_conv[:], conv_rows, w_u.unsqueeze(1).broadcast_to([P, 3, DI]), ALU.mult
                                    ).then_inc(wc_ready, 1)
            dve.wait_ge(id_ready, 1)
            for h in range(H2):
                nc.vector.tensor_scalar(skip_diag[:, h, :], ident[:], dskip[:, h:h + 1], None, ALU.mult).then_inc(skip_ready, 1)
            nc.vector.tensor_tensor(fold[:], ident[:, 0:64], ident[:, 64:P], ALU.add).then_inc(skip_ready, 1)
            dve.wait_ge(rstd_ready, 1)
            norm(0)
            dve.wait_ge(exp_ready, 1)
            nc.vector.tensor_scalar(decay[:], decay[:], -1.0, None, ALU.mult).then_inc(decay_ready, 1)
            for i in range(1, 4):
                dve.wait_ge(x_in[i], 16)
                statistics(i * QT, (i + 1) * QT)
            dve.wait_ge(rstd_ready, 2)
            norm(1)
            softplus(0)
            split(0, 0)
            low(0, 0)
            norm(2)
            norm(3)
            dve.wait_ge(tp_free, PAIRS)
            nc.vector.memset(first_columns(da[:].rearrange("p k s n -> p (k s) n")), 0.0).then_inc(da_zeroed, 1)
            dve.wait_ge(da_zeroed, 1)

            def body(n, par, uses, first, last):
                for i in range(ITEMS):
                    if i == 1:
                        dve.wait_ge(delta_ready, H2 * (n + 1))
                        nc.vector.memset(first_columns(onep[:]), 0.0).then_inc(da_zeroed, 1)
                    if i == 2:
                        dve.wait_ge(da_zeroed, n + 2)
                    dve.wait_ge(da_ready, ITEMS * n + i + 1 + (i == 1))
                    dve.wait_ge(dbu_ready, ITEMS * n + i + 1)
                    nc.vector.tensor_tensor_scan(states[:, i % RING].rearrange("p s t -> p (s t)"),
                                                 factors_of(i, par)[:].rearrange("p s t -> p (s t)"),
                                                 states[:, i % RING].rearrange("p s t -> p (s t)"),
                                                 0.0, ALU.mult, ALU.add).then_inc(scan_done, 1)
                    if i:
                        times_c(n, i - 1)
                    elif not first:
                        times_c(n - 1, ITEMS - 1)
                    if i == 2 and not first:
                        gate(n - 1, 1 - par, 1)
                    if i == 10:
                        gate(n, par, 0)
                    if i == 5 and not last:
                        softplus(n + 1)
                    if i == 10 and not last:
                        split(n + 1, 1 - par)
                    if i == 12 and not last:
                        low(n + 1, 1 - par)

            over_pairs(dve, body)
            times_c(PAIRS - 1, ITEMS - 1)
            gate(PAIRS - 1, (PAIRS - 1) % 2, 1)
            dve.wait_ge(gate_done, 2 * PAIRS)

        @block.sync
        def _(sp):
            def spread(m, par, uses):
                sp.wait_ge(c_hi, m + 1)
                if not (isinstance(m, int) and m < 2):
                    sp.wait_ge(b_in[par], 32 * uses)
                    sp.wait_ge(dbu_ready, ITEMS * (m - 1))
                    sp.wait_ge(da_ready, ITEMS * (m - 1))
                sp.dma_start(b_rows[par], bcf[16:32, :]).then_inc(rows_out[par], 16)
                sp.wait_ge(rows_out[par], 16 * uses + 16)
                for sh in range(2):
                    sp.dma_start(b_dup[64 * sh:64 * sh + 64, par],
                                 b_rows[par, NSP * sh:NSP * sh + NSP, :].unsqueeze(0).broadcast_to([64, NSP, N])
                                 ).then_inc(b_in[par], 16)
                for h in range(H2):
                    sp.wait_ge(du_ready[h], m + 1)
                    for g in range(2):
                        for sh in range(2):
                            sp.dma_start(dup[64 * sh:64 * sh + 64, par, :, h, g, :],
                                         dd[64 * g:64 * g + 64, :, h]).then_inc(dup_in[par][h], 16)

            for i in range(4):
                if i == 1:
                    sp.wait_ge(w_loaded, SMALL)
                sp.dma_start(X[:, i * QT:(i + 1) * QT, :], x_v[:, i * QT:(i + 1) * QT, :]).then_inc(x_in[i], 16)
            spread(0, 0, 0)
            spread(1, 1, 0)
            with sp.Fori(0, (PAIRS - 2) // 2) as j:
                spread(2 * j + 2, 0, j + 1)
                spread(2 * j + 3, 1, j + 1)
            for i in range(2):
                sp.wait_ge(rows_out[i], 16 * PAIRS // 2)
                sp.wait_ge(b_in[i], 32 * PAIRS // 2)


def experts(nc, a, X, O, xhT, ident, eps, out_v, k):
    B, S, DM, TILES = (k[n] for n in ("B", "S", "DM", "TILES"))
    E, F = a["wgT"].shape[1:]
    CAP = int(S * 2.0 / E)
    FH = F // P
    PAIRS, N, CH = B // 2, 2 * S, 2 * S // P
    GB = P // E
    GROUPS = B // GB
    SLOTS = E * CAP
    EG = SLOTS // P
    Y = O

    with ExitStack() as ctx:
        def sb(name, shape, dt=F32, c=ctx):
            return c.enter_context(nc.sbuf_tensor(name, shape, dt))

        def ps(name, shape, c):
            return c.enter_context(nc.psum_tensor(name, shape, F32))

        def sems(c, *names):
            return [c.enter_context(nc.semaphore(n)) for n in names]

        mvf = sb("mvf", [P, TILES, 2])
        rstdf = sb("rstdf", [P, TILES])
        gate_wT = sb("gate_wT", [P, E])
        wsgT = sb("wsgT", [P, F])
        wsuT = sb("wsuT", [P, F])
        wsdT = sb("wsdT", [P, FH, DM])
        mask_e = sb("mask_e", [P, E])
        mask_b = sb("mask_b", [P, GB])
        pick_b = sb("pick_b", [P, GB, P], BF16)
        row_t = sb("row_t", [P, S])
        col_t = sb("col_t", [P, 2])
        idx_x = sb("idx_x", [P, GROUPS, SLOTS], BF16)
        slot_i = sb("slot_i", [P, EG, GROUPS, GB])
        slot_w = sb("slot_w", [P, EG, GROUPS, GB])

        def normed(dve, dst, t):
            return nc.vector.tensor_scalar(dst, X[:, bass.ds(t, 1), :], mvf[:, bass.ds(t, 1), 0], rstdf[:, bass.ds(t, 1)],
                                           ALU.subtract, ALU.mult)

        with ExitStack() as c:
            G4 = 4
            GP, GT = PAIRS // G4, TILES // G4
            st = sb("st", [P, TILES, 6], c=c)
            mvo = sb("mvo", [P, TILES, 2], c=c)
            part = sb("part", [P, 2, TILES], c=c)
            lno = sb("lno", [P, 2, TILES], c=c)
            rstdo = sb("rstdo", [P, TILES], c=c)
            i_t = sb("i_t", [P, S], mybir.dt.int32, c=c)
            i_p = sb("i_p", [P, 2], mybir.dt.int32, c=c)
            xf = sb("xf", [P, 2, CH, DM], c=c)
            hT = sb("hT", [P, GP, N], c=c)
            gl = sb("gl", [P, FH, N], c=c)
            hs = sb("hs", [P, FH, N], c=c)
            tp, lp, yp = ps("tp3", [P, N], c), ps("lp3", [P, N], c), ps("yp3", [P, N], c)
            gp, up = ps("gp", [P, FH, N], c), ps("up", [P, FH, N], c)
            top = sb("top", [P, TILES], c=c)
            den = sb("den", [P, TILES], c=c)
            scores = sb("scores", [P, 2, B, E], c=c)
            rest = sb("rest", [P, GROUPS, 2, S], c=c)
            L = sb("L", [P, TILES, E], c=c)
            best = sb("best", [P, GROUPS, CAP], c=c)
            best_i = sb("best_i", [P, GROUPS, CAP], mybir.dt.uint32, c=c)
            best_f = sb("best_f", [P, GROUPS, CAP], c=c)
            w_x = sb("w_x", [P, GROUPS, SLOTS], c=c)
            sp_t = [v[:, S * i:S * (i + 1)] for v in (tp, lp) for i in range(2)]
            sl = ps("sl", [P, GROUPS, 2, EG, GB], c)
            me = mask_e[:].unsqueeze(2).broadcast_to([P, E, CAP])
            soft, exp_done, sc_ready, turned_s, found, taken, spread, expanded, w_expanded, sl_ready, sl_out = sems(
                c, "soft", "exp_done", "sc_ready", "turned_s", "found", "taken", "spread", "expanded", "w_expanded",
                "sl_ready", "sl_out")
            wf_loaded, ones_set, masks_ready, iota_ready, copied = sems(
                c, "wf_loaded", "ones_set", "masks_ready", "iota_ready", "copied")
            so_ready, mo_ready, lo_ready, ro_ready, on_ready = sems(c, "so_ready", "mo_ready", "lo_ready", "ro_ready", "on_ready")
            sx_ready, mx_ready, lx_ready, rx_ready, x_ready = sems(c, "sx_ready", "mx_ready", "lx_ready", "rx_ready", "x_ready")
            comb_ready, xf_ready, tp_ready, hT_ready, lp_ready, lp_free = sems(
                c, "comb_ready", "xf_ready", "tp3_ready", "hT_ready", "lp_ready", "lp_free")
            gp_ready, gl_ready, up_ready, hs_ready, yp_ready, yp_free = sems(
                c, "gp_ready", "gl_ready", "up_ready", "hs_ready", "yp_ready", "yp_free")
            block = c.enter_context(nc.Block())

            def groups(eng, body):
                body(0)
                with eng.Fori(0, G4 - 2) as j:
                    body(j + 1)

            LAST = range(PAIRS - GP, PAIRS)

            @block.sync
            def _(sp):
                for tile, name in ((gate_wT, "gate_wT"), (wsgT, "wsgT"), (wsuT, "wsuT"), (wsdT, "wsdT")):
                    sp.dma_start(tile[:], a[name]).then_inc(wf_loaded, 16)

            @block.gpsimd
            def _(pool):
                nc.gpsimd.memset(mask_e[:], 0.0).then_inc(ones_set, 1)
                nc.gpsimd.memset(mask_b[:], 1.0).then_inc(ones_set, 1)
                nc.gpsimd.iota(i_t[:], pattern=[[1, S]], base=0, channel_multiplier=0).then_inc(iota_ready, 1)
                nc.gpsimd.iota(i_p[:], pattern=[[P, 2]], base=0, channel_multiplier=1).then_inc(iota_ready, 1)
                pool.wait_ge(ones_set, 2)
                nc.gpsimd.affine_select(out=mask_b[:], in_=mask_b[:], compare_op=ALU.is_ge, fill=0.0, base=0,
                                        pattern=[[-E, GB]], channel_multiplier=1).then_inc(masks_ready, 1)
                pool.wait_ge(masks_ready, 1)
                nc.gpsimd.affine_select(out=mask_b[:], in_=mask_b[:], compare_op=ALU.is_ge, fill=0.0, base=E - 1,
                                        pattern=[[E, GB]], channel_multiplier=-1).then_inc(masks_ready, 1)
                for n in range(GB):
                    if n:
                        pool.wait_ge(masks_ready, n + 2)
                    nc.gpsimd.affine_select(out=mask_e[:], in_=mask_e[:], compare_op=ALU.not_equal, fill=1.0,
                                            base=-E * n, pattern=[[-1, E]], channel_multiplier=1).then_inc(masks_ready, 1)
                with pool.Fori(0, PAIRS) as n:
                    pool.wait_ge(on_ready, CH * n + CH)
                    gx = X[:, bass.ds(CH * n, CH), :].rearrange("p (b c) d -> p b c d", c=2)
                    nc.gpsimd.tensor_tensor(gx, gx, O[:, bass.ds(2 * n, 2)], ALU.add).then_inc(x_ready, 1)
                for g in range(GROUPS):
                    pool.wait_ge(found, GROUPS * (CAP // 8 - 1) + g + 1)
                    nc.gpsimd.tensor_tensor(w_x[:, g].rearrange("p (e c) -> p e c", e=E), me,
                                            best[:, g].unsqueeze(1).broadcast_to([P, E, CAP]), ALU.mult).then_inc(w_expanded, 1)

            @block.scalar
            def _(act):
                def inverse(g, mvt, r, l, ready, l_ready, r_ready):
                    act.wait_ge(ready, 2 * g + 2)
                    nc.scalar.activation(lno[:, l, bass.ds(g * GT, GT)], mvt[:, bass.ds(g * GT, GT), 1], ACT.Ln,
                                         scale=1.0 / P, bias=eps[:, 0:1]).then_inc(l_ready, 1)
                    act.wait_ge(l_ready, g + 1)
                    nc.scalar.activation(r[:, bass.ds(g * GT, GT)], lno[:, l, bass.ds(g * GT, GT)], ACT.Exp,
                                         scale=-0.5).then_inc(r_ready, 1)

                def inverse_o(g):
                    inverse(g, mvo, rstdo, 0, mo_ready, lo_ready, ro_ready)

                def inverse_x(g):
                    inverse(g, mvf, rstdf, 1, mx_ready, lx_ready, rx_ready)

                def turned(n, i):
                    act.wait_ge(tp_ready, n + 1)
                    if not is_at(n, 0, 1, 2, 3):
                        act.wait_ge(up_ready, FH * (n - 3))
                    nc.scalar.activation(hT[:, i, :], tp[:], ACT.Copy).then_inc(hT_ready, 1)

                def gelus(n):
                    for h in range(FH):
                        act.wait_ge(gp_ready, FH * n + h + 1)
                        if not is_at(n, 0):
                            act.wait_ge(hs_ready, FH * (n - 1) + h + 1)
                        nc.scalar.activation(gl[:, h], gp[:, h], ACT.Gelu).then_inc(gl_ready, 1)

                def evacuate(n):
                    act.wait_ge(yp_ready, n + 1)
                    nc.scalar.activation(Y[:, bass.ds(2 * n, 2)], yp[:].rearrange("p (b c d) -> p b c d", b=2, d=DM),
                                         ACT.Copy).then_inc(yp_free, 1)

                def body(g):
                    for i in range(GP):
                        n = GP * g + i
                        gelus(n)
                        if i == 1:
                            inverse_o(g + 1)
                        if i < 3:
                            turned(n + 1, i + 1)
                            evacuate(n)
                        else:
                            inverse_x(g + 1)
                            evacuate(n)
                            turned(n + 1, 0)

                inverse_o(0)
                inverse_x(0)
                turned(0, 0)
                groups(act, body)
                for i in range(1, GP):
                    turned(LAST[i], i)
                gelus(LAST[0])
                act.wait_ge(soft, 2)
                nc.scalar.activation(L[:], L[:], ACT.Exp).then_inc(exp_done, 1)
                for n in LAST[1:]:
                    gelus(n)
                    evacuate(n - 1)
                evacuate(LAST[-1])
                act.wait_ge(yp_free, PAIRS)

            @block.vector
            def _(dve):
                def statistics(g, which, source, s_ready, mvt, m_ready):
                    for t in range(GT * g, GT * g + GT):
                        nc.vector.bn_stats(st[:, t, :], source(t)).then_inc(s_ready, 1)
                    dve.wait_ge(s_ready, GT * g + GT)
                    gs = bass.ds(g * GT, GT)
                    s_ap, d_ap = part[:, 0, gs], part[:, 1, gs]
                    nc.vector.tensor_tensor(s_ap, st[:, gs, 1], st[:, gs, 4], ALU.add).then_inc(comb_ready, 1)
                    nc.vector.tensor_tensor(d_ap, st[:, gs, 1], st[:, gs, 4], ALU.subtract).then_inc(comb_ready, 1)
                    nc.vector.tensor_tensor(mvt[:, gs, 1], st[:, gs, 2], st[:, gs, 5], ALU.add).then_inc(comb_ready, 1)
                    dve.wait_ge(comb_ready, 8 * g + 4 * which + 3)
                    nc.vector.tensor_scalar(mvt[:, gs, 0], s_ap, 0.5, None, ALU.mult).then_inc(m_ready, 1)
                    nc.vector.scalar_tensor_tensor(d_ap, d_ap, P / 4, d_ap, ALU.mult, ALU.mult).then_inc(comb_ready, 1)
                    dve.wait_ge(comb_ready, 8 * g + 4 * which + 4)
                    nc.vector.tensor_tensor(mvt[:, gs, 1], mvt[:, gs, 1], d_ap, ALU.add).then_inc(m_ready, 1)

                def statistics_o(g):
                    statistics(g, 0, lambda t: O[:, t // 2, t % 2, :], so_ready, mvo, mo_ready)

                def statistics_x(g):
                    dve.wait_ge(x_ready, GP * (g + 1))
                    statistics(g, 1, lambda t: X[:, t, :], sx_ready, mvf, mx_ready)

                def norm_o(g):
                    dve.wait_ge(ro_ready, g + 1)
                    for t in range(GT * g, GT * g + GT):
                        o = O[:, t // 2, t % 2, :]
                        nc.vector.tensor_scalar(o, o, mvo[:, t, 0:1], rstdo[:, t:t + 1], ALU.subtract, ALU.mult
                                                ).then_inc(on_ready, 1)

                def norm(n, par):
                    if not is_at(n, 0, 1):
                        dve.wait_ge(tp_ready, n - 1)
                    for i in range(CH):
                        ins = normed(dve, xf[:, par, i, :], CH * n + i)
                    ins.then_inc(xf_ready, 1)

                def take_logits(n):
                    dve.wait_ge(lp_ready, n + 1)
                    nc.vector.tensor_copy(L[:, bass.ds(CH * n, CH), :], lp[:, 0:CH * E].rearrange("p (c e) -> p c e", e=E)
                                          ).then_inc(lp_free, 1)

                def products(n):
                    if not is_at(n, 0):
                        dve.wait_ge(yp_ready, n)
                    for h in range(FH):
                        dve.wait_ge(up_ready, FH * n + h + 1)
                        dve.wait_ge(gl_ready, FH * n + h + 1)
                        nc.vector.tensor_tensor(hs[:, h], gl[:, h], up[:, h], ALU.mult).then_inc(hs_ready, 1)

                def body(g):
                    for i in range(GP):
                        n, par = GP * g + i, i % 2
                        take_logits(n)
                        products(n)
                        if i < 2:
                            norm(n + 2, par)
                        if i == 0:
                            statistics_o(g + 1)
                        elif i == 1:
                            norm_o(g + 1)
                        elif i == 2:
                            statistics_x(g + 1)
                        else:
                            dve.wait_ge(rx_ready, g + 2)
                            norm(n + 1, 1 - par)
                            norm(n + 2, par)

                statistics_o(0)
                dve.wait_ge(iota_ready, 2)
                nc.vector.tensor_copy(row_t[:], i_t[:]).then_inc(copied, 1)
                nc.vector.tensor_copy(col_t[:], i_p[:]).then_inc(copied, 1)
                norm_o(0)
                dve.wait_ge(masks_ready, 2 + GB)
                nc.vector.tensor_copy(pick_b[:], mask_b[:].unsqueeze(2).broadcast_to([P, GB, P])).then_inc(copied, 1)
                statistics_x(0)
                dve.wait_ge(rx_ready, 1)
                norm(0, 0)
                norm(1, 1)
                for g in range(G4 - 1):
                    body(g)
                norm(LAST[2], 0)
                take_logits(LAST[0])
                norm(LAST[3], 1)
                for n in LAST[1:]:
                    take_logits(n)
                dve.wait_ge(lp_free, PAIRS)
                wide = [P, TILES, E]
                nc.vector.tensor_reduce(top[:], L[:], AX.X, ALU.max).then_inc(soft, 1)
                dve.wait_ge(soft, 1)
                nc.vector.tensor_tensor(L[:], L[:], top[:].unsqueeze(2).broadcast_to(wide), ALU.subtract).then_inc(soft, 1)
                products(LAST[0])
                dve.wait_ge(exp_done, 1)
                nc.vector.tensor_reduce(den[:], L[:], AX.X, ALU.add).then_inc(soft, 1)
                dve.wait_ge(soft, 3)
                nc.vector.reciprocal(den[:], den[:]).then_inc(soft, 1)
                dve.wait_ge(soft, 4)
                lv = L[:].rearrange("p (b c) e -> p c b e", c=2)
                dv = den[:].rearrange("p (b c) -> p c b", c=2)
                for h in range(2):
                    nc.vector.tensor_tensor(scores[:, h], lv[:, h], dv[:, h].unsqueeze(2).broadcast_to([P, B, E]),
                                            ALU.mult).then_inc(sc_ready, 1)
                for r in range(CAP // 8):
                    if r < GP - 1:
                        products(LAST[r + 1])
                    for g in range(GROUPS):
                        src = sp_t[g] if r == 0 else rest[:, g, (r - 1) % 2, :]
                        if r == 0:
                            dve.wait_ge(turned_s, g - g % 2 + 2)
                        else:
                            dve.wait_ge(taken, GROUPS * (r - 1) + g + 1)
                        b8 = best[:, g, 8 * r:8 * r + 8]
                        nc.vector.max(b8, src).then_inc(found, 1)
                        dve.wait_ge(found, GROUPS * r + g + 1)
                        nc.vector.max_index(best_i[:, g, 8 * r:8 * r + 8], b8, src).then_inc(spread, 1)
                        if r < CAP // 8 - 1:
                            nc.vector.match_replace(rest[:, g, r % 2, :], b8, src, -1.0).then_inc(taken, 1)
                n = CAP // 8 * GROUPS
                dve.wait_ge(spread, n)
                nc.vector.tensor_copy(best_f[:], best_i[:]).then_inc(spread, 1)
                dve.wait_ge(spread, n + 1)
                for g in range(GROUPS):
                    nc.vector.tensor_tensor(idx_x[:, g].rearrange("p (e c) -> p e c", e=E), me,
                                            best_f[:, g].unsqueeze(1).broadcast_to([P, E, CAP]), ALU.mult).then_inc(expanded, 1)
                dve.wait_ge(sl_ready, 1)
                nc.vector.tensor_copy(slot_i[:], sl[:, :, 0].rearrange("p g e b -> p e g b")).then_inc(sl_out, 1)
                nc.vector.tensor_copy(slot_w[:], sl[:, :, 1].rearrange("p g e b -> p e g b")).then_inc(sl_out, 1)
                dve.wait_ge(sl_out, 2)
                dve.wait_ge(copied, 3)

            @block.tensor
            def _(pe):
                def turn(n, par):
                    pe.wait_ge(xf_ready, n + 1)
                    if not is_at(n, 0):
                        pe.wait_ge(hT_ready, n)
                    for i in range(CH):
                        mm = nc.tensor.transpose(tp[:, i * P:(i + 1) * P], xf[:, par, i, :], ident[:])
                    mm.then_inc(tp_ready, 1)

                def logits(n, k):
                    pe.wait_ge(hT_ready, n + 1)
                    if not is_at(n, 0):
                        pe.wait_ge(lp_free, n)
                    for i in range(CH):
                        mm = nc.tensor.matmul(lp[:, i * E:(i + 1) * E], hT[:, k, i * P:(i + 1) * P], gate_wT[:],
                                              start=True, stop=True)
                    mm.then_inc(lp_ready, 1)

                def gate_up(n, k):
                    for h in range(FH):
                        if not is_at(n, 0):
                            pe.wait_ge(gl_ready, FH * (n - 1) + h + 1)
                            pe.wait_ge(hs_ready, FH * (n - 1) + h + 1)
                        nc.tensor.matmul(gp[:, h], wsgT[:, h * P:(h + 1) * P], hT[:, k, :], start=True, stop=True
                                         ).then_inc(gp_ready, 1)
                        nc.tensor.matmul(up[:, h], wsuT[:, h * P:(h + 1) * P], hT[:, k, :], start=True, stop=True
                                         ).then_inc(up_ready, 1)

                def down(n):
                    pe.wait_ge(hs_ready, FH * n + FH)
                    if not is_at(n, 0):
                        pe.wait_ge(yp_free, n)
                    for i in range(CH):
                        for h in range(FH):
                            mm = nc.tensor.matmul(yp[:, i * DM:(i + 1) * DM], hs[:, h, i * P:(i + 1) * P], wsdT[:, h, :],
                                                  start=(h == 0), stop=(h == FH - 1))
                    mm.then_inc(yp_ready, 1)

                def body(g):
                    for k in range(GP):
                        n, par = GP * g + k, k % 2
                        logits(n, k)
                        gate_up(n, k)
                        if k < 3:
                            turn(n + 1, 1 - par)
                        down(n)
                        if k == 3:
                            turn(n + 1, 1 - par)

                pe.wait_ge(wf_loaded, 64)
                turn(0, 0)
                groups(pe, body)
                logits(LAST[0], 0)
                for k in range(1, GP):
                    turn(LAST[k], k % 2)
                    logits(LAST[k], k)
                gate_up(LAST[0], 0)
                down(LAST[0])
                gate_up(LAST[1], 1)
                pe.wait_ge(sc_ready, 2)
                for g in range(GROUPS):
                    for h in range(2):
                        mm = nc.tensor.transpose(sp_t[g][:, h * P:(h + 1) * P],
                                                 scores[:, h, g * GB:(g + 1) * GB, :].rearrange("p b e -> p (b e)"), ident[:])
                    mm.then_inc(turned_s, 1)
                down(LAST[1])
                for k in range(2, GP):
                    gate_up(LAST[k], k)
                    down(LAST[k])
                for g in range(GROUPS):
                    for w, (x, mask, ready) in enumerate(((idx_x, pick_b[:, :, 0], expanded), (w_x, mask_b[:], w_expanded))):
                        pe.wait_ge(ready, g + 1)
                        for e in range(EG):
                            mm = nc.tensor.matmul(sl[:, g, w, e, :], x[:, g, e * P:(e + 1) * P], mask, start=True, stop=True)
                mm.then_inc(sl_ready, 1)

        XG = sb("XG", [P, E, B, CAP])
        WB = 2
        weights = [sb("wg", [P, WB, F]), sb("wu", [P, WB, F]), sb("wd", [P, WB, FH, DM])]
        w_in = sems(ctx, *(f"we{i}" for i in range(WB)))

        def load_weights(sp, n, par):
            for tile, name in zip(weights, ("wgT", "wuT", "wdT")):
                sp.dma_start(tile[:, par], a[name][:, bass.ds(n, 1)]).then_inc(w_in[par], 16)

        gather(nc, XG, normed, idx_x, pick_b, col_t, load_weights, k)
        XO = XG[:].rearrange("p (g e) b c -> p g (e b c)", g=EG).rearrange("p g (b d) -> p g b d", d=DM)
        first_out = sb("first_out", [P, 1, B, DM])
        run_experts(nc, XG, XO, first_out, weights, w_in, load_weights)
        scatter(nc, X, Y, [first_out[:, 0]] + [XO[:, g] for g in range(EG - 1)], row_t, slot_i, slot_w, eps, out_v, k)


def by_two(eng, count, body, tail=1):
    body(0, 0)
    with eng.Fori(0, (count - tail) // 2) as j:
        body(2 * j + 1, 1)
        body(2 * j + 2, 0)
    for n in range(count - tail, count):
        body(n, n % 2)


def is_at(n, *values):
    return isinstance(n, int) and n in values


def gather(nc, XG, normed, idx_x, pick_b, col_t, load_weights, k):
    E, B, CAP = XG.shape[1:]
    SLOTS, GB, DM = E * CAP, pick_b.shape[1], k["DM"]
    with ExitStack() as c:
        def sb(name, shape, dt=F32):
            return c.enter_context(nc.sbuf_tensor(name, shape, dt))

        xt = sb("xt", [P, B, 2, DM])
        x_hi, x_lo = sb("x_hi", [P, B, 2, DM], BF16), sb("x_lo", [P, 2, 2, 2, DM], BF16)
        ib = sb("ib", [P, 2, SLOTS], BF16)
        hot = sb("hot", [P, 2, 2, SLOTS], BF16)
        ip = c.enter_context(nc.psum_tensor("ip", [P, 2, SLOTS], F32))
        xp = c.enter_context(nc.psum_tensor("xp", [P, 2, SLOTS], F32))
        ip_ready, ib_ready, hot_ready, xt_ready, hi_ready, rest_ready, mid_ready, low_ready, xp_ready, xp_free = [
            c.enter_context(nc.semaphore(n + "_g")) for n in (
                "ip_ready", "ib_ready", "hot_ready", "xt_ready", "hi_ready", "rest_ready", "mid_ready", "low_ready",
                "xp_ready", "xp_free")]
        block = c.enter_context(nc.Block())

        @block.sync
        def _(sp):
            load_weights(sp, 0, 0)
            load_weights(sp, 1, 1)

        @block.tensor
        def _(pe):
            def indices(n, par, g, b):
                if not is_at(n, 0, 1):
                    pe.wait_ge(ib_ready, n - 1)
                nc.tensor.matmul(ip[:, par], pick_b[:, bass.ds(b, 1), :], idx_x[:, g, :], start=True, stop=True
                                 ).then_inc(ip_ready, 1)

            def take(n, par):
                if not is_at(n, 0, 1):
                    pe.wait_ge(xp_free, n - 1)
                pe.wait_ge(hot_ready, n + 1)
                pe.wait_ge(low_ready, n + 1)
                for h in range(2):
                    parts = x_hi[:, bass.ds(n, 1), h, :], x_lo[:, par, 0, h, :], x_lo[:, par, 1, h, :]
                    for i, part in enumerate(parts):
                        mm = nc.tensor.matmul(xp[:, par], part, hot[:, par, h, :], start=(h + i == 0), stop=(h + i == 3))
                mm.then_inc(xp_ready, 1)

            indices(0, 0, 0, 0)
            indices(1, 1, 0, 1)
            for g in range(B // GB):
                if g == 0:
                    for b in range(2):
                        indices(b + 2, b, g, b + 2)
                        take(b, b)
                with pe.Fori(int(g == 0), GB // 2 - 1) as j:
                    for i in range(2):
                        indices(GB * g + 2 * j + i + 2, i, g, 2 * j + i + 2)
                        take(GB * g + 2 * j + i, i)
                for b in range(GB - 2, GB):
                    if g < B // GB - 1:
                        indices(GB * g + b + 2, b % 2, g + 1, b + 2 - GB)
                    take(GB * g + b, b % 2)

        @block.scalar
        def _(act):
            def index_copy(n, par):
                act.wait_ge(ip_ready, n + 1)
                if not is_at(n, 0, 1):
                    act.wait_ge(hot_ready, n - 1)
                nc.scalar.activation(ib[:, par], ip[:, par], ACT.Copy).then_inc(ib_ready, 1)

            def high(n):
                act.wait_ge(xt_ready, 2 * n + 2)
                nc.scalar.activation(x_hi[:, bass.ds(n, 1)], xt[:, bass.ds(n, 1)], ACT.Copy).then_inc(hi_ready, 1)

            def middle(n, par):
                act.wait_ge(rest_ready, n + 1)
                if not is_at(n, 0, 1):
                    act.wait_ge(xp_ready, n - 1)
                nc.scalar.activation(x_lo[:, par:par + 1, 0], xt[:, bass.ds(n, 1)], ACT.Copy).then_inc(mid_ready, 1)

            def body(n, par):
                if not is_at(n, B - 2, B - 1):
                    index_copy(n + 2, par)
                    middle(n + 2, par)
                if not is_at(n, B - 4, B - 3, B - 2, B - 1):
                    high(n + 4)
                act.wait_ge(xp_ready, n + 1)
                nc.scalar.activation(XG[:, :, bass.ds(n, 1), :], xp[:, par].rearrange("p (e c) -> p e c", e=E), ACT.Copy
                                     ).then_inc(xp_free, 1)

            for n in range(2):
                high(n)
                index_copy(n, n)
                middle(n, n)
            high(2)
            high(3)
            by_two(act, B, body, 5)
            act.wait_ge(xp_free, B)

        @block.vector
        def _(dve):
            def norms(n):
                for h in range(2):
                    normed(dve, xt[:, bass.ds(n, 1), h, :], 2 * n + h).then_inc(xt_ready, 1)

            def body(n, par):
                dve.wait_ge(ib_ready, n + 1)
                if not is_at(n, 0, 1):
                    dve.wait_ge(xp_ready, n - 1)
                for h in range(2):
                    mark = nc.vector.tensor_scalar(hot[:, par, h, :], ib[:, par], col_t[:, h:h + 1], None, ALU.is_equal)
                mark.then_inc(hot_ready, 1)
                if not is_at(n, B - 4, B - 3, B - 2, B - 1):
                    norms(n + 4)

            for n in range(4):
                norms(n)
            by_two(dve, B, body, 5)

        @block.gpsimd
        def _(pool):
            def rest(n):
                pool.wait_ge(hi_ready, n + 1)
                nc.gpsimd.tensor_tensor(xt[:, bass.ds(n, 1)], xt[:, bass.ds(n, 1)], x_hi[:, bass.ds(n, 1)], ALU.subtract).then_inc(rest_ready, 1)

            def low(n, par):
                pool.wait_ge(mid_ready, n + 1)
                nc.gpsimd.tensor_tensor(x_lo[:, par:par + 1, 1], xt[:, bass.ds(n, 1)], x_lo[:, par:par + 1, 0], ALU.subtract
                                        ).then_inc(low_ready, 1)

            def body(n, par):
                if not is_at(n, B - 2, B - 1):
                    low(n + 2, par)
                if not is_at(n, B - 4, B - 3, B - 2, B - 1):
                    rest(n + 4)

            for n in range(2):
                rest(n)
                low(n, n)
            rest(2)
            rest(3)
            by_two(pool, B, body, 5)
            pool.wait_ge(low_ready, B)


def run_experts(nc, XG, XO, first_out, weights, w_in, load_weights):
    E, B, CAP = XG.shape[1:]
    wg, wu, wd = weights
    FH = wd.shape[2]
    CB = B // 2
    M = CB * CAP
    DM = wd.shape[3]
    BT = P // CAP
    EP = P // CAP
    with ExitStack() as c:
        def sb(name, shape):
            return c.enter_context(nc.sbuf_tensor(name, shape, F32))

        gl, hx = sb("glx", [P, FH, M]), sb("hx", [P, 2, FH, M])
        gp = c.enter_context(nc.psum_tensor("gpx", [P, FH, M], F32))
        up = c.enter_context(nc.psum_tensor("upx", [P, FH, M], F32))
        dp = c.enter_context(nc.psum_tensor("dpx", [P, 2, M], F32))
        gp_ready, up_ready, gl_ready, hx_ready, dp_ready, dp_free = [
            c.enter_context(nc.semaphore(n)) for n in ("gpx_ready", "upx_ready", "glx_ready", "hx_ready", "dpx_ready", "dpx_free")]
        block = c.enter_context(nc.Block())

        @block.sync
        def _(sp):
            with sp.Fori(0, E // 2 - 1) as j:
                for par in range(2):
                    n = 2 * j + 2 + par
                    sp.wait_ge(dp_ready, 2 * n - 2)
                    load_weights(sp, n, par)

        @block.tensor
        def _(pe):
            def up_gate(n, par, chunk):
                k = 2 * n + chunk
                for h in range(FH):
                    if not is_at(k, 0):
                        pe.wait_ge(hx_ready, FH * (k - 1) + h + 1)
                    x = XG[:, bass.ds(n, 1), CB * chunk:CB * chunk + CB]
                    nc.tensor.matmul(gp[:, h], wg[:, par, h * P:(h + 1) * P], x, start=True, stop=True).then_inc(gp_ready, 1)
                    nc.tensor.matmul(up[:, h], wu[:, par, h * P:(h + 1) * P], x, start=True, stop=True).then_inc(up_ready, 1)

            def down(n, par, chunk):
                k = 2 * n + chunk
                pe.wait_ge(hx_ready, FH * k + FH)
                if not is_at(k, 0, 1):
                    pe.wait_ge(dp_free, k - 1)
                for q in range(M // P):
                    for h in range(FH):
                        mm = nc.tensor.matmul(dp[:, chunk, q * DM:(q + 1) * DM], hx[:, chunk, h, q * P:(q + 1) * P],
                                              wd[:, par, h, :], start=(h == 0), stop=(h == FH - 1))
                mm.then_inc(dp_ready, 1)

            def expert(n, par, uses, last=False):
                up_gate(n, par, 1)
                down(n, par, 0)
                if not last:
                    pe.wait_ge(w_in[1 - par], 48 * uses + 48)
                    up_gate(n + 1, 1 - par, 0)
                down(n, par, 1)

            pe.wait_ge(w_in[0], 48)
            up_gate(0, 0, 0)
            expert(0, 0, 0)
            with pe.Fori(0, E // 2 - 1) as j:
                expert(2 * j + 1, 1, j + 1)
                expert(2 * j + 2, 0, j + 1)
            expert(E - 1, 1, 0, last=True)

        @block.scalar
        def _(act):
            def gelus(k):
                for h in range(FH):
                    act.wait_ge(gp_ready, FH * k + h + 1)
                    if not is_at(k, 0):
                        act.wait_ge(hx_ready, FH * (k - 1) + h + 1)
                    nc.scalar.activation(gl[:, h], gp[:, h], ACT.Gelu).then_inc(gl_ready, 1)

            def put_away(n, e, chunk, dst):
                act.wait_ge(dp_ready, 2 * n + chunk + 1)
                for b in range(BT):
                    to = dst[CAP * e:CAP * e + CAP, :, CB * chunk:CB * chunk + CB, :].rearrange(
                        "p g (q b) d -> p (g q) b d", b=BT)[:, :, b, :]
                    ins = nc.scalar.activation(to, dp[CAP * b:CAP * b + CAP, chunk].rearrange("p (q d) -> p q d", d=DM), ACT.Copy)
                ins.then_inc(dp_free, 1)

            def group(g, dst):
                for e in range(EP):
                    n = EP * g + e
                    gelus(2 * n + 1)
                    put_away(n, e, 0, dst)
                    if not is_at(n, E - 1):
                        gelus(2 * n + 2)
                    put_away(n, e, 1, dst)

            gelus(0)
            group(0, first_out)
            with act.Fori(1, E // EP - 1) as g:
                group(g, XO[:, bass.ds(g - 1, 1)])
            group(E // EP - 1, XO[:, E // EP - 2:E // EP - 1])
            act.wait_ge(dp_free, 2 * E)

        @block.vector
        def _(dve):
            def body(k, par):
                for h in range(FH):
                    dve.wait_ge(gl_ready, FH * k + h + 1)
                    dve.wait_ge(up_ready, FH * k + h + 1)
                    if not is_at(k, 0, 1):
                        dve.wait_ge(dp_ready, k - 1)
                    nc.vector.tensor_tensor(hx[:, par, h], gl[:, h], up[:, h], ALU.mult).then_inc(hx_ready, 1)

            by_two(dve, 2 * E, body)
            dve.wait_ge(hx_ready, FH * 2 * E)


def scatter(nc, X, Y, made, row_t, slot_i, slot_w, eps, out_v, k):
    S, DM, TILES = k["S"], k["DM"], k["TILES"]
    B, EG = k["B"], len(made)
    G4, GB = 4, B // 4
    PB = GB // 2
    AT = GB
    DE = EG // 2
    AE = EG - DE
    slot_ib, slot_wb = (v[:].rearrange("p e g b -> p e (g b)") for v in (slot_i, slot_w))
    with ExitStack() as c:
        def sb(name, shape):
            return c.enter_context(nc.sbuf_tensor(name, shape, F32))

        put = sb("put", [P, 2, EG, S])
        dist = sb("dist", [P, 2, AE, S])
        neg_i, neg_w = sb("neg_i", [P, AE, B]), sb("neg_w", [P, AE, B])
        st, part = sb("st5", [P, TILES, 6]), sb("part5", [P, 3, TILES])
        mean, lnv, rstd, shift = [sb(n, [P, TILES]) for n in ("mean5", "lnv5", "rstd5", "shift5")]
        yp = c.enter_context(nc.psum_tensor("yss", [P, 2, 512], F32))
        (neg_ready, dist_ready, put_act, put_dve, yp_ready, y_ready, st_ready, sq_ready, var_ready, ln_ready, r_ready,
         shift_ready, n_dve, n_act, x_dve, x_pool, stored) = [c.enter_context(nc.semaphore(f"{n}5")) for n in (
             "neg_ready", "dist_ready", "put_act", "put_dve", "yp_ready", "y_ready", "st_ready", "sq_ready", "var_ready",
             "ln_ready", "r_ready", "shift_ready", "n_dve", "n_act", "x_dve", "x_pool", "stored")]
        block = c.enter_context(nc.Block())

        @block.tensor
        def _(pe):
            def body(n, par):
                pe.wait_ge(put_dve, n + 1)
                pe.wait_ge(put_act, n + 1)
                if not is_at(n, 0, 1):
                    pe.wait_ge(y_ready, n - 1)
                for h in range(2):
                    for g in range(EG):
                        mm = nc.tensor.matmul(yp[:, par, h * DM:(h + 1) * DM], put[:, par, g, h * P:(h + 1) * P],
                                              made[g][:, bass.ds(n, 1), :], start=(g == 0), stop=(g == EG - 1))
                mm.then_inc(yp_ready, 1)

            by_two(pe, B, body, 3)

        @block.scalar
        def _(act):
            def places(n, par):
                for e in range(AE):
                    nc.scalar.activation(dist[:, par, e], row_t[:], ACT.Abs, bias=neg_i[:, e, bass.ds(n, 1)]
                                         ).then_inc(dist_ready, 1)
                if not is_at(n, 0, 1):
                    act.wait_ge(yp_ready, n - 1)
                for e in range(AE):
                    act.wait_ge(dist_ready, AE * n + e + 1)
                    ins = nc.scalar.activation(put[:, par, DE + e], dist[:, par, e], ACT.Relu,
                                               scale=neg_w[:, e, bass.ds(n, 1)], bias=slot_wb[:, DE + e, bass.ds(n, 1)])
                ins.then_inc(put_act, 1)

            nc.scalar.preload_act_table_set(LOG)
            nc.scalar.activation(neg_i[:], slot_ib[:, DE:], ACT.Copy, scale=-1.0).then_inc(neg_ready, 1)
            nc.scalar.activation(neg_w[:], slot_wb[:, DE:], ACT.Copy, scale=-1.0).then_inc(neg_ready, 1)
            act.wait_ge(neg_ready, 2)
            by_two(act, B, places, 3)
            act.wait_ge(var_ready, 1)
            nc.scalar.activation(lnv[:], part[:, 2, :], ACT.Ln, scale=1.0 / P, bias=eps[:, 0:1]).then_inc(ln_ready, 1)
            act.wait_ge(ln_ready, 1)
            nc.scalar.activation(rstd[:], lnv[:], ACT.Exp, scale=-0.5).then_inc(r_ready, 1)
            act.wait_ge(shift_ready, 1)
            for g in range(G4):
                for t in range(2 * GB * (g + 1) - AT, 2 * GB * (g + 1)):
                    yt = Y[:, t // 2, t % 2, :]
                    ins = nc.scalar.activation(yt, yt, ACT.Identity, scale=rstd[:, t:t + 1], bias=shift[:, t:t + 1])
                ins.then_inc(n_act, 1)
            act.wait_ge(n_act, G4)

        @block.vector
        def _(dve):
            def places(n, par):
                if not is_at(n, 0, 1):
                    dve.wait_ge(yp_ready, n - 1)
                for e in range(DE):
                    ins = nc.vector.tensor_scalar(put[:, par, e, :], row_t[:], slot_ib[:, e, bass.ds(n, 1)],
                                                  slot_wb[:, e, bass.ds(n, 1)], ALU.is_equal, ALU.mult)
                ins.then_inc(put_dve, 1)

            def body(n, par):
                dve.wait_ge(yp_ready, n + 1)
                yb = Y[:, bass.ds(n, 1)]
                nc.vector.tensor_tensor(yb, yp[:, par, 0:2 * DM].rearrange("p (c d) -> p c d", c=2), yb, ALU.add
                                        ).then_inc(y_ready, 1)
                if not is_at(n, B - 1, B - 2):
                    places(n + 2, par)
                dve.wait_ge(y_ready, n + 1)
                for h in range(2):
                    nc.vector.bn_stats(st[:, bass.ds(2 * n + h, 1), :], Y[:, bass.ds(n, 1), h, :]).then_inc(st_ready, 1)

            places(0, 0)
            places(1, 1)
            by_two(dve, B, body, 3)
            dve.wait_ge(st_ready, TILES)
            total, diff, var = part[:, 0, :], part[:, 1, :], part[:, 2, :]
            nc.vector.tensor_tensor(diff, st[:, :, 1], st[:, :, 4], ALU.subtract).then_inc(sq_ready, 1)
            nc.vector.tensor_tensor(var, st[:, :, 2], st[:, :, 5], ALU.add).then_inc(sq_ready, 1)
            nc.vector.tensor_tensor(total, st[:, :, 1], st[:, :, 4], ALU.add).then_inc(sq_ready, 1)
            dve.wait_ge(sq_ready, 3)
            nc.vector.scalar_tensor_tensor(diff, diff, P / 4, diff, ALU.mult, ALU.mult).then_inc(sq_ready, 1)
            dve.wait_ge(sq_ready, 4)
            nc.vector.tensor_tensor(var, var, diff, ALU.add).then_inc(var_ready, 1)
            nc.vector.tensor_scalar(mean[:], total, 0.5, None, ALU.mult).then_inc(sq_ready, 1)
            dve.wait_ge(sq_ready, 5)
            dve.wait_ge(r_ready, 1)
            nc.vector.scalar_tensor_tensor(shift[:], mean[:], -1.0, rstd[:], ALU.mult, ALU.mult).then_inc(shift_ready, 1)

            def norm(g):
                for t in range(2 * GB * g, 2 * GB * (g + 1) - AT):
                    yt = Y[:, t // 2, t % 2, :]
                    nc.vector.tensor_scalar(yt, yt, mean[:, t:t + 1], rstd[:, t:t + 1], ALU.subtract, ALU.mult
                                            ).then_inc(n_dve, 1)

            def add(g):
                dve.wait_ge(n_dve, (2 * GB - AT) * (g + 1))
                dve.wait_ge(n_act, g + 1)
                xv = X[:, 2 * (GB * g + PB):2 * GB * (g + 1), :].rearrange("p (b c) d -> p b c d", c=2)
                nc.vector.tensor_tensor(xv, xv, Y[:, GB * g + PB:GB * (g + 1)], ALU.add).then_inc(x_dve, 1)

            norm(0)
            for g in range(1, G4):
                norm(g)
                add(g - 1)
            add(G4 - 1)

        @block.gpsimd
        def _(pool):
            with pool.Fori(0, G4) as g:
                pool.wait_ge(n_dve, (2 * GB - AT) * g + 2 * PB)
                xv = X[:, bass.ds(2 * GB * g, 2 * PB), :].rearrange("p (b c) d -> p b c d", c=2)
                nc.gpsimd.tensor_tensor(xv, xv, Y[:, bass.ds(GB * g, PB)], ALU.add).then_inc(x_pool, 1)

        @block.sync
        def _(sp):
            with sp.Fori(0, G4) as g:
                sp.wait_ge(x_dve, g + 1)
                sp.wait_ge(x_pool, g + 1)
                tiles = bass.ds(2 * GB * g, 2 * GB)
                sp.dma_start(out_v[:, tiles, :], X[:, tiles, :]).then_inc(stored, 16)
            sp.wait_ge(stored, 16 * G4)


def kernel(**inputs):
    import concourse.bacc as bacc
    from concourse.bass_utils import run_bass_kernel_spmd

    arrays = lay_out(inputs)
    nc = bacc.Bacc("TRN2", target_bir_lowering=False, num_devices=1)
    feeds, aps = {}, {}
    for name, v in arrays.items():
        feeds[f"in_{name}"] = v
        aps[name] = nc.dram_tensor(f"in_{name}", v.shape, mybir.dt.from_np(v.dtype), kind="ExternalInput").ap()
    shape = inputs["L0_attn_x"].shape
    out = nc.dram_tensor("out", shape, F32, kind="ExternalOutput").ap()
    build(nc, aps, out)
    r = run_bass_kernel_spmd(nc, [feeds], core_ids=[0])
    return r.results[0]["out"]


def lay_out(inputs):
    i = {n.removeprefix("L0_"): np.asarray(v) for n, v in inputs.items()}
    DI, E, F, D = i["attn_out_proj_w"].shape[0], *i["ffn_Wg"].shape

    def rows(w):
        return np.ascontiguousarray(w.reshape(-1, P, w.shape[1]).transpose(1, 0, 2))

    wx = i["attn_x_proj_w"]
    bc = np.concatenate([wx[:, DI + 16:DI + 32], wx[:, DI:DI + 16]], 1)
    return {
        "x": np.ascontiguousarray(i["attn_x"]),
        "w_u": np.ascontiguousarray(i["attn_in_proj_w"][:, 0:DI]),
        "w_z": np.ascontiguousarray(i["attn_in_proj_w"][:, DI:]),
        "conv_w": np.ascontiguousarray(i["attn_conv_w"][:, 0, :].T),
        "conv_b": np.ascontiguousarray(i["attn_conv_b"].reshape(-1, P).T),
        "w_xdT": rows(wx[:, 0:DI].T),
        "w_dt": rows(i["attn_dt_proj_w"]),
        "w_bc": rows(np.concatenate([bc] * 4, 1)),
        "dt_b": np.ascontiguousarray(i["attn_dt_proj_b"].reshape(-1, P).T),
        "w_out": rows(i["attn_out_proj_w"]),
        "a_log": np.ascontiguousarray(i["attn_A_log"].reshape(DI // 64, 64, 2, 8).transpose(2, 1, 0, 3).reshape(P, -1)),
        "dskip": np.ascontiguousarray(i["attn_D_param"].reshape(-1, P).T),
        "gate_wT": np.ascontiguousarray(i["ffn_gate_w"].T),
        "wgT": np.ascontiguousarray(i["ffn_Wg"].transpose(2, 0, 1)),
        "wuT": np.ascontiguousarray(i["ffn_Wu"].transpose(2, 0, 1)),
        "wdT": np.ascontiguousarray(i["ffn_Wd"].reshape(E, D, F // P, P).transpose(3, 0, 2, 1)),
        "wsgT": np.ascontiguousarray(i["ffn_Ws_g"].T),
        "wsuT": np.ascontiguousarray(i["ffn_Ws_u"].T),
        "wsdT": np.ascontiguousarray(i["ffn_Ws_d"].reshape(D, F // P, P).transpose(2, 1, 0)),
    }
```
